# Optimizing a Trainium2 kernel written in Bass

```python
import numpy as np
import jax
import jax.numpy as jnp

def _softmax(x, axis=-1):
    return jax.nn.softmax(x, axis=axis)

def _gelu(x):
    return jax.nn.gelu(x, approximate=True)

def _silu(x):
    return jax.nn.silu(x)

def _sigmoid(x):
    return jax.nn.sigmoid(x)

def _layernorm(x, axis=-1, eps=1e-05):
    m = jnp.mean(x, axis=axis, keepdims=True)
    v = jnp.var(x, axis=axis, keepdims=True)
    return (x - m) / jnp.sqrt(v + eps)

def _scatter_add(tgt, idx, src, axis=0):
    return tgt.at[idx].add(src)

def _segment_sum(src, seg, n):
    return jax.ops.segment_sum(src, seg, n)
kernel_name = 'mk_decoder_postln_d2_seqx_r4_7a6aaf'

def setup_inputs(seed: int=0):
    np.random.seed(seed)
    _w = jnp.asarray

    def _rec_inputs():
        import jax
        import jax.numpy as jnp
        _rk = jax.random.key(seed)
        x = -0.0002928 + 1 * jax.random.normal(jax.random.fold_in(_rk, 1), (8, 256, 256), jnp.float32)
        _lenS = 256 - jax.random.randint(jax.random.fold_in(_rk, 7), (8,), 0, max(1, 256 // 4) + 1, jnp.int32)
        _lenS2 = 256 - jax.random.randint(jax.random.fold_in(_rk, 8), (8,), 0, max(1, 256 // 4) + 1, jnp.int32)
        _ctx_1024P = jax.random.normal(jax.random.fold_in(_rk, 11), (8, 16, 256), jnp.float32)
        _ctx_1024c = jax.random.dirichlet(jax.random.fold_in(_rk, 511), 0.3 * jnp.ones((16,), jnp.float32), (8, 256))
        _ctx_1024t = jnp.einsum('bsk,bkd->bsd', _ctx_1024c, _ctx_1024P)
        _ctx_1024t = _ctx_1024t * jax.lax.rsqrt(jnp.mean(jnp.square(_ctx_1024t)) + 1e-12) * 0.953939
        ctx_1024 = 0.000227908 + 0.99994 * (_ctx_1024t + 0.3 * jax.random.normal(jax.random.fold_in(_rk, 611), (8, 256, 256), jnp.float32))
        itok_BxSx64_0_2047 = jax.random.randint(jax.random.fold_in(_rk, 13), (8, 256, 64), 0, 512, jnp.int32)
        _validS = jnp.arange(256)[None, :] < _lenS[:, None]
        _validS2 = jnp.arange(256)[None, :] < _lenS2[:, None]
        _causal = jnp.tril(jnp.ones((256, 256), dtype=bool))
        mask_SxS_bc0 = jnp.logical_not(jnp.broadcast_to(_causal[:, :], (256, 256)))
        return (x, ctx_1024, itok_BxSx64_0_2047, mask_SxS_bc0)
    x, ctx_1024, itok_BxSx64_0_2047, mask_SxS_bc0 = _rec_inputs()

    def _L0_attn_setup():
        import jax, jax.numpy as jnp
        import numpy as np
        N_HEADS = 1
        LATENT_DIM = 256
        SCALE = 1.0 / float(np.sqrt(LATENT_DIM * N_HEADS))
        key = jax.random.key(seed)
        kx, kq, ko = jax.random.split(key, 3)
        B, S, D = (4, 1024, 256)
        x = jax.random.normal(kx, (B, S, D), dtype=jnp.float32)
        w_qkv = jax.random.normal(kq, (3 * N_HEADS * (LATENT_DIM // N_HEADS), D), dtype=jnp.float32) * 0.02
        w_o = jax.random.normal(ko, (LATENT_DIM, N_HEADS * (LATENT_DIM // N_HEADS)), dtype=jnp.float32) * 0.02
        return {'x': x, 'w_qkv': w_qkv, 'w_o': w_o}
    _L0_attn_all = _L0_attn_setup()
    _L0_attn_in = {k: v for k, v in _L0_attn_all.items() if k in ('w_qkv', 'w_o')}
    del _L0_attn_all

    def _L0_xattn_setup():
        import jax, jax.numpy as jnp
        import numpy as np
        from jax import lax
        H = 16
        K1, K2 = (3, 3)
        LN_EPS = 1e-05

        def _ln(x, g, b):
            m = jnp.mean(x, axis=-1, keepdims=True)
            v = jnp.mean(jnp.square(x - m), axis=-1, keepdims=True)
            return (x - m) * lax.rsqrt(v + LN_EPS) * g + b

        def _gelu(x):
            return jax.nn.gelu(x, approximate=False)
        key = jax.random.key(seed)
        B, T, D, Th = (4, 256, 256, 64)
        C = 2 * D
        ks = jax.random.split(key, 16)

        def w(k, shape):
            fan_in = shape[0]
            return (jax.random.normal(k, shape, jnp.float32) / np.sqrt(fan_in)).astype(jnp.float32)
        inp = {'x': jax.random.normal(ks[0], (B, T, D), jnp.float32), 'historical_data': jax.random.normal(ks[1], (B, Th, D), jnp.float32), 'Wq': w(ks[2], (D, D)), 'Wk': w(ks[3], (D, D)), 'Wv': w(ks[4], (D, D)), 'hist_W': w(ks[5], (D, C)), 'hist_b': jnp.zeros((C,), jnp.float32), 'hist_ln_g': jnp.ones((C,), jnp.float32), 'hist_ln_b': jnp.zeros((C,), jnp.float32), 'ctx_W1': w(ks[6], (C, C // 4)), 'ctx_b1': jnp.zeros((C // 4,), jnp.float32), 'ctx_W2': w(ks[7], (C // 4, 1)), 'ctx_b2': jnp.zeros((1,), jnp.float32), 'kg_W1': w(ks[8], (C, D)), 'kg_b1': jnp.zeros((D,), jnp.float32), 'kg_ln_g': jnp.ones((D,), jnp.float32), 'kg_ln_b': jnp.zeros((D,), jnp.float32), 'kg_W2': w(ks[9], (D, H * K1 * K2)), 'kg_b2': jnp.zeros((H * K1 * K2,), jnp.float32), 'proj_W': w(ks[10], (D, D)), 'proj_b': jnp.zeros((D,), jnp.float32), 'causal_mask': jnp.triu(jnp.ones((T, T), bool), k=1)}
        return inp
    _L0_xattn_all = _L0_xattn_setup()
    _L0_xattn_in = {k: v for k, v in _L0_xattn_all.items() if k in ('Wq', 'Wk', 'Wv', 'hist_W', 'hist_b', 'hist_ln_g', 'hist_ln_b', 'ctx_W1', 'ctx_b1', 'ctx_W2', 'ctx_b2', 'kg_W1', 'kg_b1', 'kg_ln_g', 'kg_ln_b', 'kg_W2', 'kg_b2', 'proj_W', 'proj_b')}
    del _L0_xattn_all

    def _L0_ffn_setup():
        import jax, jax.numpy as jnp
        import numpy as np
        D_MODEL = 256
        N_HEADS = 16
        HEAD_DIM = D_MODEL // N_HEADS
        KV_LATENT = 128
        N_EXPERTS = 4
        D_HIDDEN = 4 * D_MODEL
        B, T = (2, 256)

        def rmsnorm(x, w, eps=1e-06):
            return w * (x * jax.lax.rsqrt(jnp.mean(x * x, axis=-1, keepdims=True) + eps))

        def layernorm(x, g, b, eps=1e-05):
            mu = jnp.mean(x, axis=-1, keepdims=True)
            var = jnp.mean((x - mu) ** 2, axis=-1, keepdims=True)
            return (x - mu) * jax.lax.rsqrt(var + eps) * g + b

        def apply_rope(x):
            t, d = (x.shape[2], x.shape[3])
            half = d // 2
            pos = jnp.arange(t, dtype=x.dtype)[:, None]
            inv_freq = 1.0 / 10000.0 ** (jnp.arange(half, dtype=x.dtype) / half)
            ang = pos * inv_freq[None, :]
            sin, cos = (jnp.sin(ang), jnp.cos(ang))
            x1, x2 = (x[..., :half], x[..., half:])
            return jnp.concatenate([x1 * cos - x2 * sin, x1 * sin + x2 * cos], axis=-1)

        def mla_attention(x, Wq, Wdkv, Wuk, Wuv, Wo, ln_g, ln_b):
            b, t, _ = x.shape
            q = (x @ Wq.T).reshape(b, t, N_HEADS, HEAD_DIM).transpose(0, 2, 1, 3)
            latent = layernorm(x @ Wdkv.T, ln_g, ln_b)
            k = (latent @ Wuk.T).reshape(b, t, N_HEADS, HEAD_DIM).transpose(0, 2, 1, 3)
            v = (latent @ Wuv.T).reshape(b, t, N_HEADS, HEAD_DIM).transpose(0, 2, 1, 3)
            q = apply_rope(q)
            k = apply_rope(k)
            scores = jnp.einsum('bhqd,bhkd->bhqk', q, k) / np.sqrt(HEAD_DIM)
            causal = jnp.tril(jnp.ones((t, t), dtype=bool))
            scores = jnp.where(causal, scores, -jnp.inf)
            attn = jax.nn.softmax(scores, axis=-1)
            out = jnp.einsum('bhqk,bhkd->bhqd', attn, v).transpose(0, 2, 1, 3).reshape(b, t, D_MODEL)
            return out @ Wo.T

        def moe(x, gate_w, gate_b, W1, b1, W2, b2):
            logits = x @ gate_w.T + gate_b
            top = jnp.argmax(logits, axis=-1)
            onehot = jax.nn.one_hot(top, N_EXPERTS, dtype=x.dtype)
            h = jax.nn.relu(jnp.einsum('btd,ehd->bteh', x, W1) + b1)
            y = jnp.einsum('bteh,edh->bted', h, W2) + b2
            return jnp.einsum('bted,bte->btd', y, onehot)
        key = jax.random.key(seed)
        ks = jax.random.split(key, 16)
        s = lambda fan_in: 1.0 / np.sqrt(fan_in)
        return {'x': jax.random.normal(ks[0], (B, T, D_MODEL), jnp.float32), 'norm1_w': jnp.ones((D_MODEL,), jnp.float32), 'norm2_w': jnp.ones((D_MODEL,), jnp.float32), 'Wq': jax.random.normal(ks[1], (D_MODEL, D_MODEL), jnp.float32) * s(D_MODEL), 'Wdkv': jax.random.normal(ks[2], (KV_LATENT, D_MODEL), jnp.float32) * s(D_MODEL), 'Wuk': jax.random.normal(ks[3], (D_MODEL, KV_LATENT), jnp.float32) * s(KV_LATENT), 'Wuv': jax.random.normal(ks[4], (D_MODEL, KV_LATENT), jnp.float32) * s(KV_LATENT), 'Wo': jax.random.normal(ks[5], (D_MODEL, D_MODEL), jnp.float32) * s(D_MODEL), 'ln_g': jnp.ones((KV_LATENT,), jnp.float32), 'ln_b': jnp.zeros((KV_LATENT,), jnp.float32), 'gate_w': jax.random.normal(ks[6], (N_EXPERTS, D_MODEL), jnp.float32) * s(D_MODEL), 'gate_b': jnp.zeros((N_EXPERTS,), jnp.float32), 'W1': jax.random.normal(ks[7], (N_EXPERTS, D_HIDDEN, D_MODEL), jnp.float32) * s(D_MODEL), 'b1': jnp.zeros((N_EXPERTS, D_HIDDEN), jnp.float32), 'W2': jax.random.normal(ks[8], (N_EXPERTS, D_MODEL, D_HIDDEN), jnp.float32) * s(D_HIDDEN), 'b2': jnp.zeros((N_EXPERTS, D_MODEL), jnp.float32)}
    _L0_ffn_all = _L0_ffn_setup()
    _L0_ffn_in = {k: v for k, v in _L0_ffn_all.items() if k in ('norm1_w', 'norm2_w', 'Wq', 'Wdkv', 'Wuk', 'Wuv', 'Wo', 'ln_g', 'ln_b', 'gate_w', 'gate_b', 'W1', 'b1', 'W2', 'b2')}
    del _L0_ffn_all

    def _L1_attn_setup():
        import jax, jax.numpy as jnp
        import numpy as np
        _J6 = jnp.array([[0, 0, 0, 0, 0, 1], [0, 0, 0, 0, -1, 0], [0, 0, 0, 1, 0, 0], [0, 0, 1, 0, 0, 0], [0, -1, 0, 0, 0, 0], [1, 0, 0, 0, 0, 0]], dtype=jnp.float32)
        _PAIRS4 = [(0, 1), (0, 2), (0, 3), (1, 2), (1, 3), (2, 3)]

        def exterior(p1, p2):
            parts = [p1[..., i] * p2[..., j] - p1[..., j] * p2[..., i] for i, j in _PAIRS4]
            L = jnp.stack(parts, axis=-1)
            n = jnp.maximum(jnp.linalg.norm(L, axis=-1, keepdims=True), 1e-12)
            return L / n
        key = jax.random.key(seed)
        B, T, D, H = (2, 512, 256, 16)
        ks = jax.random.split(key, 10)
        w = lambda k, shape: jax.random.normal(k, shape, jnp.float32) * 0.02
        return {'x': jax.random.normal(ks[0], (B, T, D), jnp.float32), 'qkv_w': w(ks[1], (3 * D, D)), 'qkv_b': jnp.zeros((3 * D,), jnp.float32), 'w1w': w(ks[2], (4 * H, D)), 'w2w': w(ks[3], (4 * H, D)), 'r1w': w(ks[4], (4 * H, D)), 'r2w': w(ks[5], (4 * H, D)), 'memv_w': w(ks[6], (D, D)), 'memv_b': jnp.zeros((D,), jnp.float32), 'memg_w': w(ks[7], (H, D)), 'memg_b': jnp.zeros((H,), jnp.float32), 'mem_scale': jnp.full((H,), 0.1, jnp.float32), 'iter_mix': jnp.array(0.0, jnp.float32), 'out_w': w(ks[8], (D, D)), 'out_b': jnp.zeros((D,), jnp.float32), 'decay_logits': jnp.full((H,), 4.6, jnp.float32)}
    _L1_attn_all = _L1_attn_setup()
    _L1_attn_in = {k: v for k, v in _L1_attn_all.items() if k in ('qkv_w', 'qkv_b', 'w1w', 'w2w', 'r1w', 'r2w', 'memv_w', 'memv_b', 'memg_w', 'memg_b', 'mem_scale', 'iter_mix', 'out_w', 'out_b', 'decay_logits')}
    del _L1_attn_all

    def _L1_xattn_setup():
        import jax, jax.numpy as jnp
        import numpy as np
        B, NQ, NKV, K = (2, 256, 512, 64)
        D, H, LAT = (256, 16, 128)
        HD = D // H
        SCALE = 1.0 / np.sqrt(HD)
        key = jax.random.key(seed)
        ks = jax.random.split(key, 7)
        s = lambda fan_in: 1.0 / np.sqrt(fan_in)
        return {'x_q': jax.random.normal(ks[0], (B, NQ, D), jnp.float32), 'x_kv': jax.random.normal(ks[1], (B, NKV, D), jnp.float32), 'indices': jax.random.randint(ks[2], (B, NQ, K), 0, NKV), 'W_q': jax.random.normal(ks[3], (D, D), jnp.float32) * s(D), 'W_kv_down': jax.random.normal(ks[4], (LAT, D), jnp.float32) * s(D), 'W_kv_up': jax.random.normal(ks[5], (2 * D, LAT), jnp.float32) * s(LAT), 'W_out': jax.random.normal(ks[6], (D, D), jnp.float32) * s(D)}
    _L1_xattn_all = _L1_xattn_setup()
    _L1_xattn_in = {k: v for k, v in _L1_xattn_all.items() if k in ('W_q', 'W_kv_down', 'W_kv_up', 'W_out')}
    del _L1_xattn_all

    def _L1_ffn_setup():
        import jax, jax.numpy as jnp
        import numpy as np
        B, T, D, R, KEXP = (4, 1024, 256, 64, 8)
        RH = max(D, 32)
        SCALE = 0.02

        def _fused_branch(Q_side, K_side, V, W, U, b, router_w1, router_b1, router_w2, router_b2, expert_bias):
            xV = jnp.einsum('btd,kdr->btkr', Q_side, V)
            yW = jnp.einsum('btd,kdr->btkr', K_side, W)
            cum_yW = jnp.cumsum(yW, axis=1)
            prod = xV * cum_yW
            h = jax.nn.gelu(Q_side @ router_w1.T + router_b1, approximate=False)
            logits = h @ router_w2.T + router_b2 + expert_bias
            weights = jax.nn.softmax(logits, axis=-1)
            out = jnp.einsum('btkr,kdr->btd', prod * weights[..., None], U)
            out = out + weights @ b
            n_valid = jnp.arange(1, Q_side.shape[1] + 1, dtype=Q_side.dtype)
            return out / n_valid[None, :, None]
        key = jax.random.key(seed)
        ks = jax.random.split(key, 20)
        x = jax.random.normal(ks[0], (B, T, D), dtype=jnp.float32)
        W_Q = jax.random.normal(ks[1], (D, D), dtype=jnp.float32) * (1.0 / np.sqrt(D))
        W_K = jax.random.normal(ks[2], (D, D), dtype=jnp.float32) * (1.0 / np.sqrt(D))
        W_O = jax.random.normal(ks[3], (D, D), dtype=jnp.float32) * (1.0 / np.sqrt(D))
        W_inv = jnp.eye(D, dtype=jnp.float32) + 0.01 * jax.random.normal(ks[4], (D, D), dtype=jnp.float32)
        V_fwd = jax.random.normal(ks[5], (KEXP, D, R), dtype=jnp.float32) * SCALE
        W_fwd = jax.random.normal(ks[6], (KEXP, D, R), dtype=jnp.float32) * SCALE
        U_fwd = jax.random.normal(ks[7], (KEXP, D, R), dtype=jnp.float32) * SCALE
        b_fwd = jnp.zeros((KEXP, D), dtype=jnp.float32)
        V_inv = jax.random.normal(ks[8], (KEXP, D, R), dtype=jnp.float32) * SCALE
        W_inv_exp = jax.random.normal(ks[9], (KEXP, D, R), dtype=jnp.float32) * SCALE
        U_inv = jax.random.normal(ks[10], (KEXP, D, R), dtype=jnp.float32) * SCALE
        b_inv = jnp.zeros((KEXP, D), dtype=jnp.float32)
        router_w1 = jax.random.normal(ks[11], (RH, D), dtype=jnp.float32) * (1.0 / np.sqrt(D))
        router_b1 = jnp.zeros((RH,), dtype=jnp.float32)
        router_w2 = jax.random.normal(ks[12], (KEXP, RH), dtype=jnp.float32) * (1.0 / np.sqrt(RH))
        router_b2 = jnp.zeros((KEXP,), dtype=jnp.float32)
        alpha_bi = jnp.asarray(0.5, dtype=jnp.float32)
        expert_bias = jnp.zeros((KEXP,), dtype=jnp.float32)
        return dict(x=x, W_Q=W_Q, W_K=W_K, W_O=W_O, W_inv=W_inv, V_fwd=V_fwd, W_fwd=W_fwd, U_fwd=U_fwd, b_fwd=b_fwd, V_inv=V_inv, W_inv_exp=W_inv_exp, U_inv=U_inv, b_inv=b_inv, router_w1=router_w1, router_b1=router_b1, router_w2=router_w2, router_b2=router_b2, alpha_bi=alpha_bi, expert_bias=expert_bias)
    _L1_ffn_all = _L1_ffn_setup()
    _L1_ffn_in = {k: v for k, v in _L1_ffn_all.items() if k in ('W_Q', 'W_K', 'W_O', 'W_inv', 'V_fwd', 'W_fwd', 'U_fwd', 'b_fwd', 'V_inv', 'W_inv_exp', 'U_inv', 'b_inv', 'router_w1', 'router_b1', 'router_w2', 'router_b2', 'alpha_bi', 'expert_bias')}
    del _L1_ffn_all
    return {'x': x, 'ctx_1024': ctx_1024, 'itok_BxSx64_0_2047': itok_BxSx64_0_2047, 'mask_SxS_bc0': mask_SxS_bc0, 'L0_attn_w_qkv': _L0_attn_in['w_qkv'], 'L0_attn_w_o': _L0_attn_in['w_o'], 'L0_xattn_Wq': _L0_xattn_in['Wq'], 'L0_xattn_Wk': _L0_xattn_in['Wk'], 'L0_xattn_Wv': _L0_xattn_in['Wv'], 'L0_xattn_hist_W': _L0_xattn_in['hist_W'], 'L0_xattn_hist_b': _L0_xattn_in['hist_b'], 'L0_xattn_hist_ln_g': _L0_xattn_in['hist_ln_g'], 'L0_xattn_hist_ln_b': _L0_xattn_in['hist_ln_b'], 'L0_xattn_ctx_W1': _L0_xattn_in['ctx_W1'], 'L0_xattn_ctx_b1': _L0_xattn_in['ctx_b1'], 'L0_xattn_ctx_W2': _L0_xattn_in['ctx_W2'], 'L0_xattn_ctx_b2': _L0_xattn_in['ctx_b2'], 'L0_xattn_kg_W1': _L0_xattn_in['kg_W1'], 'L0_xattn_kg_b1': _L0_xattn_in['kg_b1'], 'L0_xattn_kg_ln_g': _L0_xattn_in['kg_ln_g'], 'L0_xattn_kg_ln_b': _L0_xattn_in['kg_ln_b'], 'L0_xattn_kg_W2': _L0_xattn_in['kg_W2'], 'L0_xattn_kg_b2': _L0_xattn_in['kg_b2'], 'L0_xattn_proj_W': _L0_xattn_in['proj_W'], 'L0_xattn_proj_b': _L0_xattn_in['proj_b'], 'L0_ffn_norm1_w': _L0_ffn_in['norm1_w'], 'L0_ffn_norm2_w': _L0_ffn_in['norm2_w'], 'L0_ffn_Wq': _L0_ffn_in['Wq'], 'L0_ffn_Wdkv': _L0_ffn_in['Wdkv'], 'L0_ffn_Wuk': _L0_ffn_in['Wuk'], 'L0_ffn_Wuv': _L0_ffn_in['Wuv'], 'L0_ffn_Wo': _L0_ffn_in['Wo'], 'L0_ffn_ln_g': _L0_ffn_in['ln_g'], 'L0_ffn_ln_b': _L0_ffn_in['ln_b'], 'L0_ffn_gate_w': _L0_ffn_in['gate_w'], 'L0_ffn_gate_b': _L0_ffn_in['gate_b'], 'L0_ffn_W1': _L0_ffn_in['W1'], 'L0_ffn_b1': _L0_ffn_in['b1'], 'L0_ffn_W2': _L0_ffn_in['W2'], 'L0_ffn_b2': _L0_ffn_in['b2'], 'L1_attn_qkv_w': _L1_attn_in['qkv_w'], 'L1_attn_qkv_b': _L1_attn_in['qkv_b'], 'L1_attn_w1w': _L1_attn_in['w1w'], 'L1_attn_w2w': _L1_attn_in['w2w'], 'L1_attn_r1w': _L1_attn_in['r1w'], 'L1_attn_r2w': _L1_attn_in['r2w'], 'L1_attn_memv_w': _L1_attn_in['memv_w'], 'L1_attn_memv_b': _L1_attn_in['memv_b'], 'L1_attn_memg_w': _L1_attn_in['memg_w'], 'L1_attn_memg_b': _L1_attn_in['memg_b'], 'L1_attn_mem_scale': _L1_attn_in['mem_scale'], 'L1_attn_iter_mix': _L1_attn_in['iter_mix'], 'L1_attn_out_w': _L1_attn_in['out_w'], 'L1_attn_out_b': _L1_attn_in['out_b'], 'L1_attn_decay_logits': _L1_attn_in['decay_logits'], 'L1_xattn_W_q': _L1_xattn_in['W_q'], 'L1_xattn_W_kv_down': _L1_xattn_in['W_kv_down'], 'L1_xattn_W_kv_up': _L1_xattn_in['W_kv_up'], 'L1_xattn_W_out': _L1_xattn_in['W_out'], 'L1_ffn_W_Q': _L1_ffn_in['W_Q'], 'L1_ffn_W_K': _L1_ffn_in['W_K'], 'L1_ffn_W_O': _L1_ffn_in['W_O'], 'L1_ffn_W_inv': _L1_ffn_in['W_inv'], 'L1_ffn_V_fwd': _L1_ffn_in['V_fwd'], 'L1_ffn_W_fwd': _L1_ffn_in['W_fwd'], 'L1_ffn_U_fwd': _L1_ffn_in['U_fwd'], 'L1_ffn_b_fwd': _L1_ffn_in['b_fwd'], 'L1_ffn_V_inv': _L1_ffn_in['V_inv'], 'L1_ffn_W_inv_exp': _L1_ffn_in['W_inv_exp'], 'L1_ffn_U_inv': _L1_ffn_in['U_inv'], 'L1_ffn_b_inv': _L1_ffn_in['b_inv'], 'L1_ffn_router_w1': _L1_ffn_in['router_w1'], 'L1_ffn_router_b1': _L1_ffn_in['router_b1'], 'L1_ffn_router_w2': _L1_ffn_in['router_w2'], 'L1_ffn_router_b2': _L1_ffn_in['router_b2'], 'L1_ffn_alpha_bi': _L1_ffn_in['alpha_bi'], 'L1_ffn_expert_bias': _L1_ffn_in['expert_bias']}

def reference(x, ctx_1024, itok_BxSx64_0_2047, mask_SxS_bc0, L0_attn_w_qkv, L0_attn_w_o, L0_xattn_Wq, L0_xattn_Wk, L0_xattn_Wv, L0_xattn_hist_W, L0_xattn_hist_b, L0_xattn_hist_ln_g, L0_xattn_hist_ln_b, L0_xattn_ctx_W1, L0_xattn_ctx_b1, L0_xattn_ctx_W2, L0_xattn_ctx_b2, L0_xattn_kg_W1, L0_xattn_kg_b1, L0_xattn_kg_ln_g, L0_xattn_kg_ln_b, L0_xattn_kg_W2, L0_xattn_kg_b2, L0_xattn_proj_W, L0_xattn_proj_b, L0_ffn_norm1_w, L0_ffn_norm2_w, L0_ffn_Wq, L0_ffn_Wdkv, L0_ffn_Wuk, L0_ffn_Wuv, L0_ffn_Wo, L0_ffn_ln_g, L0_ffn_ln_b, L0_ffn_gate_w, L0_ffn_gate_b, L0_ffn_W1, L0_ffn_b1, L0_ffn_W2, L0_ffn_b2, L1_attn_qkv_w, L1_attn_qkv_b, L1_attn_w1w, L1_attn_w2w, L1_attn_r1w, L1_attn_r2w, L1_attn_memv_w, L1_attn_memv_b, L1_attn_memg_w, L1_attn_memg_b, L1_attn_mem_scale, L1_attn_iter_mix, L1_attn_out_w, L1_attn_out_b, L1_attn_decay_logits, L1_xattn_W_q, L1_xattn_W_kv_down, L1_xattn_W_kv_up, L1_xattn_W_out, L1_ffn_W_Q, L1_ffn_W_K, L1_ffn_W_O, L1_ffn_W_inv, L1_ffn_V_fwd, L1_ffn_W_fwd, L1_ffn_U_fwd, L1_ffn_b_fwd, L1_ffn_V_inv, L1_ffn_W_inv_exp, L1_ffn_U_inv, L1_ffn_b_inv, L1_ffn_router_w1, L1_ffn_router_b1, L1_ffn_router_w2, L1_ffn_router_b2, L1_ffn_alpha_bi, L1_ffn_expert_bias):
    import jax
    import jax.numpy as jnp

    def _L0_attn_ref(x, w_qkv, w_o):
        import jax, jax.numpy as jnp
        import numpy as np
        N_HEADS = 1
        LATENT_DIM = 256
        SCALE = 1.0 / float(np.sqrt(LATENT_DIM * N_HEADS))
        B, S, _ = x.shape
        qkv = jnp.einsum('bsd,fd->bsf', x, w_qkv)
        qkv = qkv.reshape(B, S, N_HEADS, 3 * LATENT_DIM).transpose(0, 2, 1, 3)
        q, k, v = jnp.split(qkv, 3, axis=-1)
        attn_logits = jnp.einsum('bhqd,bhkd->bhqk', q, k) * SCALE
        attention = jax.nn.softmax(attn_logits, axis=1)
        values = jnp.einsum('bhqk,bhkd->bhqd', attention, v)
        values = values.transpose(0, 2, 1, 3).reshape(B, S, N_HEADS * LATENT_DIM)
        return jnp.einsum('bsf,of->bso', values, w_o)

    def _L0_xattn_ref(x, historical_data, Wq, Wk, Wv, hist_W, hist_b, hist_ln_g, hist_ln_b, ctx_W1, ctx_b1, ctx_W2, ctx_b2, kg_W1, kg_b1, kg_ln_g, kg_ln_b, kg_W2, kg_b2, proj_W, proj_b, causal_mask):
        import jax, jax.numpy as jnp
        import numpy as np
        from jax import lax
        H = 16
        K1, K2 = (3, 3)
        LN_EPS = 1e-05

        def _ln(x, g, b):
            m = jnp.mean(x, axis=-1, keepdims=True)
            v = jnp.mean(jnp.square(x - m), axis=-1, keepdims=True)
            return (x - m) * lax.rsqrt(v + LN_EPS) * g + b

        def _gelu(x):
            return jax.nn.gelu(x, approximate=False)
        B, T, D = x.shape
        hd = D // H
        scale = hd ** (-0.5)
        q = (x @ Wq).reshape(B, T, H, hd).transpose(0, 2, 1, 3)
        k = (x @ Wk).reshape(B, T, H, hd).transpose(0, 2, 1, 3)
        v = (x @ Wv).reshape(B, T, H, hd).transpose(0, 2, 1, 3)
        attn = jnp.einsum('bhqd,bhkd->bhqk', q, k) * scale
        eh = _gelu(_ln(historical_data @ hist_W + hist_b, hist_ln_g, hist_ln_b))
        aw = _gelu(eh @ ctx_W1 + ctx_b1) @ ctx_W2 + ctx_b2
        aw = jax.nn.softmax(aw, axis=1)
        cc = jnp.sum(eh * aw, axis=1)
        kp = _gelu(_ln(cc @ kg_W1 + kg_b1, kg_ln_g, kg_ln_b)) @ kg_W2 + kg_b2
        kernels = jax.nn.softmax(kp.reshape(B, H, K1 * K2), axis=-1)
        kernels = kernels.reshape(B * H, 1, K1, K2)
        mask = causal_mask[None, None]
        attn0 = jnp.where(mask, 0.0, attn).reshape(1, B * H, T, T)
        attn = lax.conv_general_dilated(attn0, kernels, window_strides=(1, 1), padding=((K1 // 2, K1 // 2), (K2 // 2, K2 // 2)), feature_group_count=B * H, dimension_numbers=('NCHW', 'OIHW', 'NCHW')).reshape(B, H, T, T)
        attn = jnp.where(mask, -jnp.inf, attn)
        p = jax.nn.softmax(attn, axis=-1)
        out = jnp.einsum('bhqk,bhkd->bhqd', p, v)
        out = out.transpose(0, 2, 1, 3).reshape(B, T, D)
        return out @ proj_W + proj_b

    def _L0_ffn_ref(x, norm1_w, norm2_w, Wq, Wdkv, Wuk, Wuv, Wo, ln_g, ln_b, gate_w, gate_b, W1, b1, W2, b2):
        import jax, jax.numpy as jnp
        import numpy as np
        D_MODEL = 256
        N_HEADS = 16
        HEAD_DIM = D_MODEL // N_HEADS
        KV_LATENT = 128
        N_EXPERTS = 4
        D_HIDDEN = 4 * D_MODEL
        B, T = (2, 256)

        def rmsnorm(x, w, eps=1e-06):
            return w * (x * jax.lax.rsqrt(jnp.mean(x * x, axis=-1, keepdims=True) + eps))

        def layernorm(x, g, b, eps=1e-05):
            mu = jnp.mean(x, axis=-1, keepdims=True)
            var = jnp.mean((x - mu) ** 2, axis=-1, keepdims=True)
            return (x - mu) * jax.lax.rsqrt(var + eps) * g + b

        def apply_rope(x):
            t, d = (x.shape[2], x.shape[3])
            half = d // 2
            pos = jnp.arange(t, dtype=x.dtype)[:, None]
            inv_freq = 1.0 / 10000.0 ** (jnp.arange(half, dtype=x.dtype) / half)
            ang = pos * inv_freq[None, :]
            sin, cos = (jnp.sin(ang), jnp.cos(ang))
            x1, x2 = (x[..., :half], x[..., half:])
            return jnp.concatenate([x1 * cos - x2 * sin, x1 * sin + x2 * cos], axis=-1)

        def mla_attention(x, Wq, Wdkv, Wuk, Wuv, Wo, ln_g, ln_b):
            b, t, _ = x.shape
            q = (x @ Wq.T).reshape(b, t, N_HEADS, HEAD_DIM).transpose(0, 2, 1, 3)
            latent = layernorm(x @ Wdkv.T, ln_g, ln_b)
            k = (latent @ Wuk.T).reshape(b, t, N_HEADS, HEAD_DIM).transpose(0, 2, 1, 3)
            v = (latent @ Wuv.T).reshape(b, t, N_HEADS, HEAD_DIM).transpose(0, 2, 1, 3)
            q = apply_rope(q)
            k = apply_rope(k)
            scores = jnp.einsum('bhqd,bhkd->bhqk', q, k) / np.sqrt(HEAD_DIM)
            causal = jnp.tril(jnp.ones((t, t), dtype=bool))
            scores = jnp.where(causal, scores, -jnp.inf)
            attn = jax.nn.softmax(scores, axis=-1)
            out = jnp.einsum('bhqk,bhkd->bhqd', attn, v).transpose(0, 2, 1, 3).reshape(b, t, D_MODEL)
            return out @ Wo.T

        def moe(x, gate_w, gate_b, W1, b1, W2, b2):
            logits = x @ gate_w.T + gate_b
            top = jnp.argmax(logits, axis=-1)
            onehot = jax.nn.one_hot(top, N_EXPERTS, dtype=x.dtype)
            h = jax.nn.relu(jnp.einsum('btd,ehd->bteh', x, W1) + b1)
            y = jnp.einsum('bteh,edh->bted', h, W2) + b2
            return jnp.einsum('bted,bte->btd', y, onehot)
        x = x + mla_attention(rmsnorm(x, norm1_w), Wq, Wdkv, Wuk, Wuv, Wo, ln_g, ln_b)
        x = x + moe(rmsnorm(x, norm2_w), gate_w, gate_b, W1, b1, W2, b2)
        return x

    def _L1_attn_ref(x, qkv_w, qkv_b, w1w, w2w, r1w, r2w, memv_w, memv_b, memg_w, memg_b, mem_scale, iter_mix, out_w, out_b, decay_logits):
        import jax, jax.numpy as jnp
        import numpy as np
        _J6 = jnp.array([[0, 0, 0, 0, 0, 1], [0, 0, 0, 0, -1, 0], [0, 0, 0, 1, 0, 0], [0, 0, 1, 0, 0, 0], [0, -1, 0, 0, 0, 0], [1, 0, 0, 0, 0, 0]], dtype=jnp.float32)
        _PAIRS4 = [(0, 1), (0, 2), (0, 3), (1, 2), (1, 3), (2, 3)]

        def exterior(p1, p2):
            parts = [p1[..., i] * p2[..., j] - p1[..., j] * p2[..., i] for i, j in _PAIRS4]
            L = jnp.stack(parts, axis=-1)
            n = jnp.maximum(jnp.linalg.norm(L, axis=-1, keepdims=True), 1e-12)
            return L / n
        B, T, D = x.shape
        H = decay_logits.shape[0]
        dh = D // H
        pd = 6
        scale = dh ** (-0.5)
        qkv = (x @ qkv_w.T + qkv_b).reshape(B, T, 3, H, dh)
        qkv = jnp.transpose(qkv, (2, 0, 3, 1, 4))
        q, k, v = (qkv[0], qkv[1], qkv[2])
        scores = jnp.einsum('bhtd,bhsd->bhts', q, k) * scale
        causal = jnp.triu(jnp.ones((T, T), dtype=bool), 1)
        scores = jnp.where(causal, -jnp.inf, scores)
        attn = jax.nn.softmax(scores, axis=-1)
        seq_out = jnp.einsum('bhts,bhsd->bhtd', attn, v)
        seq_out = jnp.transpose(seq_out, (0, 2, 1, 3)).reshape(B, T, D)
        x_prev = jnp.concatenate([jnp.zeros((B, 1, D), x.dtype), x[:, :-1]], axis=1)
        w1 = (x_prev @ w1w.T).reshape(B, T, H, 4)
        w2 = (x @ w2w.T).reshape(B, T, H, 4)
        write_lines = exterior(w1, w2)
        r1 = (x @ r1w.T).reshape(B, T, H, 4)
        r2 = (x @ r2w.T).reshape(B, T, H, 4)
        read_lines = exterior(r1, r2)
        Jw = jnp.einsum('bthi,ij->bhtj', write_lines, _J6)
        rd = jnp.transpose(read_lines, (0, 2, 1, 3))
        decays = jax.nn.sigmoid(decay_logits)
        pos = jnp.arange(T, dtype=x.dtype)
        outer = Jw[..., :, None] * Jw[..., None, :]
        decay_inv = (1.0 / jnp.maximum(decays, 1e-06))[:, None] ** pos[None, :]
        outer_scaled = outer * decay_inv[None, :, :, None, None]
        M_cumsum = jnp.cumsum(outer_scaled, axis=2)
        M_cumsum = jnp.concatenate([jnp.zeros((B, H, 1, pd, pd), x.dtype), M_cumsum[:, :, :-1]], axis=2)
        decay_fwd = decays[:, None] ** pos[None, :]
        M_all = M_cumsum * decay_fwd[None, :, :, None, None]
        rd_M = jnp.einsum('bhti,bhtij->bhtj', rd, M_all)
        score_M = jnp.sum(rd_M * rd, axis=-1)
        score_M2 = jnp.sum(rd_M * rd_M, axis=-1)
        alpha = jax.nn.sigmoid(iter_mix)
        mem_score = (1 - alpha) * score_M + alpha * score_M2
        mem_val = x @ memv_w.T + memv_b
        gate = jax.nn.sigmoid(x @ memg_w.T + memg_b)
        mem_score_t = jnp.transpose(mem_score, (0, 2, 1))
        gated = jax.nn.sigmoid(mem_score_t * mem_scale) * gate
        gated = jnp.mean(gated, axis=-1, keepdims=True)
        return (seq_out + gated * mem_val) @ out_w.T + out_b

    def _L1_xattn_ref(x_q, x_kv, indices, W_q, W_kv_down, W_kv_up, W_out):
        import jax, jax.numpy as jnp
        import numpy as np
        B, NQ, NKV, K = (2, 256, 512, 64)
        D, H, LAT = (256, 16, 128)
        HD = D // H
        SCALE = 1.0 / np.sqrt(HD)
        b, nq, d = x_q.shape
        q = (x_q @ W_q.T).reshape(b, nq, H, HD)
        c_kv = x_kv @ W_kv_down.T
        c_sel = c_kv[jnp.arange(b)[:, None, None], indices]
        kv = (c_sel @ W_kv_up.T).reshape(b, nq, K, 2, H, HD)
        k = kv[:, :, :, 0]
        v = kv[:, :, :, 1]
        scores = jnp.einsum('bqhd,bqkhd->bqkh', q, k) * SCALE
        attn = jax.nn.softmax(scores, axis=2)
        out = jnp.einsum('bqkh,bqkhd->bqhd', attn, v).reshape(b, nq, d)
        return out @ W_out.T

    def _L1_ffn_ref(x, W_Q, W_K, W_O, W_inv, V_fwd, W_fwd, U_fwd, b_fwd, V_inv, W_inv_exp, U_inv, b_inv, router_w1, router_b1, router_w2, router_b2, alpha_bi, expert_bias):
        import jax, jax.numpy as jnp
        import numpy as np
        B, T, D, R, KEXP = (4, 1024, 256, 64, 8)
        RH = max(D, 32)
        SCALE = 0.02

        def _fused_branch(Q_side, K_side, V, W, U, b, router_w1, router_b1, router_w2, router_b2, expert_bias):
            xV = jnp.einsum('btd,kdr->btkr', Q_side, V)
            yW = jnp.einsum('btd,kdr->btkr', K_side, W)
            cum_yW = jnp.cumsum(yW, axis=1)
            prod = xV * cum_yW
            h = jax.nn.gelu(Q_side @ router_w1.T + router_b1, approximate=False)
            logits = h @ router_w2.T + router_b2 + expert_bias
            weights = jax.nn.softmax(logits, axis=-1)
            out = jnp.einsum('btkr,kdr->btd', prod * weights[..., None], U)
            out = out + weights @ b
            n_valid = jnp.arange(1, Q_side.shape[1] + 1, dtype=Q_side.dtype)
            return out / n_valid[None, :, None]
        Q = x @ W_Q.T
        K = x @ W_K.T
        invQ = Q @ W_inv.T
        invK = K @ W_inv.T
        fwd = _fused_branch(Q, K, V_fwd, W_fwd, U_fwd, b_fwd, router_w1, router_b1, router_w2, router_b2, expert_bias)
        inv = _fused_branch(invQ, invK, W_inv_exp, V_inv, U_inv, b_inv, router_w1, router_b1, router_w2, router_b2, expert_bias)
        out = fwd + alpha_bi * inv
        return out @ W_O.T
    x = _layernorm(x + _L0_attn_ref(x, L0_attn_w_qkv, L0_attn_w_o), axis=-1)
    x = _layernorm(x + _L0_xattn_ref(x, ctx_1024, L0_xattn_Wq, L0_xattn_Wk, L0_xattn_Wv, L0_xattn_hist_W, L0_xattn_hist_b, L0_xattn_hist_ln_g, L0_xattn_hist_ln_b, L0_xattn_ctx_W1, L0_xattn_ctx_b1, L0_xattn_ctx_W2, L0_xattn_ctx_b2, L0_xattn_kg_W1, L0_xattn_kg_b1, L0_xattn_kg_ln_g, L0_xattn_kg_ln_b, L0_xattn_kg_W2, L0_xattn_kg_b2, L0_xattn_proj_W, L0_xattn_proj_b, mask_SxS_bc0), axis=-1)
    x = _layernorm(x + _L0_ffn_ref(x, L0_ffn_norm1_w, L0_ffn_norm2_w, L0_ffn_Wq, L0_ffn_Wdkv, L0_ffn_Wuk, L0_ffn_Wuv, L0_ffn_Wo, L0_ffn_ln_g, L0_ffn_ln_b, L0_ffn_gate_w, L0_ffn_gate_b, L0_ffn_W1, L0_ffn_b1, L0_ffn_W2, L0_ffn_b2), axis=-1)
    x = _layernorm(x + _L1_attn_ref(x, L1_attn_qkv_w, L1_attn_qkv_b, L1_attn_w1w, L1_attn_w2w, L1_attn_r1w, L1_attn_r2w, L1_attn_memv_w, L1_attn_memv_b, L1_attn_memg_w, L1_attn_memg_b, L1_attn_mem_scale, L1_attn_iter_mix, L1_attn_out_w, L1_attn_out_b, L1_attn_decay_logits), axis=-1)
    x = _layernorm(x + _L1_xattn_ref(x, ctx_1024, itok_BxSx64_0_2047, L1_xattn_W_q, L1_xattn_W_kv_down, L1_xattn_W_kv_up, L1_xattn_W_out), axis=-1)
    x = _layernorm(x + _L1_ffn_ref(x, L1_ffn_W_Q, L1_ffn_W_K, L1_ffn_W_O, L1_ffn_W_inv, L1_ffn_V_fwd, L1_ffn_W_fwd, L1_ffn_U_fwd, L1_ffn_b_fwd, L1_ffn_V_inv, L1_ffn_W_inv_exp, L1_ffn_U_inv, L1_ffn_b_inv, L1_ffn_router_w1, L1_ffn_router_b1, L1_ffn_router_w2, L1_ffn_router_b2, L1_ffn_alpha_bi, L1_ffn_expert_bias), axis=-1)
    return x

_drawn_inputs = setup_inputs


def setup_inputs(seed=0):
    import zlib

    import numpy as np

    out = dict(_drawn_inputs(seed))
    spreads = {'L0_xattn_hist_b': (0.0, 0.494),
     'L0_xattn_hist_ln_g': (1.0, 0.6),
     'L0_xattn_hist_ln_b': (0.0, 0.483),
     'L0_xattn_ctx_b1': (0.0, 0.8),
     'L0_xattn_kg_b1': (0.0, 0.646),
     'L0_xattn_kg_ln_g': (1.0, 0.6),
     'L0_xattn_kg_ln_b': (0.0, 0.681),
     'L0_xattn_kg_b2': (0.0, 0.661),
     'L0_xattn_proj_b': (0.0, 0.1),
     'L0_ffn_norm1_w': (1.0, 0.2),
     'L0_ffn_norm2_w': (1.0, 0.2),
     'L0_ffn_ln_g': (1.0, 0.2),
     'L0_ffn_ln_b': (0.0, 0.1),
     'L0_ffn_gate_b': (0.0, 0.1),
     'L0_ffn_b1': (0.0, 0.322),
     'L0_ffn_b2': (0.0, 0.1),
     'L1_attn_qkv_b': (0.0, 0.279),
     'L1_attn_memv_b': (0.0, 0.665),
     'L1_attn_memg_b': (0.0, 0.8),
     'L1_attn_mem_scale': (0.10000000149011612, 0.6),
     'L1_attn_out_b': (0.0, 0.1),
     'L1_attn_decay_logits': (4.599999904632568, 0.6),
     'L1_ffn_b_fwd': (0.0, 2.0),
     'L1_ffn_b_inv': (0.0, 2.0),
     'L1_ffn_router_b1': (0.0, 2.0),
     'L1_ffn_router_b2': (0.0, 2.0),
     'L1_ffn_expert_bias': (0.0, 2.0)}
    factors = {'L0_xattn_ctx_W1': 5.719,
     'L0_xattn_ctx_W2': 6.611,
     'L1_attn_w1w': 8.0,
     'L1_attn_w2w': 64.0,
     'L1_attn_r1w': 64.0,
     'L1_attn_r2w': 8.0,
     'L1_attn_memg_w': 8.0,
     'L1_ffn_W_Q': 7.452,
     'L1_ffn_W_K': 7.673,
     'L1_ffn_W_O': 6.935,
     'L1_ffn_W_inv': 8.0,
     'L1_ffn_V_fwd': 8.0,
     'L1_ffn_W_fwd': 8.0,
     'L1_ffn_U_fwd': 8.0,
     'L1_ffn_V_inv': 8.0,
     'L1_ffn_W_inv_exp': 8.0,
     'L1_ffn_U_inv': 8.0,
     'L1_ffn_router_w1': 8.0,
     'L1_ffn_router_w2': 8.0}
    for name, (base, spread) in spreads.items():
        noise = np.random.default_rng([zlib.crc32(name.encode()), seed]).standard_normal(out[name].shape)
        drawn = base * np.exp(spread * noise) if base else spread * noise
        out[name] = jnp.asarray(drawn.astype(out[name].dtype))
    for name, factor in factors.items():
        out[name] = (out[name] * factor).astype(out[name].dtype)
    return out
```

```python
from contextlib import ExitStack

import numpy as np

import concourse.bass as bass
from concourse import mybir

F32 = mybir.dt.float32
BF16 = mybir.dt.bfloat16
I32 = mybir.dt.int32
ALU = mybir.AluOpType
ACT = mybir.ActivationFunctionType
AX = mybir.AxisListType

P = 128
B, T, D = 8, 256, 256
TT = T // P
KT = D // P
H, HD = 16, 16
SCALE = 0.25
HC = 512
NE, HID = 4, 1024
MT = HID // P
LAT = 128
KE, R = 8, 64
NI = 64
NEG = -1.0e30
LN_EPS = 1e-5
PAIRS = [(0, 1), (0, 2), (0, 3), (1, 2), (1, 3), (2, 3)]

HIST = [("hist_W", KT * HC), ("ctx_W1", 4 * P), ("ctx_W2", 1), ("ctx_b1", 1), ("kg_W1", 4 * D), ("kg_W2", KT * 144),
        ("hist_b", HC), ("hist_g", HC), ("hist_lb", HC), ("ctx_b2", 1),
        ("kg_b1", D), ("kg_g", D), ("kg_lb", D), ("kg_b2", 144)]
LAY0 = [("wv", 512), ("wo", 512), ("xqkv", KT * 768), ("xproj", 512), ("mq", 512), ("mdkv", KT * LAT), ("mukv", 512),
        ("mo", 512), ("gate", KT * NE), ("W1", KT * NE * HID), ("W2", NE * MT * D), ("w1w", KT * 64), ("w2w", KT * 64),
        ("rw", KT * P), ("memg", KT * H), ("proj_b", D), ("norm1", D), ("norm2", D), ("ln_g", LAT), ("ln_b", LAT),
        ("gate_b", NE), ("b1", NE * MT), ("b2", NE * D), ("cos", TT * 8), ("sin", TT * 8)]
LAY1 = [("qkv", KT * 768), ("memv", 512), ("outw", 512), ("yq", 512), ("ydown", KT * LAT), ("yup", 512), ("yout", 512),
        ("fQ", 512), ("fK", 512), ("fO", 512), ("finv", 512), ("fV0", 1024), ("fW0", 1024), ("fV1", 1024), ("fW1", 1024),
        ("fU0", 1024), ("fU1", 1024), ("r1", 512), ("r2", KT * KE), ("r1b", KT), ("r2b", KE), ("eb", KE), ("alpha", 1),
        ("qkv_b", 768), ("memv_b", D), ("out_b", D), ("b8", 2 * D), ("sel8", 4 * P), ("rn", TT)]
CONST = [("ident", P), ("causal", TT * T), ("shift", 3 * P), ("halo_up", 32), ("halo_dn", 32), ("iota", T),
         ("half", 1), ("decay", 1), ("mscale", 1), ("memg_b", 1), ("mix", 1), ("bsel", B)]


def offsets(table):
    at, out = 0, {}
    for name, n in table:
        out[name] = (at, n)
        at += n
    return out, at


HIST_AT, HIST_N = offsets(HIST)
LAY0_AT, LAY0_N = offsets(LAY0)
LAY1_AT, LAY1_N = offsets(LAY1)
CONST_AT, CONST_N = offsets(CONST)


class Steps:

    def __init__(self, eng, own):
        self.eng, self.own, self.count, self.open = eng, own, {}, {}

    def post(self, ins, sem=None):
        sem = self.own if sem is None else sem
        n = self.count.get(sem.name, 0) + 1
        self.count[sem.name] = n
        ins.then_inc(sem, 1)
        self.open[sem.name] = (sem, n)
        return ins

    def settle(self):
        for sem, n in self.open.values():
            self.eng.wait_ge(sem, n)
        self.open = {}


class Ring:

    def __init__(self, banks, full, free):
        self.banks, self.full, self.free, self.filled, self.taken = banks, full, free, 0, 0

    def claim(self, pe):
        i, n = self.filled % len(self.banks), self.filled // len(self.banks)
        if n:
            pe.wait_ge(self.free[i], n)
        return self.banks[i]

    def fill(self, ins):
        ins.then_inc(self.full[self.filled % len(self.banks)], 1)
        self.filled += 1

    def moved(self, pe):
        for i in range(len(self.banks)):
            n = (self.filled - i + len(self.banks) - 1) // len(self.banks)
            if n:
                pe.wait_ge(self.free[i], n)

    def take(self, eng):
        i = self.taken % len(self.banks)
        eng.wait_ge(self.full[i], self.taken // len(self.banks) + 1)
        return self.banks[i]

    def release(self, steps, ins):
        steps.post(ins, self.free[self.taken % len(self.banks)])
        self.taken += 1


def decoder(nc, x, xT, ctxT, itok, hist, lay0, lay1, const, negm, feat, gate_d, out):
    with ExitStack() as ctx:
        names = {}

        def sb(name, shape, dt=F32):
            return ctx.enter_context(nc.sbuf_tensor(name, shape, dt))

        def S(name):
            if name not in names:
                names[name] = ctx.enter_context(nc.semaphore(name))
            return names[name]

        SC = ctx.enter_context(nc.psum_tensor("SC", [P, 512], F32))
        SM = [ctx.enter_context(nc.psum_tensor(f"SM{i}", [P, 512], F32)) for i in range(2)]
        PT = [ctx.enter_context(nc.psum_tensor(f"PT{i}", [P, 512], F32)) for i in range(2)]
        OA = ctx.enter_context(nc.psum_tensor("OA", [P, 512], F32))
        PJ = [ctx.enter_context(nc.psum_tensor(f"PJ{i}", [P, 512], F32)) for i in range(2)]
        sm_full = [S(f"sm_full{i}") for i in range(2)]
        pt_full, pt_free = [S(f"pt_full{i}") for i in range(2)], [S(f"pt_free{i}") for i in range(2)]
        sc_full, sc_free = S("sc_full"), S("sc_free")
        oa_free = S("oa_free")
        pj_full, pj_free = [S(f"pj_full{i}") for i in range(2)], [S(f"pj_free{i}") for i in range(2)]

        arena = sb("arena", [P, max(LAY0_N, LAY1_N + 7700, HIST_N)])
        const_sb = sb("const_sb", [P, CONST_N])
        Xall = sb("Xall", [P, B, TT, D])
        KB = sb("KB", [P, B * 144])

        def hist_w(name):
            a, n = HIST_AT[name]
            return arena[:, a:a + n]

        def w0(name):
            a, n = LAY0_AT[name]
            return arena[:, a:a + n]

        def w1(name):
            a, n = LAY1_AT[name]
            return arena[:, a:a + n]

        def c(name):
            a, n = CONST_AT[name]
            return const_sb[:, a:a + n]

        def k3(ap, k):
            return ap.rearrange("p (k n) -> p k n", k=k)

        ident = c("ident")

        identb = sb("identb", [P, P], BF16)
        notmask = sb("notmask", [P, TT, T])
        masks = sb("masks", [P, 2, TT, T], BF16)
        ones = sb("ones", [P, T])
        Xin = sb("Xin", [P, TT, D])
        X = sb("X", [P, TT, D])
        X2 = sb("X2", [P, TT, D])
        Y = sb("Y", [P, TT, D])
        Z = sb("Z", [P, TT, D])
        XT = sb("XT", [P, KT, T + 1])
        YT = sb("YT", [P, KT, T])
        CT = sb("CT", [P, KT, T])
        qpad = sb("qpad", [P, TT, H, 32])
        kpad = sb("kpad", [P, TT, H, 32])
        V = sb("V", [P, TT, D])
        QT = sb("QT", [P, 4, T])
        mask_in = QT[:, 0:2, :].bitcast(I32)
        KTr = sb("KTr", [P, 4, T])
        PR = [sb(f"PR{i}", [P, TT, T]) for i in range(2)]
        PS = [sb(f"PS{i}", [P, 2, T]) for i in range(2)]
        AM = [sb(f"AM{i}", [P, TT, T + 2]) for i in range(2)]
        band = [sb(f"band{i}", [P, 3, P]) for i in range(2)]
        btmp = sb("btmp", [P, 3, P])
        haloU = sb("haloU", [P, H, 3, 32])
        haloD = sb("haloD", [P, H, 3, 32])
        kcur = sb("kcur", [P, H, 3, 3])
        negmax = sb("negmax", [P, H, TT])
        rsum = sb("rsum", [P, TT, H])
        rinv = sb("rinv", [P, TT, H])
        small = sb("small", [P, 128])
        stats = sb("stats", [P, TT, 6])
        mv = sb("mv", [P, TT, 2])
        var = sb("var", [P, TT])
        rstd = sb("rstd", [P, TT])
        CC = sb("CC", [P, B, 4])
        big = sb("big", [P, 4096])
        OUT = sb("OUT", [P, TT, D])
        Gt = sb("Gt", [P, TT, B])


        def flip(pe, ring, src, ready=None):
            bank = ring.claim(pe)
            for k in range(KT):
                for t in range(TT):
                    ins = pe.transpose(bank[:, k * T + t * P:k * T + (t + 1) * P], src[:, t, k * P:(k + 1) * P], ident)
            ring.fill(ins)

        def rows(pe, ring, actT, w, n0, n1):
            bank = ring.claim(pe)
            n = n1 - n0
            for t in range(TT):
                for k in range(KT):
                    ins = pe.matmul(bank[:, t * n:(t + 1) * n], actT[:, k, t * P:(t + 1) * P], w[:, k, n0:n1],
                                    start=k == 0, stop=k == KT - 1)
            ring.fill(ins)

        def columns(pe, bank, w, actT, m0=0, stop=True):
            for m in range(2):
                for k in range(KT):
                    ins = pe.matmul(bank[:, m * T:(m + 1) * T], w[:, k, m0 + m * P:m0 + (m + 1) * P], actT[:, k, :],
                                    start=k == 0, stop=k == KT - 1)
            return ins

        def two(bank, n=256):
            return bank[:, 0:2 * n].rearrange("p (a b) -> p a b", a=2)

        def move(dve, st, ring, dst):
            bank = ring.take(dve)
            ring.release(st, dve.tensor_copy(dst, two(bank)))

        def root_dve(dve, st, src, scale, eps, n):
            st.post(dve.tensor_scalar(var[:], src, scale, eps, ALU.mult, ALU.add), S("var_ready"))
            dve.wait_ge(S("rstd_ready"), n)

        def root_pool(pool, n):
            pool.wait_ge(S("var_ready"), n)
            pool.tensor_tensor(rstd[:], var[:], c("half").broadcast_to([P, TT]), ALU.pow).then_inc(S("rstd_ready"), 1)

        def layernorm(dve, st, dst, src, n, flag):
            for t in range(TT):
                st.post(dve.bn_stats(stats[:, t, :], src[:, t, :]))
            st.settle()
            for t in range(TT):
                st.post(dve.bn_aggr(mv[:, t, :], stats[:, t, :]))
            st.settle()
            root_dve(dve, st, mv[:, :, 1], 1.0, LN_EPS, n)
            for t in range(TT):
                st.post(dve.tensor_scalar(dst[:, t, :], src[:, t, :], mv[:, t, 0:1], rstd[:, t:t + 1],
                                          ALU.subtract, ALU.mult), S(flag))

        def rmsnorm(dve, st, dst, src, weight, n, flag):
            for t in range(TT):
                st.post(dve.scalar_tensor_tensor(dst[:, t, :], src[:, t, :], 1.0, src[:, t, :], ALU.mult, ALU.mult,
                                                 accum_out=small[:, 100 + t:101 + t]))
            st.settle()
            root_dve(dve, st, small[:, 100:102], 1.0 / D, 1e-6, n)
            st.settle()
            for t in range(TT):
                st.post(dve.scalar_tensor_tensor(dst[:, t, :], src[:, t, :], rstd[:, t:t + 1], weight,
                                                 ALU.mult, ALU.mult), S(flag))

        def flip_heads(pe, ring, padded):
            for g2 in range(2):
                bank = ring.claim(pe)
                for g in range(2):
                    for t in range(TT):
                        src = padded[:, t, (2 * g2 + g) * 4:(2 * g2 + g) * 4 + 4, :].rearrange("p h d -> p (h d)")
                        ins = pe.transpose(bank[:, g * T + t * P:g * T + (t + 1) * P], src, ident)
                ring.fill(ins)

        def move_heads(dve, st, ring, dst):
            for g2 in range(2):
                bank = ring.take(dve)
                ring.release(st, dve.tensor_copy(dst[:, 2 * g2:2 * g2 + 2, :], two(bank)))

        def attention_pe(pe, mode, inst):
            base = inst * H

            def qk(bank, h, stop):
                i, g = 32 * (h % 4), h // 4
                for t in range(TT):
                    ins = pe.matmul(bank[:, t * T:(t + 1) * T], QT[i:i + HD, g, t * P:(t + 1) * P], KTr[i:i + HD, g, :],
                                    start=True, stop=stop)
                    if not stop:
                        ins = pe.matmul(bank[:, t * T:(t + 1) * T], identb[:], masks[:, mode_mask, t, :],
                                        start=False, stop=True)
                return ins

            mode_mask = 1 if mode == "causal" else 0

            def scores(h):
                n = base + h
                if mode == "conv":
                    if h:
                        pe.wait_ge(sc_free, h)
                    qk(SC, h, True).then_inc(sc_full, 1)
                else:
                    if n >= 2:
                        pe.wait_ge(S("exp_done"), 2 * (n - 1))
                    qk(SM[n % 2], h, False).then_inc(sm_full[n % 2], 1)

            def conv(h):
                n = base + h
                if n >= 2:
                    pe.wait_ge(S("exp_done"), 2 * (n - 1))
                pe.wait_ge(sc_free, h + 1)
                pe.wait_ge(S("band_ready"), h + 1)
                a, bank, bd = AM[h % 2], SM[n % 2], band[h % 2]
                for t in range(TT):
                    o = t * T
                    for s in range(3):
                        pe.matmul(bank[:, o:o + T], bd[:, s, :], a[:, t, s:s + T], start=s == 0, stop=False)
                    for s in range(3):
                        if t == 0:
                            pe.matmul(bank[96:128, o:o + T], haloU[0:1, h, s, :], a[0:1, 1, s:s + T],
                                      start=False, stop=False, skip_group_check=True)
                        else:
                            pe.matmul(bank[0:32, o:o + T], haloD[96:128, h, s, :], a[96:128, 0, s:s + T],
                                      start=False, stop=False, skip_group_check=True)
                    ins = pe.matmul(bank[:, o:o + T], identb[:], masks[:, 0, t, :], start=False, stop=True)
                ins.then_inc(sm_full[n % 2], 1)

            def flip_probs(h):
                n = base + h
                if mode == "count":
                    pe.wait_ge(S("weighted"), 2 * (h + 1))
                else:
                    pe.wait_ge(S("exp_done"), 2 * (n + 1))
                if n >= 2:
                    pe.wait_ge(pt_free[n % 2], n // 2)
                bank = PT[n % 2]
                for k in range(TT):
                    for t in range(TT):
                        ins = pe.transpose(bank[:, k * T + t * P:k * T + (t + 1) * P],
                                           PR[n % 2][:, t, k * P:(k + 1) * P], ident)
                ins.then_inc(pt_full[n % 2], 1)

            def values(h):
                n = base + h
                pe.wait_ge(pt_free[n % 2], n // 2 + 1)
                if h == 0 and inst:
                    pe.wait_ge(oa_free, inst)
                for t in range(TT):
                    for k in range(TT):
                        ins = pe.matmul(OA[:, t * D + h * HD:t * D + (h + 1) * HD], PS[n % 2][:, k, t * P:(t + 1) * P],
                                        V[:, k, h * HD:(h + 1) * HD], start=k == 0, stop=k == TT - 1)
                ins.then_inc(S("values_done"), 1)

            lag = {"conv": 2, "causal": 1, "count": 2}[mode]
            for s in range(H + lag + 1):
                if s < H:
                    scores(s)
                if mode == "conv" and 1 <= s <= H:
                    conv(s - 1)
                if lag <= s < H + lag:
                    flip_probs(s - lag)
                if s > lag:
                    values(s - lag - 1)

        def attention_act(act, mode, inst):
            for h in range(H):
                n = inst * H + h
                act.wait_ge(S("max_ready"), n + 1)
                if n >= 2:
                    act.wait_ge(pt_full[n % 2], n // 2)
                for t in range(TT):
                    if mode == "count":
                        ins = act.activation(PR[n % 2][:, t, :], SM[n % 2][:, t * T:(t + 1) * T], ACT.Exp,
                                             bias=negmax[:, h, t:t + 1])
                    else:
                        ins = act.activation(PR[n % 2][:, t, :], SM[n % 2][:, t * T:(t + 1) * T], ACT.Exp,
                                             bias=negmax[:, h, t:t + 1], accum_out=rsum[:, t, h:h + 1])
                    ins.then_inc(S("exp_done"), 1)

        def attention_dve(dve, st, mode, inst, counts=None):
            base = inst * H

            def mask_scores(h):
                if h >= 2:
                    dve.wait_ge(sm_full[(base + h) % 2], (base + h) // 2)
                dve.wait_ge(sc_full, h + 1)
                st.post(dve.tensor_tensor(AM[h % 2][:, :, 1:T + 1], two(SC), notmask[:], ALU.mult), sc_free)

            def row_max(h):
                n = base + h
                dve.wait_ge(sm_full[n % 2], n // 2 + 1)
                st.post(dve.tensor_reduce(negmax[:, h, :], two(SM[n % 2]), AX.X, ALU.max, negate=True), S("max_ready"))

            def weight(h):
                n = base + h
                dve.wait_ge(S("exp_done"), 2 * (n + 1))
                for t in range(TT):
                    st.post(dve.scalar_tensor_tensor(PR[n % 2][:, t, :], PR[n % 2][:, t, :], 1.0, counts[:, t, :],
                                                     ALU.mult, ALU.mult, accum_out=rsum[:, t, h:h + 1]), S("weighted"))

            def move_probs(h):
                n = base + h
                dve.wait_ge(pt_full[n % 2], n // 2 + 1)
                if n >= 2:
                    dve.wait_ge(S("values_done"), n - 1)
                st.post(dve.tensor_copy(PS[n % 2][:], two(PT[n % 2])), pt_free[n % 2])

            if mode == "conv":
                for s in range(H + 2):
                    if s < H:
                        mask_scores(s)
                    if 1 <= s <= H:
                        row_max(s - 1)
                    if s >= 2:
                        move_probs(s - 2)
            elif mode == "causal":
                for s in range(H + 1):
                    if s < H:
                        row_max(s)
                    if s >= 1:
                        move_probs(s - 1)
            else:
                for s in range(H + 2):
                    if s < H:
                        row_max(s)
                    if 1 <= s <= H:
                        weight(s - 1)
                    if s >= 2:
                        move_probs(s - 2)
            dve.wait_ge(S("exp_done"), 2 * (base + H))
            st.settle()
            st.post(dve.reciprocal(rinv[:], rsum[:]))
            st.settle()
            dve.wait_ge(S("values_done"), base + H)
            st.post(dve.tensor_tensor(Y[:].rearrange("p t (h d) -> p (t h) d", h=H),
                                      OA[:].rearrange("p (t h d) -> p (t h) d", t=TT, h=H),
                                      rinv[:].rearrange("p t h -> p (t h)").unsqueeze(2).broadcast_to([P, TT * H, HD]),
                                      ALU.mult), oa_free)

        def clear_block():
            with nc.Block() as block:
                @block.sync
                def _(sp):
                    for s in names.values():
                        sp.sem_clear(s)

        with nc.Block() as block:
            @block.sync
            def _(sp):
                sp.dma_start(const_sb[:], const).then_inc(S("const_in"), 16)
                sp.dma_start(mask_in, negm).then_inc(S("const_in"), 16)
                sp.dma_start(arena[:, 0:HIST_N], hist).then_inc(S("hist_in"), 16)

            @block.vector
            def _(dve):
                st = Steps(dve, S("dve"))
                st.post(dve.memset(qpad[:], 0.0))
                st.post(dve.memset(kpad[:], 0.0))
                st.post(dve.memset(ones[:], 1.0))
                st.post(dve.memset(XT[:], 0.0))
                for i in range(2):
                    st.post(dve.memset(AM[i][:], 0.0))
                dve.wait_ge(S("const_in"), 32)
                st.post(dve.tensor_copy(identb[:], ident))
                st.post(dve.tensor_scalar(masks[:, 0], mask_in, NEG, None, ALU.mult))
                st.post(dve.tensor_scalar(masks[:, 1], k3(c("causal"), TT), NEG, None, ALU.mult))
                st.post(dve.tensor_scalar(notmask[:], mask_in, -1.0, 1.0, ALU.mult, ALU.add))
                dve.wait_ge(S("hist_in"), 16)
                st.settle()
        clear_block()

        EH = big[:, 0:1024].rearrange("p (t n) -> p t n", t=TT)
        EG = big[:, 1024:2048].rearrange("p (t n) -> p t n", t=TT)
        EHT = big[:, 2048:3072].rearrange("p (k t) -> p k t", k=4)
        A1 = big[:, 3072:3328]
        awr = big[0:1, 3328:3584]
        awc = small[:, 0:2]
        with nc.Fori(0, B) as b:
            with nc.Block() as block:
                ring = Ring(PJ, pj_full, pj_free)

                @block.sync
                def _(sp):
                    sp.dma_start(CT[:], ctxT[bass.ds(b, 1)].rearrange("o p k t -> (o p) k t")).then_inc(S("ctx_in"), 16)
                    sp.wait_ge(S("ctx_in"), 16)

                @block.tensor
                def _(pe):
                    pe.wait_ge(S("ctx_in"), 16)
                    W = k3(hist_w("hist_W"), KT)
                    for t in range(TT):
                        bank = ring.claim(pe)
                        for k in range(KT):
                            ins = pe.matmul(bank[:], CT[:, k, t * P:(t + 1) * P], W[:, k, :], start=k == 0, stop=k == 1)
                        ring.fill(ins)
                    pe.wait_ge(S("gelu_done"), TT)
                    for c2 in range(2):
                        bank = ring.claim(pe)
                        for cc in range(2):
                            for t in range(TT):
                                f = (2 * c2 + cc) * P
                                ins = pe.transpose(bank[:, cc * T + t * P:cc * T + (t + 1) * P], EG[:, t, f:f + P], ident)
                        ring.fill(ins)
                    ring.moved(pe)
                    for k in range(4):
                        ins = pe.matmul(SM[0][:, 0:T], k3(hist_w("ctx_W1"), 4)[:, k, :], EHT[:, k, :],
                                        start=k == 0, stop=k == 3)
                    ins.then_inc(sm_full[0], 1)
                    pe.wait_ge(S("gelu_done"), TT + 1)
                    bank = ring.claim(pe)
                    ring.fill(pe.matmul(bank[0:1, 0:T], hist_w("ctx_W2"), A1, start=True, stop=True))
                    pe.wait_ge(S("aw_ready"), 1)
                    bank = ring.claim(pe)
                    for t in range(TT):
                        ins = pe.matmul(bank[:, t:t + 1], awr[:, t * P:(t + 1) * P], ones[0:1, 0:1], start=True, stop=True)
                    ring.fill(ins)
                    ring.moved(pe)
                    bank = ring.claim(pe)
                    for f in range(4):
                        for t in range(TT):
                            ins = pe.matmul(bank[:, f:f + 1], EG[:, t, f * P:(f + 1) * P], awc[:, t:t + 1],
                                            start=t == 0, stop=t == 1)
                    ring.fill(ins)

                @block.vector
                def _(dve):
                    st = Steps(dve, S("dve"))
                    for t in range(TT):
                        bank = ring.take(dve)
                        ring.release(st, dve.tensor_tensor(EH[:, t, :], bank[:], hist_w("hist_b"), ALU.add))
                    st.settle()
                    layernorm(dve, st, EH, EH, 1, "eh_norm")
                    st.settle()
                    for t in range(TT):
                        st.post(dve.tensor_tensor(EH[:, t, :], EH[:, t, :], hist_w("hist_g"), ALU.mult))
                    st.settle()
                    for t in range(TT):
                        st.post(dve.tensor_tensor(EH[:, t, :], EH[:, t, :], hist_w("hist_lb"), ALU.add), S("eh_ready"))
                    for c2 in range(2):
                        move(dve, st, ring, EHT[:, 2 * c2:2 * c2 + 2, :])
                    bank = ring.take(dve)
                    ring.release(st, dve.tensor_scalar(awr, bank[0:1, 0:T], hist_w("ctx_b2")[0:1, :], None, ALU.add))
                    st.settle()
                    st.post(dve.tensor_reduce(small[0:1, 8:9], awr, AX.X, ALU.max, negate=True), S("awmax"))
                    dve.wait_ge(S("awexp"), 1)
                    st.post(dve.reciprocal(small[0:1, 10:11], small[0:1, 9:10]))
                    st.settle()
                    st.post(dve.tensor_scalar(awr, awr, small[0:1, 10:11], None, ALU.mult), S("aw_ready"))
                    bank = ring.take(dve)
                    ring.release(st, dve.tensor_copy(awc, bank[:, 0:2]))
                    bank = ring.take(dve)
                    ring.release(st, dve.tensor_copy(CC[:, bass.ds(b, 1), :].rearrange("p o f -> p (o f)"), bank[:, 0:4]))
                    st.settle()

                @block.gpsimd
                def _(pool):
                    root_pool(pool, 1)

                @block.scalar
                def _(act):
                    for t in range(TT):
                        act.wait_ge(S("eh_ready"), t + 1)
                        act.activation(EG[:, t, :], EH[:, t, :], ACT.Gelu).then_inc(S("gelu_done"), 1)
                    act.wait_ge(sm_full[0], 1)
                    act.activation(A1, SM[0][:, 0:T], ACT.Gelu, bias=hist_w("ctx_b1")).then_inc(S("gelu_done"), 1)
                    act.wait_ge(S("awmax"), 1)
                    act.activation(awr, awr, ACT.Exp, bias=small[0:1, 8:9],
                                   accum_out=small[0:1, 9:10]).then_inc(S("awexp"), 1)
            clear_block()

        KP = big[0:B, 0:256]
        KG = big[0:B, 256:512]
        KPT = big[:, 512:528].rearrange("p (k b) -> p k b", k=2)
        K2 = big[0:B, 528:672]
        K2v = K2.rearrange("b (h n) -> b h n", n=9)
        K1 = big[0:1, 672:672 + B * 144]
        with nc.Block() as block:
            ring = Ring(PJ, pj_full, pj_free)

            @block.tensor
            def _(pe):
                bank = ring.claim(pe)
                for f in range(4):
                    ins = pe.matmul(bank[0:B, 0:256], CC[:, :, f], k3(hist_w("kg_W1"), 4)[:, f, :], start=f == 0, stop=f == 3)
                ring.fill(ins)
                pe.wait_ge(S("gelu_done"), 1)
                bank = ring.claim(pe)
                for k in range(2):
                    ins = pe.transpose(bank[:, k * B:(k + 1) * B], KG[:, k * P:(k + 1) * P], ident[0:B, 0:B])
                ring.fill(ins)
                ring.moved(pe)
                bank = ring.claim(pe)
                for k in range(2):
                    ins = pe.matmul(bank[0:B, 0:144], KPT[:, k, :], k3(hist_w("kg_W2"), 2)[:, k, :], start=k == 0, stop=k == 1)
                ring.fill(ins)
                pe.wait_ge(S("k_row"), 16 * B)
                for i in range(3):
                    bank = ring.claim(pe)
                    ring.fill(pe.matmul(bank[:, 0:384], ones[0:1, 0:P], K1[:, i * 384:(i + 1) * 384], start=True, stop=True))

            @block.vector
            def _(dve):
                st = Steps(dve, S("dve"))
                bank = ring.take(dve)
                ring.release(st, dve.tensor_tensor(KP, bank[0:B, 0:256], hist_w("kg_b1")[0:B, :], ALU.add))
                st.post(dve.memset(var[:], 1.0))
                st.settle()
                st.post(dve.bn_stats(stats[0:B, 0, :], KP))
                st.settle()
                st.post(dve.bn_aggr(mv[0:B, 0, :], stats[0:B, 0, :]))
                st.settle()
                st.post(dve.tensor_scalar(var[0:B, 0:1], mv[0:B, 0, 1:2], LN_EPS, None, ALU.add), S("var_ready"))
                dve.wait_ge(S("rstd_ready"), 1)
                st.post(dve.tensor_scalar(KP, KP, mv[0:B, 0, 0:1], rstd[0:B, 0:1], ALU.subtract, ALU.mult))
                st.settle()
                st.post(dve.tensor_tensor(KP, KP, hist_w("kg_g")[0:B, :], ALU.mult))
                st.settle()
                st.post(dve.tensor_tensor(KP, KP, hist_w("kg_lb")[0:B, :], ALU.add), S("kp_ready"))
                bank = ring.take(dve)
                ring.release(st, dve.tensor_copy(KPT, bank[:, 0:2 * B].rearrange("p (k b) -> p k b", k=2)))
                bank = ring.take(dve)
                ring.release(st, dve.tensor_tensor(K2, bank[0:B, 0:144], hist_w("kg_b2")[0:B, :], ALU.add))
                st.settle()
                st.post(dve.tensor_reduce(small[0:B, 16:32], K2v, AX.X, ALU.max))
                st.settle()
                st.post(dve.tensor_tensor(K2v, K2v, small[0:B, 16:32].unsqueeze(2).broadcast_to([B, H, 9]), ALU.subtract),
                        S("k_shift"))
                dve.wait_ge(S("k_exp"), 1)
                st.post(dve.tensor_reduce(small[0:B, 32:48], K2v, AX.X, ALU.add))
                st.settle()
                st.post(dve.reciprocal(small[0:B, 48:64], small[0:B, 32:48]))
                st.settle()
                st.post(dve.tensor_tensor(K2v, K2v, small[0:B, 48:64].unsqueeze(2).broadcast_to([B, H, 9]), ALU.mult),
                        S("k_ready"))
                for i in range(3):
                    bank = ring.take(dve)
                    ring.release(st, dve.tensor_copy(KB[:, i * 384:(i + 1) * 384], bank[:, 0:384]))
                st.settle()

            @block.gpsimd
            def _(pool):
                root_pool(pool, 1)

            @block.scalar
            def _(act):
                act.wait_ge(S("kp_ready"), 1)
                act.activation(KG, KP, ACT.Gelu).then_inc(S("gelu_done"), 1)
                act.wait_ge(S("k_shift"), 1)
                act.activation(K2, K2, ACT.Exp).then_inc(S("k_exp"), 1)

            @block.sync
            def _(sp):
                sp.wait_ge(S("k_ready"), 1)
                for i in range(B):
                    sp.dma_start(K1[:, i * 144:(i + 1) * 144], K2[i:i + 1, :]).then_inc(S("k_row"), 16)
                sp.wait_ge(S("k_row"), 16 * B)
        clear_block()

        with nc.Block() as block:
            @block.sync
            def _(sp):
                sp.dma_start(arena[:, 0:LAY0_N], lay0).then_inc(S("lay0_in"), 16)
                sp.wait_ge(S("lay0_in"), 16)
        clear_block()

        HTv = [big[:, i * MT * T:(i + 1) * MT * T].rearrange("p (m t) -> p m t", m=MT) for i in range(2)]
        lat = Z[:, :, 0:LAT]
        FS = Z
        GS = big[0:H, 0:T]
        onehot = small[:, 64:64 + 8].rearrange("p (t e) -> p t e", t=2)
        left = small[:, 72:80].rearrange("p (t e) -> p t e", t=2)
        rope = [big[:, i * 256:(i + 1) * 256].rearrange("p (t h d) -> p t h d", t=TT, h=H) for i in range(4)]
        raw = big[:, 1024:1536].rearrange("p (t n) -> p t n", t=2)
        with nc.Fori(0, B) as b:
            with nc.Block() as block:
                ring = Ring(PJ, pj_full, pj_free)

                @block.sync
                def _(sp):
                    sp.dma_start(Xin[:], x[bass.ds(b, 1)].rearrange("o p t d -> (o p) t d")).then_inc(S("x_in"), 16)
                    sp.dma_start(YT[:], xT[bass.ds(b, 1)].rearrange("o p k t -> (o p) k t")).then_inc(S("x_in"), 16)
                    sp.wait_ge(S("feat_ready"), 1)
                    for m in range(4):
                        sp.dma_start(feat[bass.ds(b, 1), m].rearrange("o q t -> (o q) t"),
                                     FS[64 * (m % 2):64 * (m % 2) + 64, m // 2, :]).then_inc(S("feat_out"), 16)
                    sp.dma_start(gate_d[bass.ds(b, 1)].rearrange("o h t -> (o h) t"), GS).then_inc(S("feat_out"), 16)
                    sp.wait_ge(S("feat_out"), 80)

                @block.tensor
                def _(pe):
                    pe.wait_ge(S("ysum"), 1)
                    bank = ring.claim(pe)
                    for m in range(2):
                        for k in range(KT):
                            ins = pe.matmul(bank[:, m:m + 1], k3(w0("wv"), 2)[:, k, m * P:(m + 1) * P], small[:, k:k + 1],
                                            start=k == 0, stop=k == 1)
                    ring.fill(ins)
                    ring.moved(pe)
                    bank = ring.claim(pe)
                    for k in range(KT):
                        ins = pe.matmul(bank[:, 0:D], Z[:, k, 0:P], k3(w0("wo"), 2)[:, k, :], start=k == 0, stop=k == 1)
                    ring.fill(ins)
                    pe.wait_ge(S("x_ready"), 2)
                    flip(pe, ring, X)
                    ring.moved(pe)
                    W = k3(w0("xqkv"), 2)
                    for i in range(3):
                        rows(pe, ring, XT[:, :, 1:T + 1], W, i * D, (i + 1) * D)
                    ring.moved(pe)
                    flip_heads(pe, ring, qpad)
                    flip_heads(pe, ring, kpad)
                    ring.moved(pe)
                    attention_pe(pe, "conv", 0)
                    pe.wait_ge(oa_free, 1)
                    flip(pe, ring, Y)
                    ring.moved(pe)
                    rows(pe, ring, YT, k3(w0("xproj"), 2), 0, D)
                    pe.wait_ge(S("xn_ready"), 2)
                    flip(pe, ring, X)
                    ring.moved(pe)
                    rows(pe, ring, XT[:, :, 1:T + 1], k3(w0("mq"), 2), 0, D)
                    rows(pe, ring, XT[:, :, 1:T + 1], k3(w0("mdkv"), 2), 0, LAT)
                    pe.wait_ge(S("lat_ready"), 2)
                    bank = ring.claim(pe)
                    for t in range(TT):
                        ins = pe.transpose(bank[:, t * P:(t + 1) * P], lat[:, t, :], ident)
                    ring.fill(ins)
                    ring.moved(pe)
                    for i in range(2):
                        bank = ring.claim(pe)
                        for t in range(TT):
                            ins = pe.matmul(bank[:, t * D:(t + 1) * D], YT[:, 0, t * P:(t + 1) * P],
                                            w0("mukv")[:, i * D:(i + 1) * D], start=True, stop=True)
                        ring.fill(ins)
                    pe.wait_ge(S("rope_done"), 4)
                    ring.moved(pe)
                    flip_heads(pe, ring, qpad)
                    flip_heads(pe, ring, kpad)
                    ring.moved(pe)
                    attention_pe(pe, "causal", 1)
                    pe.wait_ge(oa_free, 2)
                    flip(pe, ring, Y)
                    ring.moved(pe)
                    rows(pe, ring, YT, k3(w0("mo"), 2), 0, D)
                    pe.wait_ge(S("xn_ready"), 4)
                    flip(pe, ring, Z)
                    ring.moved(pe)
                    bank = ring.claim(pe)
                    for t in range(TT):
                        for k in range(KT):
                            ins = pe.matmul(bank[:, t * NE:(t + 1) * NE], YT[:, k, t * P:(t + 1) * P],
                                            k3(w0("gate"), 2)[:, k, :], start=k == 0, stop=k == 1)
                    ring.fill(ins)
                    W = k3(w0("W1"), 2)
                    W2 = k3(w0("W2"), NE * MT)

                    def up(e):
                        for j in range(MT // 2):
                            u = e * (MT // 2) + j
                            if u < 2:
                                pe.wait_ge(S("exp_done"), 4 * H)
                            else:
                                pe.wait_ge(S("relu_done"), 2 * (u - 1))
                            columns(pe, SM[u % 2], W, YT, e * HID + 2 * j * P).then_inc(sm_full[u % 2], 1)

                    def down(e):
                        pe.wait_ge(S("relu_done"), MT * (e + 1))
                        pe.wait_ge(pt_free[e % 2], H + e // 2)
                        for t in range(TT):
                            for m in range(MT):
                                ins = pe.matmul(PT[e % 2][:, t * D:(t + 1) * D], HTv[e % 2][:, m, t * P:(t + 1) * P],
                                                W2[:, e * MT + m, :], start=m == 0, stop=m == MT - 1)
                        ins.then_inc(pt_full[e % 2], 1)

                    for e in range(NE + 1):
                        if e < NE:
                            up(e)
                        if e:
                            down(e - 1)
                    pe.wait_ge(S("x_ready"), 6)
                    flip(pe, ring, X)
                    ring.moved(pe)
                    bank = ring.claim(pe)
                    for k in range(KT):
                        pe.matmul(bank[0:64, 0:T], k3(w0("w1w"), 2)[:, k, :], XT[:, k, 0:T], start=k == 0, stop=k == 1)
                    for k in range(KT):
                        pe.matmul(bank[64:128, 0:T], k3(w0("w2w"), 2)[:, k, :], XT[:, k, 1:T + 1], start=k == 0, stop=k == 1)
                    for k in range(KT):
                        ins = pe.matmul(bank[:, T:2 * T], k3(w0("rw"), 2)[:, k, :], XT[:, k, 1:T + 1], start=k == 0, stop=k == 1)
                    ring.fill(ins)
                    bank = ring.claim(pe)
                    for k in range(KT):
                        ins = pe.matmul(bank[0:H, 0:T], k3(w0("memg"), 2)[:, k, :], XT[:, k, 1:T + 1], start=k == 0, stop=k == 1)
                    ring.fill(ins)

                @block.vector
                def _(dve):
                    st = Steps(dve, S("dve"))
                    dve.wait_ge(S("x_in"), 32)
                    st.post(dve.tensor_reduce(small[:, 0:2], YT[:], AX.X, ALU.add), S("ysum"))
                    bank = ring.take(dve)
                    ring.release(st, dve.tensor_copy(Z[:, :, 0:P], bank[:, 0:2].unsqueeze(2).broadcast_to([P, 2, P])))
                    bank = ring.take(dve)
                    ring.release(st, dve.tensor_tensor(Y[:], bank[:, 0:D].unsqueeze(1).broadcast_to([P, TT, D]), Xin[:],
                                                       ALU.add))
                    st.settle()
                    layernorm(dve, st, X, Y, 1, "x_ready")
                    move(dve, st, ring, XT[:, :, 1:T + 1])
                    bank = ring.take(dve)
                    ring.release(st, dve.tensor_scalar(qpad[:].rearrange("p t h d -> p (t h) d")[:, :, 0:HD],
                                                       bank[:].rearrange("p (a d) -> p a d", d=HD), SCALE, None, ALU.mult))
                    bank = ring.take(dve)
                    ring.release(st, dve.tensor_copy(kpad[:].rearrange("p t h d -> p (t h) d")[:, :, 0:HD],
                                                     bank[:].rearrange("p (a d) -> p a d", d=HD)))
                    move(dve, st, ring, V[:])
                    move_heads(dve, st, ring, QT)
                    move_heads(dve, st, ring, KTr)
                    attention_dve(dve, st, "conv", 0)
                    move(dve, st, ring, YT[:])
                    bank = ring.take(dve)
                    ring.release(st, dve.tensor_tensor(Y[:], two(bank), X[:], ALU.add))
                    st.settle()
                    st.post(dve.tensor_tensor(Y[:], Y[:], w0("proj_b").unsqueeze(1).broadcast_to([P, TT, D]), ALU.add))
                    st.settle()
                    layernorm(dve, st, X2, Y, 2, "x_ready")
                    st.settle()
                    rmsnorm(dve, st, X, X2, w0("norm1"), 3, "xn_ready")
                    move(dve, st, ring, XT[:, :, 1:T + 1])

                    def rotate(src, dst, scale):
                        s4 = src.rearrange("p t (h d) -> p t h d", h=H)
                        for t in range(TT):
                            cs = w0("cos")[:, t * 8:(t + 1) * 8].unsqueeze(1).broadcast_to([P, H, 8])
                            sn = w0("sin")[:, t * 8:(t + 1) * 8].unsqueeze(1).broadcast_to([P, H, 8])
                            lo, hi = s4[:, t, :, 0:8], s4[:, t, :, 8:16]
                            st.post(dve.tensor_tensor(rope[0][:, t], lo, cs, ALU.mult))
                            st.post(dve.tensor_tensor(rope[1][:, t], hi, sn, ALU.mult))
                            st.post(dve.tensor_tensor(rope[2][:, t], lo, sn, ALU.mult))
                            st.post(dve.tensor_tensor(rope[3][:, t], hi, cs, ALU.mult))
                        st.settle()
                        for i, op in ((0, ALU.subtract), (1, ALU.add)):
                            a, bb = rope[2 * i][:], rope[2 * i + 1][:]
                            d = dst[:, :, :, 8 * i:8 * i + 8].rearrange("p t h d -> p (t h) d")
                            st.post(dve.tensor_tensor(d, a.rearrange("p t h d -> p (t h) d"),
                                                      bb.rearrange("p t h d -> p (t h) d"), op), S("rope_done"))
                        st.settle()

                    bank = ring.take(dve)
                    ring.release(st, dve.tensor_scalar(raw[:], two(bank), SCALE, None, ALU.mult))
                    st.settle()
                    rotate(raw, qpad, SCALE)
                    bank = ring.take(dve)
                    ring.release(st, dve.tensor_copy(lat, two(bank, LAT)))
                    st.settle()
                    layernorm(dve, st, lat, lat, 4, "lat_norm")
                    st.settle()
                    for t in range(TT):
                        st.post(dve.tensor_tensor(lat[:, t, :], lat[:, t, :], w0("ln_g"), ALU.mult))
                    st.settle()
                    for t in range(TT):
                        st.post(dve.tensor_tensor(lat[:, t, :], lat[:, t, :], w0("ln_b"), ALU.add), S("lat_ready"))
                    bank = ring.take(dve)
                    ring.release(st, dve.tensor_copy(YT[:, 0, :], bank[:, 0:T]))
                    bank = ring.take(dve)
                    ring.release(st, dve.tensor_copy(raw[:], two(bank)))
                    st.settle()
                    rotate(raw, kpad, 1.0)
                    move(dve, st, ring, V[:])
                    move_heads(dve, st, ring, QT)
                    move_heads(dve, st, ring, KTr)
                    attention_dve(dve, st, "causal", 1)
                    move(dve, st, ring, YT[:])
                    bank = ring.take(dve)
                    ring.release(st, dve.tensor_tensor(X[:], two(bank), X2[:], ALU.add))
                    st.settle()
                    rmsnorm(dve, st, Z, X, w0("norm2"), 5, "xn_ready")
                    st.post(dve.tensor_tensor(Y[:], X[:], X2[:], ALU.add))
                    move(dve, st, ring, YT[:])
                    lg = small[:, 80:88].rearrange("p (t e) -> p t e", t=2)
                    bank = ring.take(dve)
                    ring.release(st, dve.tensor_tensor(lg, two(bank, NE), w0("gate_b").unsqueeze(1).broadcast_to([P, TT, NE]),
                                                       ALU.add))
                    st.settle()
                    st.post(dve.tensor_reduce(small[:, 88:90], lg, AX.X, ALU.max))
                    st.settle()
                    st.post(dve.tensor_tensor(onehot, lg, small[:, 88:90].unsqueeze(2).broadcast_to([P, TT, NE]),
                                              ALU.is_equal))
                    st.settle()
                    st.post(dve.tensor_scalar(left[:, :, 1], onehot[:, :, 0], -1.0, 1.0, ALU.mult, ALU.add))
                    st.settle()
                    for e in range(1, NE):
                        st.post(dve.tensor_tensor(onehot[:, :, e], onehot[:, :, e], left[:, :, e], ALU.mult))
                        st.settle()
                        if e < NE - 1:
                            st.post(dve.tensor_tensor(left[:, :, e + 1], left[:, :, e], onehot[:, :, e], ALU.subtract))
                            st.settle()
                    for e in range(NE):
                        for t in range(TT):
                            st.post(dve.scalar_tensor_tensor(Y[:, t, :], w0("b2")[:, e * D:(e + 1) * D], onehot[:, t, e:e + 1],
                                                             Y[:, t, :], ALU.mult, ALU.add))
                        st.settle()
                    for e in range(NE):
                        dve.wait_ge(pt_full[e % 2], H + e // 2 + 1)
                        for t in range(TT):
                            ins = dve.scalar_tensor_tensor(Y[:, t, :], PT[e % 2][:, t * D:(t + 1) * D], onehot[:, t, e:e + 1],
                                                           Y[:, t, :], ALU.mult, ALU.add)
                            st.post(ins, pt_free[e % 2] if t else None)
                        st.settle()
                    layernorm(dve, st, X, Y, 6, "x_ready")
                    st.settle()
                    st.post(dve.tensor_copy(Xall[:, bass.ds(b, 1)].rearrange("p o t d -> p (o t) d"), X[:]))
                    move(dve, st, ring, XT[:, :, 1:T + 1])
                    bank = ring.take(dve)
                    ring.release(st, dve.tensor_copy(FS[:], two(bank)))
                    bank = ring.take(dve)
                    ring.release(st, dve.tensor_copy(GS, bank[0:H, 0:T]))
                    st.settle()
                    st.post(dve.memset(small[:, 0:1], 0.0), S("feat_ready"))

                @block.gpsimd
                def _(pool):
                    sp_ = Steps(pool, S("pool"))
                    kb4 = KB[:].rearrange("p (b n) -> p b n", b=B)
                    sp_.post(pool.tensor_copy(kcur[:].rearrange("p h a s -> p (h a s)"),
                                              kb4[:, bass.ds(b, 1), :].rearrange("p o n -> p (o n)")))
                    sp_.settle()
                    for src, dst, a in ((c("halo_up"), haloU, 2), (c("halo_dn"), haloD, 0)):
                        for h in range(H):
                            sp_.post(pool.tensor_tensor(dst[:, h], src.unsqueeze(1).broadcast_to([P, 3, 32]),
                                                        kcur[:, h, a, :].unsqueeze(2).broadcast_to([P, 3, 32]), ALU.mult))
                    sp_.settle()
                    root_pool(pool, 1)
                    sh = k3(c("shift"), 3)
                    for h in range(H):
                        if h >= 2:
                            pool.wait_ge(sm_full[h % 2], h // 2)
                        for a in range(3):
                            dst = band[h % 2] if a == 0 else btmp
                            sp_.post(pool.tensor_tensor(dst[:], sh[:, a, :].unsqueeze(1).broadcast_to([P, 3, P]),
                                                        kcur[:, h, a, :].unsqueeze(2).broadcast_to([P, 3, P]), ALU.mult))
                            sp_.settle()
                            if a:
                                sp_.post(pool.tensor_tensor(band[h % 2][:], band[h % 2][:], btmp[:], ALU.add),
                                         S("band_ready") if a == 2 else None)
                                sp_.settle()
                    for n in range(2, 7):
                        root_pool(pool, n)

                @block.scalar
                def _(act):
                    attention_act(act, "conv", 0)
                    attention_act(act, "causal", 1)
                    for e in range(NE):
                        if e >= 2:
                            act.wait_ge(pt_full[e % 2], H + e // 2)
                        for j in range(MT // 2):
                            u = e * (MT // 2) + j
                            act.wait_ge(sm_full[u % 2], H + u // 2 + 1)
                            for m in range(2):
                                col = e * MT + 2 * j + m
                                ins = act.activation(HTv[e % 2][:, 2 * j + m, :], SM[u % 2][:, m * T:(m + 1) * T], ACT.Relu,
                                                     bias=w0("b1")[:, col:col + 1])
                                ins.then_inc(S("relu_done"), 1)
            clear_block()

        with nc.Block() as block:
            @block.sync
            def _(sp):
                sp.dma_start(arena[:, 0:LAY1_N], lay1).then_inc(S("lay1_in"), 16)
                for i in range(B):
                    sp.dma_start(big[i * H:(i + 1) * H, :].rearrange("h (m n) -> h m n", m=4),
                                 feat[i].rearrange("m (h c) t -> h m (c t)", h=H)).then_inc(S("feat_in"), 16)
                sp.dma_start(Z[:, 0, :], gate_d.rearrange("b h t -> (b h) t")).then_inc(S("feat_in"), 16)
                sp.wait_ge(S("lay1_in"), 16)

            pl = big[:].rearrange("p (m c t) -> p m c t", m=4, c=4)
            free = arena[:, LAY1_N:LAY1_N + 7700]
            sq = free[:, 0:1536].rearrange("p (c t) -> p c t", c=6)
            outer = free[:, 1536:3072].rearrange("p (c t) -> p c t", c=6)
            rdM = free[:, 3072:4608].rearrange("p (c t) -> p c t", c=6)
            MM = free[:, 4608:4608 + 6 * 257].rearrange("p (c t) -> p c t", c=6)
            L = [free[:, a:a + 1536].rearrange("p (c t) -> p c t", c=6) for a in (6150, 4608)]
            n2 = PR[0][:, 0, :]
            nr = PR[0][:, 1, :]
            dt_ = PR[1][:, 0, :]
            wt = PR[1][:, 1, :]
            rdp = big[:, 0:1536].rearrange("p (c t) -> p c t", c=6)
            tmpb = outer[:, 0:3, :]

            def bc(ap, n):
                return ap.unsqueeze(1).broadcast_to([P, n, T])

            @block.vector
            def _(dve):
                st = Steps(dve, S("dve"))
                dve.wait_ge(S("feat_in"), 16 * (B + 1))
                for s in range(2):
                    p1, p2 = pl[:, 2 * s], pl[:, 2 * s + 1]
                    for lo, n, at in ((0, 3, 0), (1, 2, 3), (2, 1, 5)):
                        st.post(dve.tensor_tensor(L[s][:, at:at + n, :], bc(p1[:, lo, :], n), p2[:, lo + 1:lo + 1 + n, :], ALU.mult))
                        st.post(dve.tensor_tensor(tmpb[:, 0:n, :], p1[:, lo + 1:lo + 1 + n, :], bc(p2[:, lo, :], n), ALU.mult))
                        st.settle()
                        st.post(dve.tensor_tensor(L[s][:, at:at + n, :], L[s][:, at:at + n, :], tmpb[:, 0:n, :], ALU.subtract))
                        st.settle()
                for s in range(2):
                    st.post(dve.tensor_tensor(sq, L[s], L[s], ALU.mult))
                    st.settle()
                    st.post(dve.tensor_reduce(n2, sq.rearrange("p c t -> p t c"), AX.X, ALU.add), S("n2_ready"))
                    dve.wait_ge(S("root_ready"), s + 1)
                    st.post(dve.tensor_scalar(nr, nr, 1e-12, None, ALU.max))
                    st.settle()
                    st.post(dve.reciprocal(nr, nr))
                    st.settle()
                    if s == 0:
                        st.post(dve.tensor_tensor(L[0], L[0], bc(nr, 6), ALU.mult))
                    else:
                        for i in range(6):
                            st.post(dve.scalar_tensor_tensor(rdp[:, 5 - i, :], L[1][:, i, :], -1.0 if i in (1, 4) else 1.0, nr,
                                                             ALU.mult, ALU.mult))
                    st.settle()
                dve.wait_ge(S("sig_exp"), 3)
                sg = small[:, 0:8]
                st.post(dve.tensor_scalar(sg[:, 0:2], small[:, 8:10], 1.0, None, ALU.add))
                st.post(dve.tensor_scalar(Z[:, 0, :], Z[:, 0, :], 1.0, None, ALU.add))
                st.settle()
                st.post(dve.reciprocal(sg[:, 2:4], sg[:, 0:2]))
                st.post(dve.reciprocal(Z[:, 0, :], Z[:, 0, :]))
                st.settle()
                dec, mix = sg[:, 2:3], sg[:, 3:4]
                st.post(dve.tensor_scalar(sg[:, 4:5], dec, 1e-6, None, ALU.max))
                st.settle()
                st.post(dve.reciprocal(sg[:, 5:6], sg[:, 4:5]))
                st.post(dve.tensor_scalar(sg[:, 0:1], dec, 1e-6, None, ALU.is_ge))
                st.settle()
                st.post(dve.tensor_tensor(sg[:, 6:7], dec, sg[:, 5:6], ALU.mult))
                st.settle()
                st.post(dve.tensor_scalar(sg[:, 6:7], sg[:, 6:7], sg[:, 0:1], 1.0, ALU.max, ALU.min))
                st.post(dve.tensor_scalar(dt_, ones[:], dec, None, ALU.mult))
                st.post(dve.memset(MM[:, :, 0:1], 0.0))
                st.settle()
                st.post(dve.tensor_scalar(n2, ones[:], sg[:, 6:7], None, ALU.mult))
                st.post(dve.memset(nr, 0.0))
                st.settle()
                st.post(dve.tensor_tensor_scan(wt[:, 1:T], n2[:, 1:T], nr[:, 1:T], 1.0, ALU.mult, ALU.add))
                st.post(dve.memset(wt[:, 0:1], 1.0))
                st.settle()
                for i in range(6):
                    st.post(dve.tensor_tensor(n2, L[0][:, i, :], wt, ALU.mult))
                    st.settle()
                    st.post(dve.tensor_tensor(outer, L[0], bc(n2, 6), ALU.mult))
                    st.settle()
                    for j in range(6):
                        st.post(dve.tensor_tensor_scan(MM[:, j, 1:T + 1], dt_, outer[:, j, :], 0.0, ALU.mult, ALU.add))
                    st.settle()
                    if i == 0:
                        st.post(dve.tensor_tensor(rdM, MM[:, :, 0:T], bc(rdp[:, i, :], 6), ALU.mult))
                    else:
                        st.post(dve.tensor_tensor(sq, MM[:, :, 0:T], bc(rdp[:, i, :], 6), ALU.mult))
                        st.settle()
                        st.post(dve.tensor_tensor(rdM, rdM, sq, ALU.add))
                    st.settle()
                st.post(dve.tensor_scalar(rdM, rdM, dec, None, ALU.mult))
                st.settle()
                st.post(dve.tensor_tensor(sq, rdM, rdp, ALU.mult))
                st.post(dve.tensor_tensor(outer, rdM, rdM, ALU.mult))
                st.settle()
                st.post(dve.tensor_reduce(n2, sq.rearrange("p c t -> p t c"), AX.X, ALU.add))
                st.post(dve.tensor_reduce(nr, outer.rearrange("p c t -> p t c"), AX.X, ALU.add))
                st.post(dve.tensor_scalar(sg[:, 7:8], mix, -1.0, 1.0, ALU.mult, ALU.add))
                st.settle()
                st.post(dve.tensor_scalar(n2, n2, sg[:, 7:8], None, ALU.mult))
                st.settle()
                st.post(dve.scalar_tensor_tensor(n2, nr, mix, n2, ALU.mult, ALU.add))
                st.settle()
                st.post(dve.tensor_scalar(n2, n2, c("mscale"), None, ALU.mult), S("score_ready"))
                dve.wait_ge(S("score_exp"), 1)
                st.post(dve.tensor_scalar(n2, n2, 1.0, None, ALU.add))
                st.settle()
                st.post(dve.reciprocal(n2, n2))
                st.settle()
                st.post(dve.tensor_tensor(n2, n2, Z[:, 0, :], ALU.mult), S("gated_ready"))
                dve.wait_ge(pj_full[0], 1)
                st.post(dve.tensor_copy(Gt[:], PJ[0][:, 0:TT * B].rearrange("p (t b) -> p t b", t=TT)))
                dve.wait_ge(S("lay1_in"), 16)
                st.post(dve.tensor_scalar(w1("qkv_b")[:, 0:D], w1("qkv_b")[:, 0:D], SCALE, None, ALU.mult))
                st.post(dve.tensor_tensor(w1("r2b"), w1("r2b"), w1("eb"), ALU.add))
                st.settle()

            @block.gpsimd
            def _(pool):
                sp_ = Steps(pool, S("pool"))
                sp_.post(pool.memset(rinv[:, 0, 0:1], 0.5))
                sp_.settle()
                for s in range(2):
                    pool.wait_ge(S("n2_ready"), s + 1)
                    pool.tensor_tensor(nr, n2, rinv[:, 0, 0:1].broadcast_to([P, T]), ALU.pow).then_inc(S("root_ready"), 1)

            @block.scalar
            def _(act):
                act.wait_ge(S("feat_in"), 16 * (B + 1))
                act.activation(small[:, 8:9], c("decay"), ACT.Exp, scale=-1.0).then_inc(S("sig_exp"), 1)
                act.activation(small[:, 9:10], c("mix"), ACT.Exp, scale=-1.0).then_inc(S("sig_exp"), 1)
                act.activation(Z[:, 1, :], Z[:, 0, :], ACT.Identity, bias=c("memg_b")).then_inc(S("gate_biased"), 1)
                act.wait_ge(S("gate_biased"), 1)
                act.activation(Z[:, 0, :], Z[:, 1, :], ACT.Exp, scale=-1.0).then_inc(S("sig_exp"), 1)
                act.wait_ge(S("score_ready"), 1)
                act.activation(n2, n2, ACT.Exp, scale=-1.0).then_inc(S("score_exp"), 1)

            @block.tensor
            def _(pe):
                pe.wait_ge(S("gated_ready"), 1)
                for t in range(TT):
                    ins = pe.matmul(PJ[0][:, t * B:(t + 1) * B], n2[:, t * P:(t + 1) * P], c("bsel"), start=True, stop=True)
                ins.then_inc(pj_full[0], 1)
        clear_block()

        spare = arena[:, LAY1_N + 3584:LAY1_N + 7700]
        idx_i = spare[:, 0:128].bitcast(I32).rearrange("p (t n) -> p t n", t=TT)
        idx = small[:].rearrange("p (t n) -> p t n", t=TT)
        idxn = spare[:, 128:256].rearrange("p (t n) -> p t n", t=TT)
        iotab = spare[:, 256:384].bitcast(BF16)
        oneh = spare[:, 384:1408].bitcast(BF16).rearrange("p (j n) -> p j n", j=8)
        Cn = arena[:, LAY1_N:LAY1_N + 512].rearrange("p (t n) -> p t n", t=2)
        gcur = spare[:, 1408:1410]
        lg8 = spare[:, 1410:1442].rearrange("p (i e) -> p i e", i=4)
        mx4 = spare[:, 1442:1454].rearrange("p (i e) -> p i e", i=3)
        WT8 = spare[0:KE, 1454:1966].rearrange("p (a t) -> p a t", a=2)
        big2 = arena[:, LAY1_N:LAY1_N + 3584]
        XC = big[:, 0:512].rearrange("p (k t) -> p k t", k=2)
        QF = [big[:, 512 + i * 512:1024 + i * 512].rearrange("p (k t) -> p k t", k=2) for i in range(4)]
        HR = [big[:, 2560 + i * 512:3072 + i * 512].rearrange("p (k t) -> p k t", k=2) for i in range(2)]
        YW = [big2[:, 512 + i * 512:1024 + i * 512].rearrange("p (k t) -> p k t", k=2) for i in range(4)]
        PD = big2[:, 2560:3584].rearrange("p (k t) -> p k t", k=4)
        with nc.Fori(0, B) as b:
            with nc.Block() as block:
                ring = Ring(PJ, pj_full, pj_free)

                @block.sync
                def _(sp):
                    sp.dma_start(CT[:], ctxT[bass.ds(b, 1)].rearrange("o p k t -> (o p) k t")).then_inc(S("ctx_in"), 16)
                    sp.dma_start(idx_i, itok[bass.ds(b, 1)].rearrange("o p t n -> (o p) t n")).then_inc(S("idx_in"), 16)
                    sp.wait_ge(S("out_ready"), 2)
                    sp.dma_start(out[bass.ds(b, 1)].rearrange("o p t d -> (o p) t d"), OUT[:]).then_inc(S("out_done"), 16)
                    sp.wait_ge(S("out_done"), 16)

                @block.tensor
                def _(pe):
                    pe.wait_ge(S("x_ready"), 1)
                    flip(pe, ring, X)
                    ring.moved(pe)
                    XTc = XT[:, :, 1:T + 1]
                    W = k3(w1("qkv"), 2)
                    for i in range(3):
                        rows(pe, ring, XTc, W, i * D, (i + 1) * D)
                    ring.moved(pe)
                    flip_heads(pe, ring, qpad)
                    flip_heads(pe, ring, kpad)
                    ring.moved(pe)
                    attention_pe(pe, "causal", 0)
                    rows(pe, ring, XTc, k3(w1("memv"), 2), 0, D)
                    pe.wait_ge(S("y_ready"), 2)
                    flip(pe, ring, Y)
                    ring.moved(pe)
                    rows(pe, ring, YT, k3(w1("outw"), 2), 0, D)
                    for t in range(TT):
                        for j in range(NI):
                            if j % 8 == 0:
                                pe.wait_ge(S("hot_ready"), t * 8 + j // 8 + 1)
                            ins = pe.matmul(SC[:, t * T:(t + 1) * T], identb[:], oneh[:, j % 8, :], start=j == 0,
                                            stop=j == NI - 1)
                            if j % 8 == 7:
                                ins.then_inc(S("hot_used"), 1)
                    pe.wait_ge(S("x_ready"), 3)
                    flip(pe, ring, X2)
                    pe.wait_ge(S("ctx_in"), 16)
                    bank = ring.claim(pe)
                    for k in range(KT):
                        ins = pe.matmul(bank[:, 0:T], k3(w1("ydown"), 2)[:, k, :], CT[:, k, :], start=k == 0, stop=k == 1)
                    ring.fill(ins)
                    ring.moved(pe)
                    rows(pe, ring, XTc, k3(w1("yq"), 2), 0, D)
                    for i in range(2):
                        bank = ring.claim(pe)
                        for t in range(TT):
                            ins = pe.matmul(bank[:, t * D:(t + 1) * D], YT[:, 0, t * P:(t + 1) * P],
                                            w1("yup")[:, i * D:(i + 1) * D], start=True, stop=True)
                        ring.fill(ins)
                    ring.moved(pe)
                    flip_heads(pe, ring, qpad)
                    flip_heads(pe, ring, kpad)
                    ring.moved(pe)
                    pe.wait_ge(S("count_ready"), 2)
                    attention_pe(pe, "count", 1)
                    pe.wait_ge(oa_free, 2)
                    flip(pe, ring, Y)
                    ring.moved(pe)
                    rows(pe, ring, YT, k3(w1("yout"), 2), 0, D)
                    pe.wait_ge(S("x_ready"), 5)
                    flip(pe, ring, X)
                    ring.moved(pe)
                    pe.wait_ge(S("cum_ready"), 2)

                    def cols(w, act_):
                        bank = ring.claim(pe)
                        ring.fill(columns(pe, bank, k3(w, 2), act_))

                    cols(w1("fQ"), XTc)
                    cols(w1("fK"), XC)
                    ring.moved(pe)
                    cols(w1("finv"), QF[0])
                    cols(w1("finv"), QF[1])
                    ring.moved(pe)
                    for br in range(2):
                        pe.wait_ge(S("exp_done"), 4 * H)
                        columns(pe, SM[br], k3(w1("r1"), 2), QF[2 * br]).then_inc(sm_full[br], 1)
                    pe.wait_ge(S("router_act"), 4)
                    bank = ring.claim(pe)
                    for br in range(2):
                        for t in range(TT):
                            i = br * 2 + t
                            for k in range(KT):
                                ins = pe.matmul(bank[:, i * KE:(i + 1) * KE], HR[br][:, k, t * P:(t + 1) * P],
                                                k3(w1("r2"), 2)[:, k, :], start=k == 0, stop=k == 1)
                    ring.fill(ins)
                    pe.wait_ge(S("wts_ready"), 1)
                    bank = ring.claim(pe)
                    for i in range(4):
                        ins = pe.transpose(bank[0:KE, i * P:(i + 1) * P], lg8[:, i, :], ident)
                    ring.fill(ins)
                    ring.moved(pe)
                    for br in range(2):
                        for j in range(2):
                            u = br * 2 + j
                            if u < 2:
                                pe.wait_ge(S("router_act"), 2 * (u + 1))
                            else:
                                pe.wait_ge(S("yw_copied"), u - 1)
                            columns(pe, SM[u % 2], k3(w1(f"fW{br}"), 2), QF[2 * br + 1], 2 * j * P).then_inc(sm_full[u % 2], 1)
                            bank = ring.claim(pe)
                            ring.fill(columns(pe, bank, k3(w1(f"fV{br}"), 2), QF[2 * br], 2 * j * P))
                            bank = ring.claim(pe)
                            for m in range(2):
                                ins = pe.matmul(bank[:, m * T:(m + 1) * T], k3(w1("sel8"), 4)[0:KE, 2 * j + m, :], WT8[:, br, :],
                                                start=True, stop=True)
                            ring.fill(ins)
                        ring.moved(pe)
                        bank = ring.claim(pe)
                        for t in range(TT):
                            for m in range(4):
                                pe.matmul(bank[:, t * D:(t + 1) * D], PD[:, m, t * P:(t + 1) * P],
                                          k3(w1(f"fU{br}"), 4)[:, m, :], start=m == 0, stop=False)
                            ins = pe.matmul(bank[:, t * D:(t + 1) * D], WT8[:, br, t * P:(t + 1) * P],
                                            k3(w1("b8"), 2)[0:KE, br, :], start=False, stop=True)
                        ring.fill(ins)
                    pe.wait_ge(S("mixed"), 2)
                    flip(pe, ring, Y)
                    ring.moved(pe)
                    rows(pe, ring, YT, k3(w1("fO"), 2), 0, D)

                @block.vector
                def _(dve):
                    st = Steps(dve, S("dve"))
                    qd = qpad[:].rearrange("p t h d -> p (t h) d")[:, :, 0:HD]
                    kd = kpad[:].rearrange("p t h d -> p (t h) d")[:, :, 0:HD]
                    st.post(dve.tensor_copy(X[:], Xall[:, bass.ds(b, 1)].rearrange("p o t d -> p (o t) d")), S("x_ready"))
                    st.post(dve.tensor_copy(gcur, Gt[:, :, bass.ds(b, 1)].rearrange("p t o -> p (t o)")))
                    move(dve, st, ring, XT[:, :, 1:T + 1])
                    qb, kb, vb = [w1("qkv_b")[:, i * D:(i + 1) * D] for i in range(3)]
                    bank = ring.take(dve)
                    for t in range(TT):
                        ins = dve.scalar_tensor_tensor(qpad[:, t, :, 0:HD], bank[:, t * D:(t + 1) * D].rearrange("p (h d) -> p h d", d=HD),
                                                       SCALE, qb.rearrange("p (h d) -> p h d", d=HD), ALU.mult, ALU.add)
                        ring.release(st, ins) if t else st.post(ins)
                    bank = ring.take(dve)
                    for t in range(TT):
                        ins = dve.tensor_tensor(kpad[:, t, :, 0:HD], bank[:, t * D:(t + 1) * D].rearrange("p (h d) -> p h d", d=HD),
                                                kb.rearrange("p (h d) -> p h d", d=HD), ALU.add)
                        ring.release(st, ins) if t else st.post(ins)
                    bank = ring.take(dve)
                    ring.release(st, dve.tensor_tensor(V[:], two(bank), vb.unsqueeze(1).broadcast_to([P, TT, D]), ALU.add))
                    move_heads(dve, st, ring, QT)
                    move_heads(dve, st, ring, KTr)
                    attention_dve(dve, st, "causal", 0)
                    bank = ring.take(dve)
                    ring.release(st, dve.tensor_tensor(Z[:], two(bank), w1("memv_b").unsqueeze(1).broadcast_to([P, TT, D]),
                                                       ALU.add))
                    st.settle()
                    for t in range(TT):
                        st.post(dve.scalar_tensor_tensor(Y[:, t, :], Z[:, t, :], gcur[:, t:t + 1], Y[:, t, :],
                                                         ALU.mult, ALU.add), S("y_ready"))
                    move(dve, st, ring, YT[:])
                    bank = ring.take(dve)
                    ring.release(st, dve.tensor_tensor(Y[:], two(bank), X[:], ALU.add))
                    st.settle()
                    st.post(dve.tensor_tensor(Y[:], Y[:], w1("out_b").unsqueeze(1).broadcast_to([P, TT, D]), ALU.add))
                    st.settle()
                    layernorm(dve, st, X2, Y, 1, "x_ready")
                    dve.wait_ge(S("idx_in"), 16)
                    st.settle()
                    st.post(dve.tensor_copy(idx, idx_i))
                    st.post(dve.tensor_copy(iotab, c("iota")))
                    st.settle()
                    st.post(dve.tensor_scalar(idxn, idx, 0.0, float(T), ALU.is_lt, ALU.mult))
                    st.settle()
                    st.post(dve.tensor_tensor(idx, idx, idxn, ALU.add))
                    st.settle()
                    st.post(dve.tensor_scalar(idx, idx, 0.0, float(T - 1), ALU.max, ALU.min))
                    st.settle()
                    for t in range(TT):
                        for j8 in range(NI // 8):
                            if t or j8:
                                dve.wait_ge(S("hot_used"), t * 8 + j8)
                            for j in range(8):
                                ins = dve.tensor_scalar(oneh[:, j, :], iotab, idx[:, t, j8 * 8 + j:j8 * 8 + j + 1], None,
                                                        ALU.is_equal)
                                if j == 7:
                                    st.post(ins, S("hot_ready"))
                    dve.wait_ge(S("hot_used"), 16)
                    st.post(dve.tensor_copy(Cn, two(SC)), S("count_ready"))
                    st.settle()
                    st.post(dve.tensor_scalar(masks[:, 0], Cn, 0.0, NEG, ALU.is_equal, ALU.mult), S("count_ready"))
                    move(dve, st, ring, XT[:, :, 1:T + 1])
                    bank = ring.take(dve)
                    ring.release(st, dve.tensor_copy(YT[:, 0, :], bank[:, 0:T]))
                    bank = ring.take(dve)
                    ring.release(st, dve.tensor_scalar(qd, bank[:].rearrange("p (a d) -> p a d", d=HD), SCALE, None, ALU.mult))
                    bank = ring.take(dve)
                    ring.release(st, dve.tensor_copy(kd, bank[:].rearrange("p (a d) -> p a d", d=HD)))
                    move(dve, st, ring, V[:])
                    move_heads(dve, st, ring, QT)
                    move_heads(dve, st, ring, KTr)
                    attention_dve(dve, st, "count", 1, Cn)
                    move(dve, st, ring, YT[:])
                    bank = ring.take(dve)
                    ring.release(st, dve.tensor_tensor(Y[:], two(bank), X2[:], ALU.add))
                    st.settle()
                    layernorm(dve, st, X, Y, 2, "x_ready")
                    move(dve, st, ring, XT[:, :, 1:T + 1])
                    st.settle()
                    for k in range(KT):
                        st.post(dve.tensor_tensor_scan(XC[:, k, :], ones[:], XT[:, k, 1:T + 1], 0.0, ALU.mult, ALU.add),
                                S("cum_ready"))
                    move(dve, st, ring, QF[0])
                    move(dve, st, ring, QF[1])
                    move(dve, st, ring, QF[2])
                    move(dve, st, ring, QF[3])
                    bank = ring.take(dve)
                    ring.release(st, dve.tensor_tensor(lg8, bank[:, 0:4 * KE].rearrange("p (i e) -> p i e", i=4),
                                                       w1("r2b").unsqueeze(1).broadcast_to([P, 4, KE]), ALU.add))
                    st.settle()
                    st.post(dve.tensor_reduce(mx4[:, 0, :], lg8, AX.X, ALU.max))
                    st.settle()
                    st.post(dve.tensor_tensor(lg8, lg8, mx4[:, 0, :].unsqueeze(2).broadcast_to([P, 4, KE]), ALU.subtract),
                            S("lg_shift"))
                    dve.wait_ge(S("lg_exp"), 1)
                    st.post(dve.tensor_reduce(mx4[:, 1, :], lg8, AX.X, ALU.add))
                    st.settle()
                    st.post(dve.reciprocal(mx4[:, 2, :], mx4[:, 1, :]))
                    st.settle()
                    st.post(dve.tensor_tensor(lg8, lg8, mx4[:, 2, :].unsqueeze(2).broadcast_to([P, 4, KE]), ALU.mult),
                            S("wts_ready"))
                    bank = ring.take(dve)
                    ring.release(st, dve.tensor_copy(WT8.rearrange("e a t -> e (a t)"), bank[0:KE, :]))
                    st.settle()
                    for br in range(2):
                        for j in range(2):
                            u = br * 2 + j
                            dve.wait_ge(S("yw_copied"), u + 1)
                            bank = ring.take(dve)
                            ring.release(st, dve.tensor_tensor(PD[:, 2 * j:2 * j + 2, :], two(bank), YW[u], ALU.mult))
                            st.settle()
                            bank = ring.take(dve)
                            ring.release(st, dve.tensor_tensor(PD[:, 2 * j:2 * j + 2, :], two(bank), PD[:, 2 * j:2 * j + 2, :],
                                                               ALU.mult))
                        bank = ring.take(dve)
                        if br == 0:
                            ring.release(st, dve.tensor_copy(Y[:], two(bank)))
                            st.settle()
                        else:
                            for t in range(TT):
                                ins = dve.scalar_tensor_tensor(Y[:, t, :], bank[:, t * D:(t + 1) * D], w1("alpha"), Y[:, t, :],
                                                               ALU.mult, ALU.add)
                                ring.release(st, ins) if t else st.post(ins)
                            st.settle()
                            for t in range(TT):
                                st.post(dve.tensor_scalar(Y[:, t, :], Y[:, t, :], w1("rn")[:, t:t + 1], None, ALU.mult),
                                        S("mixed"))
                    move(dve, st, ring, YT[:])
                    bank = ring.take(dve)
                    ring.release(st, dve.tensor_tensor(Y[:], two(bank), X[:], ALU.add))
                    st.settle()
                    layernorm(dve, st, OUT, Y, 3, "out_ready")
                    st.settle()

                @block.gpsimd
                def _(pool):
                    for n in range(1, 4):
                        root_pool(pool, n)

                @block.scalar
                def _(act):
                    attention_act(act, "causal", 0)
                    attention_act(act, "count", 1)
                    for br in range(2):
                        act.wait_ge(sm_full[br], H + 1)
                        for m in range(2):
                            act.activation(HR[br][:, m, :], SM[br][:, m * T:(m + 1) * T], ACT.Gelu,
                                           bias=w1("r1b")[:, m:m + 1]).then_inc(S("router_act"), 1)
                    act.wait_ge(S("lg_shift"), 1)
                    act.activation(lg8, lg8, ACT.Exp).then_inc(S("lg_exp"), 1)
                    for u in range(4):
                        act.wait_ge(sm_full[u % 2], H + 2 + u // 2)
                        act.activation(YW[u], two(SM[u % 2]), ACT.Copy).then_inc(S("yw_copied"), 1)
            clear_block()


def kernel(**inputs):
    import numpy as np
    import concourse.bacc as bacc
    from concourse import mybir
    from concourse.bass_utils import run_bass_kernel_spmd as run

    a = {k: np.asarray(v) for k, v in inputs.items()}

    def chunks(w):
        k, n = w.shape
        return w.reshape(k // 128, 128, n).transpose(1, 0, 2).reshape(128, -1)

    def row(v, parts=128):
        return np.broadcast_to(np.reshape(v, (1, -1)), (128, v.size))

    def col(v):
        return v.reshape(-1, 128).T

    def first(w):
        z = np.zeros((128, w.shape[1]), w.dtype)
        z[:w.shape[0]] = w
        return z

    def tokens(v):
        return v.reshape(8, 2, 128, -1).transpose(0, 2, 1, 3)

    def feats(v):
        return v.transpose(0, 2, 1).reshape(8, 2, 128, 256).transpose(0, 2, 1, 3)

    f32 = np.float32
    p = "L0_xattn_"
    W = {"hist_W": chunks(a[p + "hist_W"]), "ctx_W1": chunks(a[p + "ctx_W1"]), "ctx_W2": a[p + "ctx_W2"],
         "ctx_b1": col(a[p + "ctx_b1"]), "kg_W1": chunks(a[p + "kg_W1"]), "kg_W2": chunks(a[p + "kg_W2"]),
         "hist_b": row(a[p + "hist_b"]), "hist_g": row(a[p + "hist_ln_g"]), "hist_lb": row(a[p + "hist_ln_b"]),
         "ctx_b2": row(a[p + "ctx_b2"]), "kg_b1": row(a[p + "kg_b1"]), "kg_g": row(a[p + "kg_ln_g"]),
         "kg_lb": row(a[p + "kg_ln_b"]), "kg_b2": row(a[p + "kg_b2"])}
    pos = np.arange(256, dtype=f32)[:, None]
    ang = pos * (1.0 / 10000.0 ** (np.arange(8, dtype=f32) / 8)).astype(f32)[None, :]
    q = "L0_ffn_"
    W.update({"wv": chunks(a["L0_attn_w_qkv"][512:].T), "wo": chunks(a["L0_attn_w_o"].T),
              "xqkv": chunks(np.concatenate([a[p + "Wq"], a[p + "Wk"], a[p + "Wv"]], axis=1)),
              "xproj": chunks(a[p + "proj_W"]), "proj_b": row(a[p + "proj_b"]),
              "mq": chunks(a[q + "Wq"].T), "mdkv": chunks(a[q + "Wdkv"].T),
              "mukv": np.concatenate([a[q + "Wuk"].T, a[q + "Wuv"].T], axis=1), "mo": chunks(a[q + "Wo"].T),
              "gate": chunks(a[q + "gate_w"].T), "W1": chunks(a[q + "W1"].reshape(4096, 256).T),
              "W2": chunks(a[q + "W2"].transpose(0, 2, 1).reshape(4096, 256)),
              "w1w": chunks(a["L1_attn_w1w"].T), "w2w": chunks(a["L1_attn_w2w"].T),
              "rw": chunks(np.concatenate([a["L1_attn_r1w"].T, a["L1_attn_r2w"].T], axis=1)),
              "memg": chunks(a["L1_attn_memg_w"].T), "norm1": row(a[q + "norm1_w"]), "norm2": row(a[q + "norm2_w"]),
              "ln_g": row(a[q + "ln_g"]), "ln_b": row(a[q + "ln_b"]), "gate_b": row(a[q + "gate_b"]),
              "b1": col(a[q + "b1"].reshape(-1)), "b2": row(a[q + "b2"]),
              "cos": chunks(np.cos(ang).astype(f32)), "sin": chunks(np.sin(ang).astype(f32))})
    r, s, t = "L1_attn_", "L1_xattn_", "L1_ffn_"

    def experts(w):
        return chunks(w.transpose(1, 0, 2).reshape(256, 512))

    def back(w):
        return chunks(w.transpose(0, 2, 1).reshape(512, 256))

    sel8 = np.zeros((128, 4, 128), f32)
    for m in range(4):
        for j in range(128):
            sel8[2 * m + j // 64, m, j] = 1.0
    W.update({"qkv": chunks(a[r + "qkv_w"].T), "memv": chunks(a[r + "memv_w"].T), "outw": chunks(a[r + "out_w"].T),
              "yq": chunks(a[s + "W_q"].T), "ydown": chunks(a[s + "W_kv_down"].T), "yup": a[s + "W_kv_up"].T,
              "yout": chunks(a[s + "W_out"].T), "fQ": chunks(a[t + "W_Q"].T), "fK": chunks(a[t + "W_K"].T),
              "fO": chunks(a[t + "W_O"].T), "finv": chunks(a[t + "W_inv"].T),
              "fV0": experts(a[t + "V_fwd"]), "fW0": experts(a[t + "W_fwd"]),
              "fV1": experts(a[t + "W_inv_exp"]), "fW1": experts(a[t + "V_inv"]),
              "fU0": back(a[t + "U_fwd"]), "fU1": back(a[t + "U_inv"]), "r1": chunks(a[t + "router_w1"].T),
              "r2": chunks(a[t + "router_w2"].T), "r1b": col(a[t + "router_b1"]), "r2b": row(a[t + "router_b2"]),
              "eb": row(a[t + "expert_bias"]), "alpha": row(a[t + "alpha_bi"]), "qkv_b": row(a[r + "qkv_b"]),
              "memv_b": row(a[r + "memv_b"]), "out_b": row(a[r + "out_b"]),
              "b8": first(np.concatenate([a[t + "b_fwd"], a[t + "b_inv"]], axis=1)), "sel8": sel8.reshape(128, 512),
              "rn": (1.0 / np.arange(1, 257, dtype=f32)).astype(f32).reshape(2, 128).T})
    shift = np.zeros((128, 3, 128), f32)
    for d in range(3):
        for i in range(128):
            if 0 <= i + d - 1 < 128:
                shift[i + d - 1, d, i] = 1.0
    up, dn = np.zeros((128, 32), f32), np.zeros((128, 32), f32)
    up[0, 31] = 1.0
    dn[127, 0] = 1.0
    bsel = np.zeros((128, 8), f32)
    for i in range(128):
        bsel[i, i // 16] = 1.0 / 16

    def heads(v):
        return np.tile(v.reshape(16, 1), (8, 1))

    mask = a["mask_SxS_bc0"]
    W.update({"ident": np.eye(128, dtype=f32), "causal": np.triu(np.ones((256, 256), f32), 1).reshape(2, 128, 256).transpose(1, 0, 2), "shift": shift.reshape(128, 384), "halo_up": up,
              "halo_dn": dn, "iota": np.broadcast_to(np.arange(256, dtype=f32), (128, 256)),
              "half": np.full((128, 1), -0.5, f32), "decay": heads(a[r + "decay_logits"]), "mscale": heads(a[r + "mem_scale"]),
              "memg_b": heads(a[r + "memg_b"]), "mix": row(a[r + "iter_mix"]), "bsel": bsel})

    def pack(table):
        return np.ascontiguousarray(np.concatenate([W[n].reshape(128, -1) for n, _ in table], axis=1))

    arrays = {"x": tokens(a["x"]), "xT": feats(a["x"]), "ctxT": feats(a["ctx_1024"]),
              "itok": tokens(a["itok_BxSx64_0_2047"]), "hist": pack(HIST), "lay0": pack(LAY0), "lay1": pack(LAY1),
              "const": pack(CONST), "mask": mask.reshape(2, 128, 256).transpose(1, 0, 2).astype(np.int32)}
    arrays = {k: np.ascontiguousarray(v) for k, v in arrays.items()}
    nc = bacc.Bacc("TRN2", target_bir_lowering=False, num_devices=1)
    ap = {k: nc.dram_tensor(k, v.shape, mybir.dt.from_np(v.dtype), kind="ExternalInput").ap() for k, v in arrays.items()}
    feat = nc.dram_tensor("feat", (B, 4, 64, T), F32, kind="Internal").ap()
    gate_d = nc.dram_tensor("gate_d", (B, H, T), F32, kind="Internal").ap()
    out = nc.dram_tensor("out", (8, 128, 2, 256), F32, kind="ExternalOutput").ap()
    decoder(nc, ap["x"], ap["xT"], ap["ctxT"], ap["itok"], ap["hist"], ap["lay0"], ap["lay1"], ap["const"], ap["mask"],
            feat, gate_d, out)
    got = run(nc, [arrays], core_ids=[0])
    return got.results[0]["out"].transpose(0, 2, 1, 3).reshape(8, 256, 256)
```

```python
from contextlib import ExitStack

import numpy as np

import concourse.bass as bass
from concourse import mybir

F32 = mybir.dt.float32
BF16 = mybir.dt.bfloat16
I32 = mybir.dt.int32
ALU = mybir.AluOpType
ACT = mybir.ActivationFunctionType
AX = mybir.AxisListType

P = 128
B, T, D = 8, 256, 256
TT = T // P
KT = D // P
H, HD = 16, 16
SCALE = 0.25
HC = 512
NE, HID = 4, 1024
MT = HID // P
LAT = 128
KE, R = 8, 64
NI = 64
NEG = -1.0e30
LN_EPS = 1e-5
PAIRS = [(0, 1), (0, 2), (0, 3), (1, 2), (1, 3), (2, 3)]

HIST = [("hist_W", KT * HC), ("ctx_W1", 4 * P), ("ctx_W2", 1), ("ctx_b1", 1), ("kg_W1", 4 * D), ("kg_W2", KT * 144),
        ("hist_b", HC), ("hist_g", HC), ("hist_lb", HC), ("ctx_b2", 1),
        ("kg_b1", D), ("kg_g", D), ("kg_lb", D), ("kg_b2", 144)]
LAY0 = [("wv", 512), ("wo", 512), ("xqkv", KT * 768), ("xproj", 512), ("mq", 512), ("mqs", 512), ("muks", D), ("mdkv", KT * LAT), ("mukv", 512),
        ("mo", 512), ("gate", KT * NE), ("W1", KT * NE * HID), ("W2", NE * MT * D), ("w1w", KT * 64), ("w2w", KT * 64),
        ("rw", KT * P), ("memg", KT * H), ("proj_b", D), ("norm1", D), ("norm2", D), ("ln_g", LAT), ("ln_b", LAT),
        ("gate_b", NE), ("b1", NE * MT), ("b2", NE * D), ("cos", T), ("sin", T)]
LAY1 = [("qkv", KT * 768), ("memv", 512), ("outw", 512), ("yq", 512), ("ydown", KT * LAT), ("yup", 512), ("yout", 512),
        ("fQ", 512), ("fK", 512), ("fO", 512), ("finv", 512), ("fV0", 1024), ("fW0", 1024), ("fV1", 1024), ("fW1", 1024),
        ("fU0", 1024), ("fU1", 1024), ("r1", 512), ("r2", KT * KE), ("r1b", KT), ("r2b", KE), ("eb", KE), ("alpha", 1),
        ("qkv_b", 768), ("memv_b", D), ("out_b", D), ("qkb", 2 * KT), ("b8", 2 * D), ("sel8", 4 * P), ("rn", TT)]
CONST = [("ident", P), ("causal", TT * T), ("shift", 3 * P), ("halo_up", 32), ("halo_dn", 32), ("iota", T),
         ("half", 1), ("decay", 1), ("mscale", 1), ("memg_b", 1), ("mix", 1), ("bsel", B), ("headq", 8), ("head1", 8),
         ("heads_on", KT * P), ("near0", P + 1), ("near1", P + 1)]


def offsets(table):
    at, out = 0, {}
    for name, n in table:
        out[name] = (at, n)
        at += n
    return out, at


HIST_AT, HIST_N = offsets(HIST)
LAY0_AT, LAY0_N = offsets(LAY0)
LAY1_AT, LAY1_N = offsets(LAY1)
CONST_AT, CONST_N = offsets(CONST)


class Steps:

    def __init__(self, eng, own):
        self.eng, self.own, self.count, self.open = eng, own, {}, {}

    def post(self, ins, sem=None):
        sem = self.own if sem is None else sem
        n = self.count.get(sem.name, 0) + 1
        self.count[sem.name] = n
        ins.then_inc(sem, 1)
        self.open[sem.name] = (sem, n)
        return ins

    def settle(self):
        for sem, n in self.open.values():
            self.eng.wait_ge(sem, n)
        self.open = {}


class Ring:

    def __init__(self, banks, full, free):
        self.banks, self.full, self.free, self.filled, self.taken = banks, full, free, 0, 0

    def claim(self, pe):
        i, n = self.filled % len(self.banks), self.filled // len(self.banks)
        if n:
            pe.wait_ge(self.free[i], n)
        return self.banks[i]

    def fill(self, ins):
        ins.then_inc(self.full[self.filled % len(self.banks)], 1)
        self.filled += 1

    def moved(self, pe):
        for i in range(len(self.banks)):
            n = (self.filled - i + len(self.banks) - 1) // len(self.banks)
            if n:
                pe.wait_ge(self.free[i], n)

    def take(self, eng):
        i = self.taken % len(self.banks)
        eng.wait_ge(self.full[i], self.taken // len(self.banks) + 1)
        return self.banks[i]

    def release(self, steps, ins):
        steps.post(ins, self.free[self.taken % len(self.banks)])
        self.taken += 1


def decoder(nc, x, xT, ctxT, itok, hist, lay0, lay1, const, negm, feat, gate_d, kern_d, flag_d, x4_d, out):
    with ExitStack() as ctx:
        names = {}

        def sb(name, shape, dt=F32):
            return ctx.enter_context(nc.sbuf_tensor(name, shape, dt))

        def S(name):
            if name not in names:
                names[name] = ctx.enter_context(nc.semaphore(name))
            return names[name]

        SC = ctx.enter_context(nc.psum_tensor("SC", [P, 512], F32))
        SM = [ctx.enter_context(nc.psum_tensor(f"SM{i}", [P, 512], F32)) for i in range(2)]
        PT = [ctx.enter_context(nc.psum_tensor(f"PT{i}", [P, 512], F32)) for i in range(2)]
        OA = ctx.enter_context(nc.psum_tensor("OA", [P, 512], F32))
        PJ = [ctx.enter_context(nc.psum_tensor(f"PJ{i}", [P, 512], F32)) for i in range(2)]
        oa_free = S("oa_free")
        lay0_in = ctx.enter_context(nc.semaphore("lay0_in"))
        pj_full, pj_free = [S(f"pj_full{i}") for i in range(2)], [S(f"pj_free{i}") for i in range(2)]

        arena = sb("arena", [P, max(LAY0_N, LAY1_N + 7700, HIST_N)])
        const_sb = sb("const_sb", [P, CONST_N])
        KB = sb("KB", [P, B * 144])
        kcols = sb("kcols", [P, KT, B * 9])

        HIST0 = arena.shape[1] - HIST_N

        def hist_w(name):
            a, n = HIST_AT[name]
            return arena[:, HIST0 + a:HIST0 + a + n]

        def w0(name):
            a, n = LAY0_AT[name]
            return arena[:, a:a + n]

        def w1(name):
            a, n = LAY1_AT[name]
            return arena[:, a:a + n]

        def c(name):
            a, n = CONST_AT[name]
            return const_sb[:, a:a + n]

        def k3(ap, k):
            return ap.rearrange("p (k n) -> p k n", k=k)

        ident = c("ident")

        identb = sb("identb", [P, P], BF16)
        notmask = sb("notmask", [P, TT, T])
        masks = sb("masks", [P, 2, TT, T], BF16)
        ones = sb("ones", [P, T])
        OUT = sb("OUT", [P, TT, D])
        Xin = sb("Xin", [P, TT, D])
        X = sb("X", [P, TT, D])
        X2 = sb("X2", [P, TT, D])
        Y = sb("Y", [P, TT, D])
        Z = sb("Z", [P, TT, D])
        XT = sb("XT", [P, KT, T + 1])
        YT = sb("YT", [P, KT, T])
        CT = sb("CT", [P, KT, T])
        VM = sb("VM", [P, TT, KT, 9 * P])
        QF = sb("QF", [P, KT, T + 2])
        KF = sb("KF", [P, KT, T + 2])
        mask_in = OUT[:].bitcast(I32)
        PR = [sb(f"PR{i}", [P, TT, T]) for i in range(2)]
        PS = [sb(f"PS{i}", [P, 2, T]) for i in range(2)]
        AM = [sb(f"AM{i}", [P, TT, T + 2]) for i in range(2)]
        band = [sb(f"band{i}", [P, 3, P]) for i in range(2)]
        btmp = sb("btmp", [P, 3, P])
        haloU = sb("haloU", [P, H, 3, 32])
        KC = haloU[:].rearrange("p h s c -> p (h s c)").rearrange("p (k a t) -> p k a t", k=KT, a=3)
        haloD = sb("haloD", [P, H, 3, 32])
        kcur = sb("kcur", [P, H, 3, 3])
        negmax = sb("negmax", [P, H, TT])
        rsum = sb("rsum", [P, TT, H])
        rinv = sb("rinv", [P, TT, H])
        small = sb("small", [P, 128])
        stats = sb("stats", [P, TT, 6])
        mv = sb("mv", [P, TT, 2])
        var = sb("var", [P, TT])
        rstd = sb("rstd", [P, TT])
        CC = sb("CC", [P, B, 4])
        big = sb("big", [P, H * (T + 2)])
        Gt = sb("Gt", [P, TT, B])
        QM = big[:].rearrange("p (h t) -> p h t", h=H)
        kcol = sb("kcol", [P, KT, 9])
        rT = sb("rT", [H, T])
        flag = sb("flag", [1, 1], I32)
        kfac = sb("kfac", [P, TT, 3, H])
        diag0 = sb("diag0", [P, TT, H])
        diag1 = sb("diag1", [P, TT, H])


        def flip(pe, ring, src, ready=None):
            bank = ring.claim(pe)
            for k in range(KT):
                for t in range(TT):
                    ins = pe.transpose(bank[:, k * T + t * P:k * T + (t + 1) * P], src[:, t, k * P:(k + 1) * P], ident)
            ring.fill(ins)

        def rows(pe, ring, actT, w, n0, n1):
            bank = ring.claim(pe)
            n = n1 - n0
            for t in range(TT):
                for k in range(KT):
                    ins = pe.matmul(bank[:, t * n:(t + 1) * n], actT[:, k, t * P:(t + 1) * P], w[:, k, n0:n1],
                                    start=k == 0, stop=k == KT - 1)
            ring.fill(ins)

        def columns(pe, bank, w, actT, m0=0, stop=True):
            for m in range(2):
                for k in range(KT):
                    ins = pe.matmul(bank[:, m * T:(m + 1) * T], w[:, k, m0 + m * P:m0 + (m + 1) * P], actT[:, k, :],
                                    start=k == 0, stop=k == KT - 1)
            return ins

        def two(bank, n=256):
            return bank[:, 0:2 * n].rearrange("p (a b) -> p a b", a=2)

        def move(dve, st, ring, dst):
            bank = ring.take(dve)
            ring.release(st, dve.tensor_copy(dst, two(bank)))

        def root_dve(dve, st, src, scale, eps, n):
            st.post(dve.tensor_scalar(var[:], src, scale, eps, ALU.mult, ALU.add), S("var_ready"))
            dve.wait_ge(S("rstd_ready"), n)

        def root_pool(pool, n):
            pool.wait_ge(S("var_ready"), n)
            pool.tensor_tensor(rstd[:], var[:], c("half").broadcast_to([P, TT]), ALU.pow).then_inc(S("rstd_ready"), 1)

        def layernorm(dve, st, dst, src, n, flag):
            for t in range(TT):
                st.post(dve.bn_stats(stats[:, t, :], src[:, t, :]))
            st.settle()
            for t in range(TT):
                st.post(dve.bn_aggr(mv[:, t, :], stats[:, t, :]))
            st.settle()
            root_dve(dve, st, mv[:, :, 1], 1.0, LN_EPS, n)
            for t in range(TT):
                st.post(dve.tensor_scalar(dst[:, t, :], src[:, t, :], mv[:, t, 0:1], rstd[:, t:t + 1],
                                          ALU.subtract, ALU.mult), S(flag))

        def rmsnorm(dve, st, dst, src, weight, n, flag):
            for t in range(TT):
                st.post(dve.scalar_tensor_tensor(dst[:, t, :], src[:, t, :], 1.0, src[:, t, :], ALU.mult, ALU.mult,
                                                 accum_out=small[:, 100 + t:101 + t]))
            st.settle()
            root_dve(dve, st, small[:, 100:102], 1.0 / D, 1e-6, n)
            st.settle()
            for t in range(TT):
                st.post(dve.scalar_tensor_tensor(dst[:, t, :], src[:, t, :], rstd[:, t:t + 1], weight,
                                                 ALU.mult, ALU.mult), S(flag))

        def vm_diag(t):
            return VM[:, t].rearrange("p k (h n) -> p k h n", h=8)[:, :, :, 0:HD]

        def move_v(dve, st, ring, bias=None):
            bank = ring.take(dve)
            for t in range(TT):
                src = bank[:, t * D:(t + 1) * D].rearrange("p (k h d) -> p k h d", k=KT, h=8)
                if bias is None:
                    ins = dve.tensor_copy(vm_diag(t), src)
                else:
                    ins = dve.tensor_tensor(vm_diag(t), src, bias.rearrange("p (k h d) -> p k h d", k=KT, h=8), ALU.add)
                ring.release(st, ins) if t == TT - 1 else st.post(ins)

        def mask_q_dve(dve, st, src):
            for h in range(8):
                st.post(dve.tensor_scalar(QM[:, h, 1:T + 1], src[:, 0, :], c("headq")[:, h:h + 1], None, ALU.mult),
                        S("qlow_ready"))

        def mask_q_pool(pool, ps, src):
            for h in range(8):
                ps.post(pool.tensor_scalar(QM[:, 8 + h, 1:T + 1], src[:, 1, :], c("headq")[:, h:h + 1], None, ALU.mult),
                        S("qhigh_ready"))

        SMs = [SM[0], SM[1], SC]

        def n_banks(mode):
            return 2 if mode == "conv" else 3

        def causal_like(mode):
            return mode in ("causal", "tally", "near")

        def q_ready(pe, h, inst):
            if h < 8:
                pe.wait_ge(S("qlow_ready"), 8 * inst + h + 1)
            else:
                pe.wait_ge(S("qhigh_ready"), 8 * inst + h - 7)

        def attention_pe(pe, mode, inst, KFd, between=None):
            base = inst * H
            half = causal_like(mode)
            NB = n_banks(mode)

            def bank_free(n):
                done = max(n - NB + 1, base)
                if done > 0:
                    pe.wait_ge(S("exp_done"), 2 * done)

            def scores(h):
                n = base + h
                k = h // 8
                if mode == "conv":
                    if h:
                        pe.wait_ge(S("masked"), h)
                    bank = SC
                else:
                    bank = SMs[n % NB]
                    bank_free(n)
                q_ready(pe, h, inst)
                if mode == "near":
                    if h == 0:
                        pe.wait_ge(S("kc_low"), 9)
                    if h == 8:
                        pe.wait_ge(S("kc_high"), 3)
                for t in range(TT):
                    o = t * T
                    cols = P if half and t == 0 else T
                    if mode == "near":
                        if t == 0:
                            pe.wait_ge(S("near_ready"), TT * (h + 1))
                        for a in range(3):
                            ins = pe.matmul(bank[:, o:o + cols], QM[:, h, t * P + a:t * P + a + P], KC[:, k, a, 0:cols],
                                            start=a == 0, stop=t == 1 and a == 2)
                            if a == 0 and t == 0:
                                pe.matmul(bank[:, 0:P], ident, near[h % 2][:, 0, 1:P + 1], start=False, stop=False)
                            elif a == 0:
                                pe.matmul(bank[:, o + P - 1:o + T], ident, near[h % 2][:, 1, :], start=False, stop=False,
                                          skip_group_check=True)
                                pe.matmul(bank[:, o + P:o + T], identb[:], masks[:, 1, 0, 0:P], start=False, stop=False,
                                          skip_group_check=True)
                    else:
                        ins = pe.matmul(bank[:, o:o + cols], QM[:, h, t * P + 1:t * P + 1 + P], KFd[:, k, 0:cols],
                                        start=True, stop=mode == "conv")
                    if half and t == 0:
                        pe.matmul(bank[:, 0:P], identb[:], masks[:, 1, 0, 0:P], start=False, stop=True)
                        ins = pe.matmul(bank[:, P:T], identb[:], masks[:, 1, 0, P:T], start=True, stop=True)
                    elif mode in ("causal", "tally"):
                        ins = pe.matmul(bank[:, o:o + T], identb[:], masks[:, 1, 1, :], start=False, stop=True)
                    elif mode == "count":
                        ins = pe.matmul(bank[:, o:o + T], identb[:], masks[:, 0, t, :], start=False, stop=True)
                ins.then_inc(S("raw_ready" if mode == "conv" else "scores_ready"), 1)

            def conv(h):
                n = base + h
                bank_free(n)
                pe.wait_ge(S("masked"), h + 1)
                pe.wait_ge(S("band_ready"), h + 1)
                a, bank, bd = AM[h % 2], SMs[n % NB], band[h % 2]
                for t in range(TT):
                    o = t * T
                    for s in range(3):
                        pe.matmul(bank[:, o:o + T], bd[:, s, :], a[:, t, s:s + T], start=s == 0, stop=False)
                    for s in range(3):
                        if t == 0:
                            pe.matmul(bank[96:128, o:o + T], haloU[0:1, h, s, :], a[0:1, 1, s:s + T],
                                      start=False, stop=False, skip_group_check=True)
                        else:
                            pe.matmul(bank[0:32, o:o + T], haloD[96:128, h, s, :], a[96:128, 0, s:s + T],
                                      start=False, stop=False, skip_group_check=True)
                    ins = pe.matmul(bank[:, o:o + T], identb[:], masks[:, 0, t, :], start=False, stop=True)
                ins.then_inc(S("scores_ready"), 1)

            def flip_probs(h):
                n = base + h
                if mode == "count":
                    pe.wait_ge(S("weighted"), 2 * (h + 1))
                else:
                    pe.wait_ge(S("exp_done"), 2 * (n + 1))
                if n >= 2:
                    pe.wait_ge(S("probs_moved"), n - 1)
                bank = PT[n % 2]
                for k in range(TT):
                    for t in range(k if half else 0, TT):
                        o = k * T + (0 if half and k else t) * P
                        ins = pe.transpose(bank[:, o:o + P], PR[n % 2][:, t, k * P:(k + 1) * P], ident)
                ins.then_inc(S("probs_flipped"), 1)

            def values(h):
                n = base + h
                g = h // 8
                pe.wait_ge(S("probs_moved"), n + 1)
                if h == 0 and inst:
                    pe.wait_ge(oa_free, inst)
                order = (1, 0) if half and h % 8 == 7 else (0, 1)
                for i, k in enumerate(order):
                    lo = P if half and k else 0
                    src = PS[n % 2][:, 1, 0:P] if lo else PS[n % 2][:, k, :]
                    ins = pe.matmul(OA[:, g * T + lo:(g + 1) * T], VM[:, k, g, (h % 8) * P:(h % 8 + 1) * P], src,
                                    start=h % 8 == 0 and i == 0, stop=h % 8 == 7 and i == 1, skip_group_check=lo > 0)
                ins.then_inc(S("values_done"), 1)

            for s in range(H + 3):
                if s < H:
                    scores(s)
                if mode == "conv" and 1 <= s <= H:
                    conv(s - 1)
                if 2 <= s < H + 2:
                    flip_probs(s - 2)
                if s >= 3:
                    values(s - 3)
                if between is not None:
                    between(s)

        def scale_pe(pe, ring, inst):
            pe.wait_ge(S("rinv_ready"), inst + 1)
            bank = ring.claim(pe)
            for t in range(TT):
                ins = pe.transpose(bank[0:H, t * P:(t + 1) * P], rinv[:, t, :], ident)
            ring.fill(ins)
            ring.moved(pe)
            bank = ring.claim(pe)
            for k in range(KT):
                ins = pe.matmul(bank[:, k * T:(k + 1) * T], k3(c("heads_on"), KT)[0:H, k, :], rT[:], start=True, stop=True)
            ring.fill(ins)

        def move_probs(eng, st, mode, n):
            eng.wait_ge(S("probs_flipped"), n + 1)
            if n >= 2:
                eng.wait_ge(S("values_done"), n - 1)
            if causal_like(mode):
                dst, src = PS[n % 2][:].rearrange("p k t -> p (k t)")[:, 0:3 * P], PT[n % 2][:, 0:3 * P]
            else:
                dst, src = PS[n % 2][:], two(PT[n % 2])
            ins = eng.tensor_copy(dst, src) if st is not None else eng.activation(dst, src, ACT.Copy)
            if st is not None:
                st.post(ins, S("probs_moved"))
            else:
                ins.then_inc(S("probs_moved"), 1)

        def attention_act(act, mode, inst):
            NB = n_banks(mode)
            half = causal_like(mode)
            for s in range(H + 2):
                if s < H:
                    h = s
                    n = inst * H + h
                    act.wait_ge(S("max_ready"), n + 1)
                    if n >= 2:
                        act.wait_ge(S("probs_flipped"), n - 1)
                    for t in range(TT):
                        cols = P if half and t == 0 else T
                        dst, src = PR[n % 2][:, t, 0:cols], SMs[n % NB][:, t * T:t * T + cols]
                        if mode == "count":
                            ins = act.activation(dst, src, ACT.Exp, bias=negmax[:, h, t:t + 1])
                        else:
                            ins = act.activation(dst, src, ACT.Exp, bias=negmax[:, h, t:t + 1], accum_out=rsum[:, t, h:h + 1])
                        ins.then_inc(S("exp_done"), 1)
                if s >= 2 and act_moves(mode):
                    move_probs(act, None, mode, inst * H + s - 2)

        def act_moves(mode):
            return mode in ("count", "near", "tally")

        def attention_dve(dve, st, mode, inst, counts=None, between=None):
            base = inst * H
            NB = n_banks(mode)

            def mask_scores(h):
                if h >= 2:
                    dve.wait_ge(S("scores_ready"), base + h - 1)
                dve.wait_ge(S("raw_ready"), h + 1)
                st.post(dve.tensor_tensor(AM[h % 2][:, :, 1:T + 1], two(SC), notmask[:], ALU.mult), S("masked"))

            def near_diagonals(h):
                if h >= 2:
                    dve.wait_ge(S("scores_ready"), base + h - 1)
                for t in range(TT):
                    st.post(dve.tensor_scalar(near[h % 2][:, t, :], c("near0"), diag1[:, t, h:h + 1], None, ALU.mult))
                st.settle()
                for t in range(TT):
                    st.post(dve.scalar_tensor_tensor(near[h % 2][:, t, :], c("near1"), diag0[:, t, h:h + 1],
                                                     near[h % 2][:, t, :], ALU.mult, ALU.add), S("near_ready"))

            def row_max(h):
                n = base + h
                dve.wait_ge(S("scores_ready"), n + 1)
                st.post(dve.tensor_reduce(negmax[:, h, :], two(SMs[n % NB]), AX.X, ALU.max, negate=True), S("max_ready"))

            def weight(h):
                n = base + h
                dve.wait_ge(S("exp_done"), 2 * (n + 1))
                for t in range(TT):
                    st.post(dve.scalar_tensor_tensor(PR[n % 2][:, t, :], PR[n % 2][:, t, :], 1.0, counts[:, t, :],
                                                     ALU.mult, ALU.mult, accum_out=rsum[:, t, h:h + 1]), S("weighted"))

            for s in range(H + 3):
                if mode == "conv" and s < H:
                    mask_scores(s)
                if mode == "near" and s < H:
                    near_diagonals(s)
                lag = 1 if mode in ("conv", "near") else 0
                if lag <= s < H + lag:
                    row_max(s - lag)
                if between is not None:
                    between(s)
                if mode == "count" and 1 <= s <= H:
                    weight(s - 1)
                if not act_moves(mode) and 2 <= s < H + 2:
                    move_probs(dve, st, mode, base + s - 2)
            dve.wait_ge(S("exp_done"), 2 * (base + H))
            st.settle()
            st.post(dve.reciprocal(rinv[:], rsum[:]), S("rinv_ready"))

        def scale_dve(dve, st, ring, inst, dst):
            bank = ring.take(dve)
            ring.release(st, dve.tensor_copy(rT[:], bank[0:H, 0:T]))
            bank = ring.take(dve)
            ring.release(st, dve.tensor_copy(dst, two(bank)))
            dve.wait_ge(S("values_done"), (inst + 1) * H)
            st.settle()
            st.post(dve.tensor_tensor(dst, two(OA), dst, ALU.mult), oa_free)

        def clear_block():
            with nc.Block() as block:
                @block.sync
                def _(sp):
                    for s in names.values():
                        sp.sem_clear(s)

        with nc.Block() as block:
            @block.sync
            def _(sp):
                sp.dma_start(const_sb[:], const).then_inc(S("const_in"), 16)
                sp.dma_start(mask_in, negm).then_inc(S("const_in"), 16)
                sp.dma_start(arena[:, HIST0:HIST0 + HIST_N], hist).then_inc(S("hist_in"), 16)
                sp.dma_start(arena[:, 0:HIST0], lay0[:, 0:HIST0]).then_inc(lay0_in, 16)
                sp.wait_ge(S("flag_ready"), 1)
                sp.dma_start(flag_d, flag[:]).then_inc(S("flag_out"), 16)
                sp.wait_ge(S("flag_out"), 16)

            @block.vector
            def _(dve):
                st = Steps(dve, S("dve"))
                st.post(dve.memset(VM[:], 0.0))
                st.post(dve.memset(ones[:], 1.0))
                st.post(dve.memset(XT[:], 0.0))
                st.post(dve.memset(QF[:], 0.0))
                st.post(dve.memset(KF[:], 0.0))
                for i in range(2):
                    st.post(dve.memset(AM[i][:], 0.0))
                dve.wait_ge(S("const_in"), 32)
                st.post(dve.tensor_copy(identb[:], ident))
                st.post(dve.tensor_scalar(masks[:, 0], mask_in, NEG, None, ALU.mult))
                st.post(dve.tensor_scalar(masks[:, 1], k3(c("causal"), TT), NEG, None, ALU.mult))
                st.post(dve.tensor_scalar(notmask[:], mask_in, -1.0, 1.0, ALU.mult, ALU.add))
                dve.wait_ge(S("hist_in"), 16)
                st.settle()
                st.post(dve.tensor_copy(X[:], mask_in))
                st.settle()
                st.post(dve.tensor_tensor(X[:], X[:], k3(c("causal"), TT), ALU.not_equal))
                st.settle()
                st.post(dve.tensor_reduce(small[:, 0:1], X[:], AX.XY, ALU.add), S("differ_rows"))
                dve.wait_ge(pj_full[0], 1)
                st.post(dve.tensor_copy(flag[:], PJ[0][0:1, 0:1]), S("flag_ready"))

            @block.tensor
            def _(pe):
                pe.wait_ge(S("differ_rows"), 1)
                pe.matmul(PJ[0][0:1, 0:1], small[:, 0:1], ones[:, 0:1], start=True, stop=True).then_inc(pj_full[0], 1)
        clear_block()

        EH = big[:, 0:1024].rearrange("p (t n) -> p t n", t=TT)
        EG = big[:, 1024:2048].rearrange("p (t n) -> p t n", t=TT)
        EHT = big[:, 2048:3072].rearrange("p (k t) -> p k t", k=4)
        A1 = big[:, 3072:3328]
        awr = big[0:1, 3328:3584]
        awc = small[:, 0:2]
        with nc.Fori(0, B) as b:
            with nc.Block() as block:
                ring = Ring(PJ, pj_full, pj_free)

                @block.sync
                def _(sp):
                    sp.dma_start(CT[:], ctxT[bass.ds(b, 1)].rearrange("o p k t -> (o p) k t")).then_inc(S("ctx_in"), 16)
                    sp.wait_ge(S("ctx_in"), 16)

                @block.tensor
                def _(pe):
                    pe.wait_ge(S("ctx_in"), 16)
                    W = k3(hist_w("hist_W"), KT)
                    for t in range(TT):
                        bank = ring.claim(pe)
                        for k in range(KT):
                            ins = pe.matmul(bank[:], CT[:, k, t * P:(t + 1) * P], W[:, k, :], start=k == 0, stop=k == 1)
                        ring.fill(ins)
                    pe.wait_ge(S("gelu_done"), TT)
                    for c2 in range(2):
                        bank = ring.claim(pe)
                        for cc in range(2):
                            for t in range(TT):
                                f = (2 * c2 + cc) * P
                                ins = pe.transpose(bank[:, cc * T + t * P:cc * T + (t + 1) * P], EG[:, t, f:f + P], ident)
                        ring.fill(ins)
                    ring.moved(pe)
                    for k in range(4):
                        ins = pe.matmul(SM[0][:, 0:T], k3(hist_w("ctx_W1"), 4)[:, k, :], EHT[:, k, :],
                                        start=k == 0, stop=k == 3)
                    ins.then_inc(S("a1_full"), 1)
                    pe.wait_ge(S("gelu_done"), TT + 1)
                    bank = ring.claim(pe)
                    ring.fill(pe.matmul(bank[0:1, 0:T], hist_w("ctx_W2"), A1, start=True, stop=True))
                    pe.wait_ge(S("aw_ready"), 1)
                    bank = ring.claim(pe)
                    for t in range(TT):
                        ins = pe.matmul(bank[:, t:t + 1], awr[:, t * P:(t + 1) * P], ones[0:1, 0:1], start=True, stop=True)
                    ring.fill(ins)
                    ring.moved(pe)
                    bank = ring.claim(pe)
                    for f in range(4):
                        for t in range(TT):
                            ins = pe.matmul(bank[:, f:f + 1], EG[:, t, f * P:(f + 1) * P], awc[:, t:t + 1],
                                            start=t == 0, stop=t == 1)
                    ring.fill(ins)

                @block.vector
                def _(dve):
                    st = Steps(dve, S("dve"))
                    for t in range(TT):
                        bank = ring.take(dve)
                        ring.release(st, dve.tensor_tensor(EH[:, t, :], bank[:], hist_w("hist_b"), ALU.add))
                    st.settle()
                    layernorm(dve, st, EH, EH, 1, "eh_norm")
                    st.settle()
                    for t in range(TT):
                        st.post(dve.tensor_tensor(EH[:, t, :], EH[:, t, :], hist_w("hist_g"), ALU.mult))
                    st.settle()
                    for t in range(TT):
                        st.post(dve.tensor_tensor(EH[:, t, :], EH[:, t, :], hist_w("hist_lb"), ALU.add), S("eh_ready"))
                    for c2 in range(2):
                        move(dve, st, ring, EHT[:, 2 * c2:2 * c2 + 2, :])
                    bank = ring.take(dve)
                    ring.release(st, dve.tensor_scalar(awr, bank[0:1, 0:T], hist_w("ctx_b2")[0:1, :], None, ALU.add))
                    st.settle()
                    st.post(dve.tensor_reduce(small[0:1, 8:9], awr, AX.X, ALU.max, negate=True), S("awmax"))
                    dve.wait_ge(S("awexp"), 1)
                    st.post(dve.reciprocal(small[0:1, 10:11], small[0:1, 9:10]))
                    st.settle()
                    st.post(dve.tensor_scalar(awr, awr, small[0:1, 10:11], None, ALU.mult), S("aw_ready"))
                    bank = ring.take(dve)
                    ring.release(st, dve.tensor_copy(awc, bank[:, 0:2]))
                    bank = ring.take(dve)
                    ring.release(st, dve.tensor_copy(CC[:, bass.ds(b, 1), :].rearrange("p o f -> p (o f)"), bank[:, 0:4]))
                    st.settle()

                @block.gpsimd
                def _(pool):
                    root_pool(pool, 1)

                @block.scalar
                def _(act):
                    for t in range(TT):
                        act.wait_ge(S("eh_ready"), t + 1)
                        act.activation(EG[:, t, :], EH[:, t, :], ACT.Gelu).then_inc(S("gelu_done"), 1)
                    act.wait_ge(S("a1_full"), 1)
                    act.activation(A1, SM[0][:, 0:T], ACT.Gelu, bias=hist_w("ctx_b1")).then_inc(S("gelu_done"), 1)
                    act.wait_ge(S("awmax"), 1)
                    act.activation(awr, awr, ACT.Exp, bias=small[0:1, 8:9],
                                   accum_out=small[0:1, 9:10]).then_inc(S("awexp"), 1)
            clear_block()

        KP = big[0:B, 0:256]
        KG = big[0:B, 256:512]
        KPT = big[:, 512:528].rearrange("p (k b) -> p k b", k=2)
        K2 = big[0:B, 528:672]
        K2v = K2.rearrange("b (h n) -> b h n", n=9)
        KH = big[0:H, 700:772].rearrange("h (b n) -> h b n", b=B)
        with nc.Block() as block:
            ring = Ring(PJ, pj_full, pj_free)

            @block.tensor
            def _(pe):
                bank = ring.claim(pe)
                for f in range(4):
                    ins = pe.matmul(bank[0:B, 0:256], CC[:, :, f], k3(hist_w("kg_W1"), 4)[:, f, :], start=f == 0, stop=f == 3)
                ring.fill(ins)
                pe.wait_ge(S("gelu_done"), 1)
                bank = ring.claim(pe)
                for k in range(2):
                    ins = pe.transpose(bank[:, k * B:(k + 1) * B], KG[:, k * P:(k + 1) * P], ident[0:B, 0:B])
                ring.fill(ins)
                ring.moved(pe)
                bank = ring.claim(pe)
                for k in range(2):
                    ins = pe.matmul(bank[0:B, 0:144], KPT[:, k, :], k3(hist_w("kg_W2"), 2)[:, k, :], start=k == 0, stop=k == 1)
                ring.fill(ins)
                pe.wait_ge(S("k_in"), 32)
                bank = ring.claim(pe)
                for k in range(KT):
                    ins = pe.matmul(bank[:, k * 72:(k + 1) * 72], k3(c("heads_on"), KT)[0:H, k, :],
                                    KH.rearrange("h b n -> h (b n)"), start=True, stop=True)
                ring.fill(ins)

            @block.vector
            def _(dve):
                st = Steps(dve, S("dve"))
                bank = ring.take(dve)
                ring.release(st, dve.tensor_tensor(KP, bank[0:B, 0:256], hist_w("kg_b1")[0:B, :], ALU.add))
                st.post(dve.memset(var[:], 1.0))
                st.settle()
                st.post(dve.bn_stats(stats[0:B, 0, :], KP))
                st.settle()
                st.post(dve.bn_aggr(mv[0:B, 0, :], stats[0:B, 0, :]))
                st.settle()
                st.post(dve.tensor_scalar(var[0:B, 0:1], mv[0:B, 0, 1:2], LN_EPS, None, ALU.add), S("var_ready"))
                dve.wait_ge(S("rstd_ready"), 1)
                st.post(dve.tensor_scalar(KP, KP, mv[0:B, 0, 0:1], rstd[0:B, 0:1], ALU.subtract, ALU.mult))
                st.settle()
                st.post(dve.tensor_tensor(KP, KP, hist_w("kg_g")[0:B, :], ALU.mult))
                st.settle()
                st.post(dve.tensor_tensor(KP, KP, hist_w("kg_lb")[0:B, :], ALU.add), S("kp_ready"))
                bank = ring.take(dve)
                ring.release(st, dve.tensor_copy(KPT, bank[:, 0:2 * B].rearrange("p (k b) -> p k b", k=2)))
                bank = ring.take(dve)
                ring.release(st, dve.tensor_tensor(K2, bank[0:B, 0:144], hist_w("kg_b2")[0:B, :], ALU.add))
                st.settle()
                st.post(dve.tensor_reduce(small[0:B, 16:32], K2v, AX.X, ALU.max))
                st.settle()
                st.post(dve.tensor_tensor(K2v, K2v, small[0:B, 16:32].unsqueeze(2).broadcast_to([B, H, 9]), ALU.subtract),
                        S("k_shift"))
                dve.wait_ge(S("k_exp"), 1)
                st.post(dve.tensor_reduce(small[0:B, 32:48], K2v, AX.X, ALU.add))
                st.settle()
                st.post(dve.reciprocal(small[0:B, 48:64], small[0:B, 32:48]))
                st.settle()
                st.post(dve.tensor_tensor(K2v, K2v, small[0:B, 48:64].unsqueeze(2).broadcast_to([B, H, 9]), ALU.mult),
                        S("k_ready"))
                bank = ring.take(dve)
                ring.release(st, dve.tensor_copy(kcols[:], bank[:, 0:144].rearrange("p (k n) -> p k n", k=KT)))
                st.settle()

            @block.gpsimd
            def _(pool):
                root_pool(pool, 1)

            @block.scalar
            def _(act):
                act.wait_ge(S("kp_ready"), 1)
                act.activation(KG, KP, ACT.Gelu).then_inc(S("gelu_done"), 1)
                act.wait_ge(S("k_shift"), 1)
                act.activation(K2, K2, ACT.Exp).then_inc(S("k_exp"), 1)

            @block.sync
            def _(sp):
                sp.wait_ge(S("k_ready"), 1)
                sp.dma_start(kern_d, K2).then_inc(S("k_out"), 16)
                sp.wait_ge(S("k_out"), 16)
                sp.dma_start(KB[:], kern_d.rearrange("b n -> (b n)").unsqueeze(0).broadcast_to([P, B * 144])).then_inc(S("k_in"), 16)
                sp.dma_start(KH, kern_d.rearrange("b (h n) -> h b n", n=9)).then_inc(S("k_in"), 16)
                sp.wait_ge(S("k_in"), 32)
        clear_block()

        with nc.Block() as block:
            @block.sync
            def _(sp):
                sp.dma_start(arena[:, HIST0:LAY0_N], lay0[:, HIST0:LAY0_N]).then_inc(lay0_in, 16)
                sp.wait_ge(lay0_in, 32)
        clear_block()

        HTv = [big[:, i * MT * T:(i + 1) * MT * T].rearrange("p (m t) -> p m t", m=MT) for i in range(2)]
        lat = Z[:, :, 0:LAT]
        FS = Z
        GS = big[0:H, 0:T]
        onehot = small[:, 64:64 + 8].rearrange("p (t e) -> p t e", t=2)
        left = small[:, 72:80].rearrange("p (t e) -> p t e", t=2)
        NP = [AM[0][:, :, 0:T], AM[1][:, :, 0:T], PS[0][:]]
        near = [band[i][:].rearrange("p a b -> p (a b)")[:, 0:2 * (P + 1)].rearrange("p (t m) -> p t m", t=TT) for i in range(2)]
        def layer0(mode):
            with nc.Fori(0, B) as b:
                with nc.Block() as block:
                    ring = Ring(PJ, pj_full, pj_free)

                    @block.sync
                    def _(sp):
                        sp.dma_start(Xin[:], x[bass.ds(b, 1)].rearrange("o p t d -> (o p) t d")).then_inc(S("x_in"), 16)
                        sp.dma_start(YT[:], xT[bass.ds(b, 1)].rearrange("o p k t -> (o p) k t")).then_inc(S("x_in"), 16)
                        sp.wait_ge(S("x_ready"), 6)
                        sp.dma_start(x4_d[bass.ds(b, 1)].rearrange("o p t d -> (o p) t d"), X[:]).then_inc(S("feat_out"), 16)
                        sp.wait_ge(S("feat_ready"), 1)
                        for m in range(4):
                            sp.dma_start(feat[bass.ds(b, 1), m].rearrange("o q t -> (o q) t"),
                                         FS[64 * (m % 2):64 * (m % 2) + 64, m // 2, :]).then_inc(S("feat_out"), 16)
                        sp.dma_start(gate_d[bass.ds(b, 1)].rearrange("o h t -> (o h) t"), GS).then_inc(S("feat_out"), 16)
                        sp.wait_ge(S("feat_out"), 96)

                    @block.tensor
                    def _(pe):
                        pe.wait_ge(S("ysum"), 1)
                        bank = ring.claim(pe)
                        for m in range(2):
                            for k in range(KT):
                                ins = pe.matmul(bank[:, m:m + 1], k3(w0("wv"), 2)[:, k, m * P:(m + 1) * P], small[:, k:k + 1],
                                                start=k == 0, stop=k == 1)
                        ring.fill(ins)
                        ring.moved(pe)
                        bank = ring.claim(pe)
                        for k in range(KT):
                            ins = pe.matmul(bank[:, 0:D], Z[:, k, 0:P], k3(w0("wo"), 2)[:, k, :], start=k == 0, stop=k == 1)
                        ring.fill(ins)
                        pe.wait_ge(S("x_ready"), 2)
                        flip(pe, ring, X)
                        ring.moved(pe)
                        W = k3(w0("xqkv"), 2)
                        for i in range(2):
                            bank = ring.claim(pe)
                            ring.fill(columns(pe, bank, W, XT[:, :, 1:T + 1], i * D))
                        rows(pe, ring, XT[:, :, 1:T + 1], W, 2 * D, 3 * D)
                        if mode == "near":
                            pe.wait_ge(S("products"), 3)
                            bank = ring.claim(pe)
                            for t in range(TT):
                                for j in range(3):
                                    for k in range(KT):
                                        o = (t * 3 + j) * H + k * 8
                                        ins = pe.matmul(bank[:, o:o + 8], NP[j][:, k, t * P:(t + 1) * P], c("head1"),
                                                        start=True, stop=True)
                            ring.fill(ins)
                        ring.moved(pe)
                        attention_pe(pe, mode, 0, KF[:, :, 1:T + 1])
                        scale_pe(pe, ring, 0)
                        pe.wait_ge(oa_free, 1)
                        rows(pe, ring, YT, k3(w0("xproj"), 2), 0, D)
                        pe.wait_ge(S("xn_ready"), 2)
                        flip(pe, ring, X)
                        ring.moved(pe)
                        rows(pe, ring, XT[:, :, 1:T + 1], k3(w0("mdkv"), 2), 0, LAT)
                        for w in ("mq", "mqs"):
                            bank = ring.claim(pe)
                            ring.fill(columns(pe, bank, k3(w0(w), 2), XT[:, :, 1:T + 1]))
                        pe.wait_ge(S("lat_ready"), 2)
                        bank = ring.claim(pe)
                        for t in range(TT):
                            ins = pe.transpose(bank[:, t * P:(t + 1) * P], lat[:, t, :], ident)
                        ring.fill(ins)
                        ring.moved(pe)
                        for w in (w0("mukv")[:, 0:D], w0("muks")):
                            bank = ring.claim(pe)
                            for m in range(2):
                                ins = pe.matmul(bank[:, m * T:(m + 1) * T], w[:, m * P:(m + 1) * P], YT[:, 0, :],
                                                start=True, stop=True)
                            ring.fill(ins)
                        bank = ring.claim(pe)
                        for t in range(TT):
                            ins = pe.matmul(bank[:, t * D:(t + 1) * D], YT[:, 0, t * P:(t + 1) * P],
                                            w0("mukv")[:, D:2 * D], start=True, stop=True)
                        ring.fill(ins)
                        pe.wait_ge(S("k_rotated"), 1)
                        ring.moved(pe)
                        attention_pe(pe, "causal", 1, KF[:, :, 1:T + 1])
                        scale_pe(pe, ring, 1)
                        pe.wait_ge(oa_free, 2)
                        rows(pe, ring, YT, k3(w0("mo"), 2), 0, D)
                        pe.wait_ge(S("xn_ready"), 4)
                        flip(pe, ring, Z)
                        ring.moved(pe)
                        bank = ring.claim(pe)
                        for t in range(TT):
                            for k in range(KT):
                                ins = pe.matmul(bank[:, t * NE:(t + 1) * NE], YT[:, k, t * P:(t + 1) * P],
                                                k3(w0("gate"), 2)[:, k, :], start=k == 0, stop=k == 1)
                        ring.fill(ins)
                        W = k3(w0("W1"), 2)
                        W2 = k3(w0("W2"), NE * MT)

                        def up(e):
                            for j in range(MT // 2):
                                u = e * (MT // 2) + j
                                if u < 3:
                                    pe.wait_ge(S("exp_done"), 4 * H)
                                else:
                                    pe.wait_ge(S("relu_done"), 2 * (u - 2))
                                columns(pe, SMs[u % 3], W, YT, e * HID + 2 * j * P).then_inc(S("up_done"), 1)

                        def down(e):
                            pe.wait_ge(S("relu_done"), MT * (e + 1))
                            if e < 2:
                                pe.wait_ge(S("probs_moved"), 2 * H)
                            else:
                                pe.wait_ge(S("y_used"), e - 1)
                            for t in range(TT):
                                for m in range(MT):
                                    ins = pe.matmul(PT[e % 2][:, t * D:(t + 1) * D], HTv[e % 2][:, m, t * P:(t + 1) * P],
                                                    W2[:, e * MT + m, :], start=m == 0, stop=m == MT - 1)
                            ins.then_inc(S("down_done"), 1)

                        for e in range(NE + 1):
                            if e < NE:
                                up(e)
                            if e:
                                down(e - 1)
                        pe.wait_ge(S("x_ready"), 6)
                        flip(pe, ring, X)
                        ring.moved(pe)
                        bank = ring.claim(pe)
                        for k in range(KT):
                            pe.matmul(bank[0:64, 0:T], k3(w0("w1w"), 2)[:, k, :], XT[:, k, 0:T], start=k == 0, stop=k == 1)
                        for k in range(KT):
                            pe.matmul(bank[64:128, 0:T], k3(w0("w2w"), 2)[:, k, :], XT[:, k, 1:T + 1], start=k == 0, stop=k == 1)
                        for k in range(KT):
                            ins = pe.matmul(bank[:, T:2 * T], k3(w0("rw"), 2)[:, k, :], XT[:, k, 1:T + 1], start=k == 0, stop=k == 1)
                        ring.fill(ins)
                        bank = ring.claim(pe)
                        for k in range(KT):
                            ins = pe.matmul(bank[0:H, 0:T], k3(w0("memg"), 2)[:, k, :], XT[:, k, 1:T + 1], start=k == 0, stop=k == 1)
                        ring.fill(ins)

                    @block.vector
                    def _(dve):
                        st = Steps(dve, S("dve"))
                        dve.wait_ge(S("x_in"), 32)
                        st.post(dve.tensor_reduce(small[:, 0:2], YT[:], AX.X, ALU.add), S("ysum"))
                        bank = ring.take(dve)
                        ring.release(st, dve.tensor_copy(Z[:, :, 0:P], bank[:, 0:2].unsqueeze(2).broadcast_to([P, 2, P])))
                        bank = ring.take(dve)
                        ring.release(st, dve.tensor_tensor(Y[:], bank[:, 0:D].unsqueeze(1).broadcast_to([P, TT, D]), Xin[:],
                                                           ALU.add))
                        st.settle()
                        layernorm(dve, st, X, Y, 1, "x_ready")
                        move(dve, st, ring, XT[:, :, 1:T + 1])
                        for dst in (QF, KF):
                            bank = ring.take(dve)
                            ring.release(st, dve.tensor_copy(dst[:, :, 1:T + 1], two(bank)))
                        st.settle()
                        st.post(dve.memset(small[:, 2:3], 0.0), S("qk_ready"))
                        mask_q_dve(dve, st, QF[:, :, 1:T + 1])
                        if mode == "near":
                            dve.wait_ge(S("kcol_ready"), 2)
                            for a in range(3):
                                st.post(dve.tensor_scalar(KC[:, 0, a, :], KF[:, 0, 0:T], kcol[:, 0, 3 * a:3 * a + 1], None,
                                                          ALU.mult), S("kc_low"))
                            st.settle()
                            for j in range(1, 3):
                                for a in range(3):
                                    st.post(dve.scalar_tensor_tensor(KC[:, 0, a, :], KF[:, 0, j:j + T],
                                                                     kcol[:, 0, 3 * a + j:3 * a + j + 1], KC[:, 0, a, :],
                                                                     ALU.mult, ALU.add), S("kc_low"))
                                st.settle()
                        move_v(dve, st, ring)
                        if mode == "near":
                            bank = ring.take(dve)
                            ring.release(st, dve.tensor_copy(kfac[:], bank[:, 0:TT * 3 * H].rearrange("p (t j h) -> p t j h", t=TT, j=3)))
                            st.settle()

                            def kf(a, j):
                                return kcur[:, :, a, j].unsqueeze(1).broadcast_to([P, TT, H])

                            st.post(dve.tensor_tensor(diag1[:], kfac[:, :, 0, :], kf(0, 2), ALU.mult))
                            st.post(dve.tensor_tensor(diag0[:], kfac[:, :, 0, :], kf(0, 1), ALU.mult))
                            st.post(dve.tensor_tensor(kfac[:, :, 1, :], kfac[:, :, 1, :], kf(0, 2), ALU.mult))
                            st.post(dve.tensor_tensor(kfac[:, :, 2, :], kfac[:, :, 2, :], kf(1, 2), ALU.mult))
                            st.settle()
                            st.post(dve.tensor_tensor(diag0[:], diag0[:], kfac[:, :, 1, :], ALU.add))
                            st.post(dve.tensor_scalar(diag1[:], diag1[:], -SCALE, None, ALU.mult))
                            st.settle()
                            st.post(dve.tensor_tensor(diag0[:], diag0[:], kfac[:, :, 2, :], ALU.add))
                            st.settle()
                            st.post(dve.tensor_scalar(diag0[:], diag0[:], -SCALE, None, ALU.mult))
                            st.settle()
                        attention_dve(dve, st, mode, 0)
                        scale_dve(dve, st, ring, 0, YT[:])
                        bank = ring.take(dve)
                        ring.release(st, dve.tensor_tensor(Y[:], two(bank), X[:], ALU.add))
                        st.settle()
                        st.post(dve.tensor_tensor(Y[:], Y[:], w0("proj_b").unsqueeze(1).broadcast_to([P, TT, D]), ALU.add))
                        st.settle()
                        layernorm(dve, st, X2, Y, 2, "x_ready")
                        st.settle()
                        rmsnorm(dve, st, X, X2, w0("norm1"), 3, "xn_ready")
                        move(dve, st, ring, XT[:, :, 1:T + 1])

                        def rotate(dst):
                            for w, to in ((w0("cos"), dst[:, :, 1:T + 1]), (w0("sin"), Y[:])):
                                bank = ring.take(dve)
                                ring.release(st, dve.tensor_tensor(to, two(bank), w.unsqueeze(1).broadcast_to([P, KT, T]),
                                                                   ALU.mult))
                            st.settle()
                            return dve.tensor_tensor(dst[:, :, 1:T + 1], dst[:, :, 1:T + 1], Y[:], ALU.add)

                        bank = ring.take(dve)
                        ring.release(st, dve.tensor_copy(lat, two(bank, LAT)))
                        st.settle()
                        layernorm(dve, st, lat, lat, 4, "lat_norm")
                        st.settle()
                        for t in range(TT):
                            st.post(dve.tensor_tensor(lat[:, t, :], lat[:, t, :], w0("ln_g"), ALU.mult))
                        st.settle()
                        for t in range(TT):
                            st.post(dve.tensor_tensor(lat[:, t, :], lat[:, t, :], w0("ln_b"), ALU.add), S("lat_ready"))
                        st.settle()
                        st.post(rotate(QF), S("qk_ready"))
                        bank = ring.take(dve)
                        ring.release(st, dve.tensor_copy(YT[:, 0, :], bank[:, 0:T]))
                        st.settle()
                        mask_q_dve(dve, st, QF[:, :, 1:T + 1])
                        st.post(rotate(KF), S("k_rotated"))
                        move_v(dve, st, ring)
                        attention_dve(dve, st, "causal", 1)
                        scale_dve(dve, st, ring, 1, YT[:])
                        bank = ring.take(dve)
                        ring.release(st, dve.tensor_tensor(X[:], two(bank), X2[:], ALU.add))
                        st.settle()
                        rmsnorm(dve, st, Z, X, w0("norm2"), 5, "xn_ready")
                        st.post(dve.tensor_tensor(Y[:], X[:], X2[:], ALU.add))
                        move(dve, st, ring, YT[:])
                        lg = small[:, 80:88].rearrange("p (t e) -> p t e", t=2)
                        bank = ring.take(dve)
                        ring.release(st, dve.tensor_tensor(lg, two(bank, NE), w0("gate_b").unsqueeze(1).broadcast_to([P, TT, NE]),
                                                           ALU.add))
                        st.settle()
                        st.post(dve.tensor_reduce(small[:, 88:90], lg, AX.X, ALU.max))
                        st.settle()
                        st.post(dve.tensor_tensor(onehot, lg, small[:, 88:90].unsqueeze(2).broadcast_to([P, TT, NE]),
                                                  ALU.is_equal))
                        st.settle()
                        st.post(dve.tensor_scalar(left[:, :, 1], onehot[:, :, 0], -1.0, 1.0, ALU.mult, ALU.add))
                        st.settle()
                        for e in range(1, NE):
                            st.post(dve.tensor_tensor(onehot[:, :, e], onehot[:, :, e], left[:, :, e], ALU.mult))
                            st.settle()
                            if e < NE - 1:
                                st.post(dve.tensor_tensor(left[:, :, e + 1], left[:, :, e], onehot[:, :, e], ALU.subtract))
                                st.settle()
                        for e in range(NE):
                            for t in range(TT):
                                st.post(dve.scalar_tensor_tensor(Y[:, t, :], w0("b2")[:, e * D:(e + 1) * D], onehot[:, t, e:e + 1],
                                                                 Y[:, t, :], ALU.mult, ALU.add))
                            st.settle()
                        for e in range(NE):
                            dve.wait_ge(S("down_done"), e + 1)
                            for t in range(TT):
                                ins = dve.scalar_tensor_tensor(Y[:, t, :], PT[e % 2][:, t * D:(t + 1) * D], onehot[:, t, e:e + 1],
                                                               Y[:, t, :], ALU.mult, ALU.add)
                                st.post(ins, S("y_used") if t else None)
                            st.settle()
                        layernorm(dve, st, X, Y, 6, "x_ready")
                        st.settle()
                        move(dve, st, ring, XT[:, :, 1:T + 1])
                        bank = ring.take(dve)
                        ring.release(st, dve.tensor_copy(FS[:], two(bank)))
                        bank = ring.take(dve)
                        ring.release(st, dve.tensor_copy(GS, bank[0:H, 0:T]))
                        st.settle()
                        st.post(dve.memset(small[:, 0:1], 0.0), S("feat_ready"))

                    @block.gpsimd
                    def _(pool):
                        ps = Steps(pool, S("pool"))
                        kb4 = KB[:].rearrange("p (b n) -> p b n", b=B)
                        ps.post(pool.tensor_copy(kcur[:].rearrange("p h a s -> p (h a s)"),
                                                 kb4[:, bass.ds(b, 1), :].rearrange("p o n -> p (o n)")), S("kcol_ready"))
                        kc4 = kcols[:].rearrange("p k (b n) -> p k b n", b=B)
                        ps.post(pool.tensor_copy(kcol[:], kc4[:, :, bass.ds(b, 1), :].rearrange("p k o n -> p k (o n)")),
                                S("kcol_ready"))
                        ps.post(pool.memset(QM[:, :, 0:1], 0.0))
                        ps.post(pool.memset(QM[:, :, T + 1:T + 2], 0.0))
                        ps.settle()
                        if mode == "conv":
                            for src, dst, a in ((c("halo_up"), haloU, 2), (c("halo_dn"), haloD, 0)):
                                for h in range(H):
                                    ps.post(pool.tensor_tensor(dst[:, h], src.unsqueeze(1).broadcast_to([P, 3, 32]),
                                                               kcur[:, h, a, :].unsqueeze(2).broadcast_to([P, 3, 32]), ALU.mult))
                            ps.settle()
                        root_pool(pool, 1)
                        pool.wait_ge(S("qk_ready"), 1)
                        if mode == "near":
                            for j, (i0, i1) in enumerate(((0, 1), (0, 2), (1, 2))):
                                ps.post(pool.tensor_tensor(NP[j], QF[:, :, i0:i0 + T], KF[:, :, i1:i1 + T], ALU.mult), S("products"))
                            for a in range(3):
                                for j in range(3):
                                    dst = KC[:, 1, a, :] if j == 0 else Xin[:, j - 1, :]
                                    ps.post(pool.tensor_scalar(dst, KF[:, 1, j:j + T], kcol[:, 1, 3 * a + j:3 * a + j + 1], None,
                                                               ALU.mult))
                                ps.settle()
                                for j in range(2):
                                    ps.post(pool.tensor_tensor(KC[:, 1, a, :], KC[:, 1, a, :], Xin[:, j, :], ALU.add),
                                            S("kc_high") if j else None)
                                    ps.settle()
                        mask_q_pool(pool, ps, QF[:, :, 1:T + 1])
                        if mode == "conv":
                            sh = k3(c("shift"), 3)
                            for h in range(H):
                                if h >= 2:
                                    pool.wait_ge(S("scores_ready"), h - 1)
                                for a in range(3):
                                    dst = band[h % 2] if a == 0 else btmp
                                    ps.post(pool.tensor_tensor(dst[:], sh[:, a, :].unsqueeze(1).broadcast_to([P, 3, P]),
                                                               kcur[:, h, a, :].unsqueeze(2).broadcast_to([P, 3, P]), ALU.mult))
                                    ps.settle()
                                    if a:
                                        ps.post(pool.tensor_tensor(band[h % 2][:], band[h % 2][:], btmp[:], ALU.add),
                                                S("band_ready") if a == 2 else None)
                                        ps.settle()
                        for n in range(2, 5):
                            root_pool(pool, n)
                        pool.wait_ge(S("qk_ready"), 2)
                        mask_q_pool(pool, ps, QF[:, :, 1:T + 1])
                        for n in range(5, 7):
                            root_pool(pool, n)

                    @block.scalar
                    def _(act):
                        attention_act(act, mode, 0)
                        attention_act(act, "causal", 1)
                        for e in range(NE):
                            if e >= 2:
                                act.wait_ge(S("down_done"), e - 1)
                            for j in range(MT // 2):
                                u = e * (MT // 2) + j
                                act.wait_ge(S("up_done"), u + 1)
                                for m in range(2):
                                    col = e * MT + 2 * j + m
                                    ins = act.activation(HTv[e % 2][:, 2 * j + m, :], SMs[u % 3][:, m * T:(m + 1) * T], ACT.Relu,
                                                         bias=w0("b1")[:, col:col + 1])
                                    ins.then_inc(S("relu_done"), 1)
                clear_block()

        differs = nc.values_load(flag[:])
        with nc.If(differs == 0):
            layer0("near")
        with nc.Else():
            layer0("conv")

        with nc.Block() as block:
            @block.sync
            def _(sp):
                for i in range(B):
                    sp.dma_start(big[i * H:(i + 1) * H, 0:4096].rearrange("h (m n) -> h m n", m=4),
                                 feat[i].rearrange("m (h c) t -> h m (c t)", h=H)).then_inc(S("feat_in"), 16)
                sp.dma_start(Z[:, 0, :], gate_d.rearrange("b h t -> (b h) t")).then_inc(S("feat_in"), 16)
                sp.dma_start(arena[:, 0:LAY1_N], lay1).then_inc(S("lay1_in"), 16)
                sp.wait_ge(S("lay1_in"), 16)

            pl = big[:, 0:4096].rearrange("p (m c t) -> p m c t", m=4, c=4)
            free = arena[:, LAY1_N:LAY1_N + 7700]
            sq = free[:, 0:1536].rearrange("p (c t) -> p c t", c=6)
            sqs = [sq, free[:, 1536:3072].rearrange("p (c t) -> p c t", c=6)]
            outer = free[:, 1536:3072].rearrange("p (c t) -> p c t", c=6)
            rdM = free[:, 3072:4608].rearrange("p (c t) -> p c t", c=6)
            MM = free[:, 4608:4608 + 6 * 257].rearrange("p (c t) -> p c t", c=6)
            L = [free[:, a:a + 1536].rearrange("p (c t) -> p c t", c=6) for a in (6150, 4608)]
            n2 = PR[0][:, 0, :]
            nr = PR[0][:, 1, :]
            dt_ = PR[1][:, 0, :]
            wt = PR[1][:, 1, :]
            rdp = big[:, 0:1536].rearrange("p (c t) -> p c t", c=6)
            tmpb = outer[:, 0:3, :]

            def bc(ap, n):
                return ap.unsqueeze(1).broadcast_to([P, n, T])

            @block.vector
            def _(dve):
                st = Steps(dve, S("dve"))
                dve.wait_ge(S("feat_in"), 16 * (B + 1))
                for s in range(2):
                    p1, p2 = pl[:, 2 * s], pl[:, 2 * s + 1]
                    for lo, n, at in ((0, 3, 0), (1, 2, 3), (2, 1, 5)):
                        st.post(dve.tensor_tensor(L[s][:, at:at + n, :], bc(p1[:, lo, :], n), p2[:, lo + 1:lo + 1 + n, :], ALU.mult))
                        st.post(dve.tensor_tensor(tmpb[:, 0:n, :], p1[:, lo + 1:lo + 1 + n, :], bc(p2[:, lo, :], n), ALU.mult))
                        st.settle()
                        st.post(dve.tensor_tensor(L[s][:, at:at + n, :], L[s][:, at:at + n, :], tmpb[:, 0:n, :], ALU.subtract))
                        st.settle()
                for s in range(2):
                    st.post(dve.tensor_tensor(sqs[s], L[s], L[s], ALU.mult))
                st.settle()
                for s in range(2):
                    st.post(dve.tensor_reduce(PR[0][:, s, :], sqs[s].rearrange("p c t -> p t c"), AX.X, ALU.add), S("n2_ready"))
                dve.wait_ge(S("root_ready"), 1)
                st.post(dve.tensor_scalar(PR[1][:], PR[1][:], 1e-12, None, ALU.max))
                st.settle()
                st.post(dve.reciprocal(PR[1][:], PR[1][:]))
                st.settle()
                st.post(dve.tensor_tensor(L[0], L[0], bc(PR[1][:, 0, :], 6), ALU.mult))
                for i in range(6):
                    st.post(dve.scalar_tensor_tensor(rdp[:, 5 - i, :], L[1][:, i, :], -1.0 if i in (1, 4) else 1.0, PR[1][:, 1, :],
                                                     ALU.mult, ALU.mult))
                st.settle()
                dve.wait_ge(S("sig_exp"), 3)
                sg = small[:, 0:8]
                st.post(dve.tensor_scalar(sg[:, 0:2], small[:, 8:10], 1.0, None, ALU.add))
                st.post(dve.tensor_scalar(Z[:, 0, :], Z[:, 0, :], 1.0, None, ALU.add))
                st.settle()
                st.post(dve.reciprocal(sg[:, 2:4], sg[:, 0:2]))
                st.post(dve.reciprocal(Z[:, 0, :], Z[:, 0, :]))
                st.settle()
                dec, mix = sg[:, 2:3], sg[:, 3:4]
                st.post(dve.tensor_scalar(sg[:, 4:5], dec, 1e-6, None, ALU.max))
                st.settle()
                st.post(dve.reciprocal(sg[:, 5:6], sg[:, 4:5]))
                st.post(dve.tensor_scalar(sg[:, 0:1], dec, 1e-6, None, ALU.is_ge))
                st.settle()
                st.post(dve.tensor_tensor(sg[:, 6:7], dec, sg[:, 5:6], ALU.mult))
                st.settle()
                st.post(dve.tensor_scalar(sg[:, 6:7], sg[:, 6:7], sg[:, 0:1], 1.0, ALU.max, ALU.min))
                st.post(dve.tensor_scalar(dt_, ones[:], dec, None, ALU.mult))
                st.post(dve.memset(MM[:, :, 0:1], 0.0))
                st.settle()
                st.post(dve.tensor_scalar(n2, ones[:], sg[:, 6:7], None, ALU.mult))
                st.post(dve.memset(nr, 0.0))
                st.settle()
                st.post(dve.tensor_tensor_scan(wt[:, 1:T], n2[:, 1:T], nr[:, 1:T], 1.0, ALU.mult, ALU.add))
                st.post(dve.memset(wt[:, 0:1], 1.0))
                st.settle()
                for i in range(6):
                    st.post(dve.tensor_tensor(n2, L[0][:, i, :], wt, ALU.mult))
                    st.settle()
                    st.post(dve.tensor_tensor(outer, L[0], bc(n2, 6), ALU.mult))
                    st.settle()
                    for j in range(6):
                        st.post(dve.tensor_tensor_scan(MM[:, j, 1:T + 1], dt_, outer[:, j, :], 0.0, ALU.mult, ALU.add))
                    st.settle()
                    if i == 0:
                        st.post(dve.tensor_tensor(rdM, MM[:, :, 0:T], bc(rdp[:, i, :], 6), ALU.mult))
                    else:
                        st.post(dve.tensor_tensor(sq, MM[:, :, 0:T], bc(rdp[:, i, :], 6), ALU.mult))
                        st.settle()
                        st.post(dve.tensor_tensor(rdM, rdM, sq, ALU.add))
                    st.settle()
                st.post(dve.tensor_scalar(rdM, rdM, dec, None, ALU.mult))
                st.settle()
                st.post(dve.tensor_tensor(sq, rdM, rdp, ALU.mult))
                st.post(dve.tensor_tensor(outer, rdM, rdM, ALU.mult))
                st.settle()
                st.post(dve.tensor_reduce(n2, sq.rearrange("p c t -> p t c"), AX.X, ALU.add))
                st.post(dve.tensor_reduce(nr, outer.rearrange("p c t -> p t c"), AX.X, ALU.add))
                st.post(dve.tensor_scalar(sg[:, 7:8], mix, -1.0, 1.0, ALU.mult, ALU.add))
                st.settle()
                st.post(dve.tensor_scalar(n2, n2, sg[:, 7:8], None, ALU.mult))
                st.settle()
                st.post(dve.scalar_tensor_tensor(n2, nr, mix, n2, ALU.mult, ALU.add))
                st.settle()
                st.post(dve.tensor_scalar(n2, n2, c("mscale"), None, ALU.mult), S("score_ready"))
                dve.wait_ge(S("score_exp"), 1)
                st.post(dve.tensor_scalar(n2, n2, 1.0, None, ALU.add))
                st.settle()
                st.post(dve.reciprocal(n2, n2))
                st.settle()
                st.post(dve.tensor_tensor(n2, n2, Z[:, 0, :], ALU.mult), S("gated_ready"))
                dve.wait_ge(pj_full[0], 1)
                st.post(dve.tensor_copy(Gt[:], PJ[0][:, 0:TT * B].rearrange("p (t b) -> p t b", t=TT)))
                dve.wait_ge(S("lay1_in"), 16)
                st.post(dve.tensor_tensor(w1("r2b"), w1("r2b"), w1("eb"), ALU.add))
                st.settle()

            @block.scalar
            def _(act):
                act.wait_ge(S("feat_in"), 16 * (B + 1))
                act.activation(small[:, 8:9], c("decay"), ACT.Exp, scale=-1.0).then_inc(S("sig_exp"), 1)
                act.activation(small[:, 9:10], c("mix"), ACT.Exp, scale=-1.0).then_inc(S("sig_exp"), 1)
                act.activation(Z[:, 1, :], Z[:, 0, :], ACT.Identity, bias=c("memg_b")).then_inc(S("gate_biased"), 1)
                act.wait_ge(S("gate_biased"), 1)
                act.activation(Z[:, 0, :], Z[:, 1, :], ACT.Exp, scale=-1.0).then_inc(S("sig_exp"), 1)
                act.wait_ge(S("n2_ready"), 2)
                act.activation(PR[1][:], PR[0][:], ACT.Sqrt).then_inc(S("root_ready"), 1)
                act.wait_ge(S("score_ready"), 1)
                act.activation(n2, n2, ACT.Exp, scale=-1.0).then_inc(S("score_exp"), 1)

            @block.tensor
            def _(pe):
                pe.wait_ge(S("gated_ready"), 1)
                for t in range(TT):
                    ins = pe.matmul(PJ[0][:, t * B:(t + 1) * B], n2[:, t * P:(t + 1) * P], c("bsel"), start=True, stop=True)
                ins.then_inc(pj_full[0], 1)
        clear_block()

        spare = arena[:, LAY1_N + 3584:LAY1_N + 7700]
        idx_i = spare[:, 0:128].bitcast(I32).rearrange("p (t n) -> p t n", t=TT)
        idx = small[:].rearrange("p (t n) -> p t n", t=TT)
        idxn = spare[:, 128:256].rearrange("p (t n) -> p t n", t=TT)
        iotab = spare[:, 256:384].bitcast(BF16)
        oneh = [spare[:, a:a + 1024].bitcast(BF16).rearrange("p (j n) -> p j n", j=8) for a in (384, 1966)]
        zerob = spare[:, 2990:2991].bitcast(BF16)[:, 0:1]
        Cn = arena[:, LAY1_N:LAY1_N + 512].rearrange("p (t n) -> p t n", t=2)
        gcur = spare[:, 1408:1410]
        lg8 = spare[:, 1410:1442].rearrange("p (i e) -> p i e", i=4)
        mx4 = spare[:, 1442:1454].rearrange("p (i e) -> p i e", i=3)
        WT8 = spare[0:KE, 1454:1966].rearrange("p (a t) -> p a t", a=2)
        big2 = arena[:, LAY1_N:LAY1_N + 3584]
        XC = big[:, 0:512].rearrange("p (k t) -> p k t", k=2)
        FQ = [big[:, 512 + i * 512:1024 + i * 512].rearrange("p (k t) -> p k t", k=2) for i in range(4)]
        HR = [big[:, 2560 + i * 512:3072 + i * 512].rearrange("p (k t) -> p k t", k=2) for i in range(2)]
        YW = [big2[:, 512 + i * 512:1024 + i * 512].rearrange("p (k t) -> p k t", k=2) for i in range(4)]
        PD = big2[:, 2560:3584].rearrange("p (k t) -> p k t", k=4)
        with nc.Fori(0, B) as b:
            with nc.Block() as block:
                ring = Ring(PJ, pj_full, pj_free)

                @block.sync
                def _(sp):
                    sp.dma_start(X[:], x4_d[bass.ds(b, 1)].rearrange("o p t d -> (o p) t d")).then_inc(S("x_in"), 16)
                    sp.dma_start(CT[:], ctxT[bass.ds(b, 1)].rearrange("o p k t -> (o p) k t")).then_inc(S("ctx_in"), 16)
                    sp.dma_start(idx_i, itok[bass.ds(b, 1)].rearrange("o p t n -> (o p) t n")).then_inc(S("idx_in"), 16)
                    sp.wait_ge(S("out_ready"), 2)
                    sp.dma_start(out[bass.ds(b, 1)].rearrange("o p t d -> (o p) t d"), OUT[:]).then_inc(S("out_done"), 16)
                    sp.wait_ge(S("out_done"), 16)

                @block.tensor
                def _(pe):
                    pe.wait_ge(S("x_in"), 16)
                    flip(pe, ring, X)
                    ring.moved(pe)
                    XTc = XT[:, :, 1:T + 1]
                    W = k3(w1("qkv"), 2)
                    for i in range(2):
                        bank = ring.claim(pe)
                        ring.fill(columns(pe, bank, W, XTc, i * D))
                    rows(pe, ring, XTc, W, 2 * D, 3 * D)
                    rows(pe, ring, XTc, k3(w1("memv"), 2), 0, D)
                    ring.moved(pe)
                    tally = ring.claim(pe)

                    def sum_hot(s):
                        g = s - 1
                        if not 0 <= g < TT * NI // 8:
                            return
                        t, j0 = g // 8, g % 8 * 8
                        pe.wait_ge(S("hot_ready"), g + 1)
                        for j in range(8):
                            ins = pe.matmul(tally[:, t * T:(t + 1) * T], identb[:], oneh[g % 2][:, j, :],
                                            start=j0 + j == 0, stop=j0 + j == NI - 1)
                        ins.then_inc(S("hot_used"), 1)

                    attention_pe(pe, "tally", 0, KF[:, :, 1:T + 1], sum_hot)
                    pe.wait_ge(S("hot_used"), TT * NI // 8)
                    ring.fill(pe.matmul(tally[0:1, 0:1], identb[:, 0:1], zerob, start=False, stop=True, skip_group_check=True))
                    pe.wait_ge(S("y_ready"), 2)
                    flip(pe, ring, Y)
                    scale_pe(pe, ring, 0)
                    pe.wait_ge(S("mixed_in"), 1)
                    ring.moved(pe)
                    rows(pe, ring, YT, k3(w1("outw"), 2), 0, D)
                    pe.wait_ge(S("x_ready"), 2)
                    flip(pe, ring, X2)
                    pe.wait_ge(S("ctx_in"), 16)
                    bank = ring.claim(pe)
                    for k in range(KT):
                        ins = pe.matmul(bank[:, 0:T], k3(w1("ydown"), 2)[:, k, :], CT[:, k, :], start=k == 0, stop=k == 1)
                    ring.fill(ins)
                    ring.moved(pe)
                    bank = ring.claim(pe)
                    ring.fill(columns(pe, bank, k3(w1("yq"), 2), XTc))
                    bank = ring.claim(pe)
                    for m in range(2):
                        ins = pe.matmul(bank[:, m * T:(m + 1) * T], w1("yup")[:, m * P:(m + 1) * P], YT[:, 0, :],
                                        start=True, stop=True)
                    ring.fill(ins)
                    bank = ring.claim(pe)
                    for t in range(TT):
                        ins = pe.matmul(bank[:, t * D:(t + 1) * D], YT[:, 0, t * P:(t + 1) * P],
                                        w1("yup")[:, D:2 * D], start=True, stop=True)
                    ring.fill(ins)
                    ring.moved(pe)
                    pe.wait_ge(S("count_ready"), 1)
                    attention_pe(pe, "count", 1, KF[:, :, 1:T + 1])
                    scale_pe(pe, ring, 1)
                    pe.wait_ge(oa_free, 2)
                    rows(pe, ring, YT, k3(w1("yout"), 2), 0, D)
                    pe.wait_ge(S("x_ready"), 4)
                    flip(pe, ring, X)
                    ring.moved(pe)
                    pe.wait_ge(S("cum_ready"), 2)

                    def cols(w, act_):
                        bank = ring.claim(pe)
                        ring.fill(columns(pe, bank, k3(w, 2), act_))

                    cols(w1("fQ"), XTc)
                    cols(w1("fK"), XC)
                    ring.moved(pe)
                    cols(w1("finv"), FQ[0])
                    cols(w1("finv"), FQ[1])
                    ring.moved(pe)
                    for br in range(2):
                        pe.wait_ge(S("exp_done"), 4 * H)
                        columns(pe, SM[br], k3(w1("r1"), 2), FQ[2 * br]).then_inc(S("router_full"), 1)
                    pe.wait_ge(S("router_act"), 4)
                    bank = ring.claim(pe)
                    for br in range(2):
                        for t in range(TT):
                            i = br * 2 + t
                            for k in range(KT):
                                ins = pe.matmul(bank[:, i * KE:(i + 1) * KE], HR[br][:, k, t * P:(t + 1) * P],
                                                k3(w1("r2"), 2)[:, k, :], start=k == 0, stop=k == 1)
                    ring.fill(ins)
                    pe.wait_ge(S("wts_ready"), 1)
                    bank = ring.claim(pe)
                    for i in range(4):
                        ins = pe.transpose(bank[0:KE, i * P:(i + 1) * P], lg8[:, i, :], ident)
                    ring.fill(ins)
                    ring.moved(pe)
                    for br in range(2):
                        for j in range(2):
                            u = br * 2 + j
                            if u < 2:
                                pe.wait_ge(S("router_act"), 2 * (u + 1))
                            else:
                                pe.wait_ge(S("yw_copied"), u - 1)
                            columns(pe, SM[u % 2], k3(w1(f"fW{br}"), 2), FQ[2 * br + 1], 2 * j * P).then_inc(S("yw_full"), 1)
                            bank = ring.claim(pe)
                            ring.fill(columns(pe, bank, k3(w1(f"fV{br}"), 2), FQ[2 * br], 2 * j * P))
                            bank = ring.claim(pe)
                            for m in range(2):
                                ins = pe.matmul(bank[:, m * T:(m + 1) * T], k3(w1("sel8"), 4)[0:KE, 2 * j + m, :], WT8[:, br, :],
                                                start=True, stop=True)
                            ring.fill(ins)
                        ring.moved(pe)
                        bank = ring.claim(pe)
                        for t in range(TT):
                            for m in range(4):
                                pe.matmul(bank[:, t * D:(t + 1) * D], PD[:, m, t * P:(t + 1) * P],
                                          k3(w1(f"fU{br}"), 4)[:, m, :], start=m == 0, stop=False)
                            ins = pe.matmul(bank[:, t * D:(t + 1) * D], WT8[:, br, t * P:(t + 1) * P],
                                            k3(w1("b8"), 2)[0:KE, br, :], start=False, stop=True)
                        ring.fill(ins)
                    pe.wait_ge(S("mixed"), 2)
                    flip(pe, ring, Y)
                    ring.moved(pe)
                    rows(pe, ring, YT, k3(w1("fO"), 2), 0, D)

                @block.vector
                def _(dve):
                    st = Steps(dve, S("dve"))
                    st.post(dve.tensor_copy(gcur, Gt[:, :, bass.ds(b, 1)].rearrange("p t o -> p (t o)")))
                    st.post(dve.tensor_copy(iotab, c("iota")))
                    st.post(dve.memset(zerob, 0.0))
                    dve.wait_ge(S("idx_in"), 16)
                    st.post(dve.tensor_copy(idx, idx_i))
                    st.settle()
                    st.post(dve.tensor_scalar(idxn, idx, 0.0, float(T), ALU.is_lt, ALU.mult))
                    st.settle()
                    st.post(dve.tensor_tensor(idx, idx, idxn, ALU.add))
                    st.settle()
                    st.post(dve.tensor_scalar(idx, idx, 0.0, float(T - 1), ALU.max, ALU.min))
                    move(dve, st, ring, XT[:, :, 1:T + 1])
                    for i, dst in enumerate((QF, KF)):
                        bank = ring.take(dve)
                        for k in range(KT):
                            ins = dve.tensor_scalar(dst[:, k, 1:T + 1], bank[:, k * T:(k + 1) * T],
                                                    w1("qkb")[:, 2 * i + k:2 * i + k + 1], None, ALU.add)
                            ring.release(st, ins) if k else st.post(ins)
                    st.settle()
                    st.post(dve.memset(mx4[:, 0, 0:1], 0.0), S("qk_ready"))
                    mask_q_dve(dve, st, QF[:, :, 1:T + 1])
                    move_v(dve, st, ring, w1("qkv_b")[:, 2 * D:3 * D])
                    bank = ring.take(dve)
                    ring.release(st, dve.tensor_tensor(Y[:], two(bank), w1("memv_b").unsqueeze(1).broadcast_to([P, TT, D]),
                                                       ALU.add))
                    st.settle()
                    for t in range(TT):
                        st.post(dve.tensor_scalar(Y[:, t, :], Y[:, t, :], gcur[:, t:t + 1], None, ALU.mult), S("y_ready"))
                    st.settle()

                    def make_hot(g):
                        if g >= TT * NI // 8:
                            return
                        if g >= 2:
                            dve.wait_ge(S("hot_used"), g - 1)
                        t, j0 = g // 8, g % 8 * 8
                        for j in range(8):
                            ins = dve.tensor_scalar(oneh[g % 2][:, j, :], iotab, idx[:, t, j0 + j:j0 + j + 1], None, ALU.is_equal)
                            st.post(ins, S("hot_ready") if j == 7 else None)

                    attention_dve(dve, st, "tally", 0, between=make_hot)
                    bank = ring.take(dve)
                    st.post(dve.tensor_copy(Cn, two(bank)), S("count_ready"))
                    ring.release(st, dve.tensor_scalar(masks[:, 0], two(bank), 0.0, NEG, ALU.is_equal, ALU.mult))
                    move(dve, st, ring, Z[:])
                    scale_dve(dve, st, ring, 0, YT[:])
                    st.settle()
                    st.post(dve.tensor_tensor(YT[:], YT[:], Z[:], ALU.add), S("mixed_in"))
                    bank = ring.take(dve)
                    ring.release(st, dve.tensor_tensor(Y[:], two(bank), X[:], ALU.add))
                    st.settle()
                    st.post(dve.tensor_tensor(Y[:], Y[:], w1("out_b").unsqueeze(1).broadcast_to([P, TT, D]), ALU.add))
                    st.settle()
                    layernorm(dve, st, X2, Y, 1, "x_ready")
                    move(dve, st, ring, XT[:, :, 1:T + 1])
                    bank = ring.take(dve)
                    ring.release(st, dve.tensor_copy(YT[:, 0, :], bank[:, 0:T]))
                    for dst in (QF, KF):
                        bank = ring.take(dve)
                        ring.release(st, dve.tensor_copy(dst[:, :, 1:T + 1], two(bank)))
                    st.settle()
                    st.post(dve.memset(mx4[:, 0, 0:1], 0.0), S("qk_ready"))
                    mask_q_dve(dve, st, QF[:, :, 1:T + 1])
                    move_v(dve, st, ring)
                    attention_dve(dve, st, "count", 1, Cn)
                    scale_dve(dve, st, ring, 1, YT[:])
                    bank = ring.take(dve)
                    ring.release(st, dve.tensor_tensor(Y[:], two(bank), X2[:], ALU.add))
                    st.settle()
                    layernorm(dve, st, X, Y, 2, "x_ready")
                    move(dve, st, ring, XT[:, :, 1:T + 1])
                    st.settle()
                    for k in range(KT):
                        st.post(dve.tensor_tensor_scan(XC[:, k, :], ones[:], XT[:, k, 1:T + 1], 0.0, ALU.mult, ALU.add),
                                S("cum_ready"))
                    move(dve, st, ring, FQ[0])
                    move(dve, st, ring, FQ[1])
                    move(dve, st, ring, FQ[2])
                    move(dve, st, ring, FQ[3])
                    bank = ring.take(dve)
                    ring.release(st, dve.tensor_tensor(lg8, bank[:, 0:4 * KE].rearrange("p (i e) -> p i e", i=4),
                                                       w1("r2b").unsqueeze(1).broadcast_to([P, 4, KE]), ALU.add))
                    st.settle()
                    st.post(dve.tensor_reduce(mx4[:, 0, :], lg8, AX.X, ALU.max))
                    st.settle()
                    st.post(dve.tensor_tensor(lg8, lg8, mx4[:, 0, :].unsqueeze(2).broadcast_to([P, 4, KE]), ALU.subtract),
                            S("lg_shift"))
                    dve.wait_ge(S("lg_exp"), 1)
                    st.post(dve.tensor_reduce(mx4[:, 1, :], lg8, AX.X, ALU.add))
                    st.settle()
                    st.post(dve.reciprocal(mx4[:, 2, :], mx4[:, 1, :]))
                    st.settle()
                    st.post(dve.tensor_tensor(lg8, lg8, mx4[:, 2, :].unsqueeze(2).broadcast_to([P, 4, KE]), ALU.mult),
                            S("wts_ready"))
                    bank = ring.take(dve)
                    ring.release(st, dve.tensor_copy(WT8.rearrange("e a t -> e (a t)"), bank[0:KE, :]))
                    st.settle()
                    for br in range(2):
                        for j in range(2):
                            u = br * 2 + j
                            dve.wait_ge(S("yw_copied"), u + 1)
                            bank = ring.take(dve)
                            ring.release(st, dve.tensor_tensor(PD[:, 2 * j:2 * j + 2, :], two(bank), YW[u], ALU.mult))
                            st.settle()
                            bank = ring.take(dve)
                            ring.release(st, dve.tensor_tensor(PD[:, 2 * j:2 * j + 2, :], two(bank), PD[:, 2 * j:2 * j + 2, :],
                                                               ALU.mult))
                        bank = ring.take(dve)
                        if br == 0:
                            ring.release(st, dve.tensor_copy(Y[:], two(bank)))
                            st.settle()
                        else:
                            for t in range(TT):
                                ins = dve.scalar_tensor_tensor(Y[:, t, :], bank[:, t * D:(t + 1) * D], w1("alpha"), Y[:, t, :],
                                                               ALU.mult, ALU.add)
                                ring.release(st, ins) if t else st.post(ins)
                            st.settle()
                            for t in range(TT):
                                st.post(dve.tensor_scalar(Y[:, t, :], Y[:, t, :], w1("rn")[:, t:t + 1], None, ALU.mult),
                                        S("mixed"))
                    move(dve, st, ring, YT[:])
                    bank = ring.take(dve)
                    ring.release(st, dve.tensor_tensor(Y[:], two(bank), X[:], ALU.add))
                    st.settle()
                    layernorm(dve, st, OUT, Y, 3, "out_ready")
                    st.settle()

                @block.gpsimd
                def _(pool):
                    ps = Steps(pool, S("pool"))
                    pool.wait_ge(S("qk_ready"), 1)
                    mask_q_pool(pool, ps, QF[:, :, 1:T + 1])
                    root_pool(pool, 1)
                    pool.wait_ge(S("qk_ready"), 2)
                    mask_q_pool(pool, ps, QF[:, :, 1:T + 1])
                    root_pool(pool, 2)
                    root_pool(pool, 3)

                @block.scalar
                def _(act):
                    attention_act(act, "tally", 0)
                    attention_act(act, "count", 1)
                    for br in range(2):
                        act.wait_ge(S("router_full"), br + 1)
                        for m in range(2):
                            act.activation(HR[br][:, m, :], SM[br][:, m * T:(m + 1) * T], ACT.Gelu,
                                           bias=w1("r1b")[:, m:m + 1]).then_inc(S("router_act"), 1)
                    act.wait_ge(S("lg_shift"), 1)
                    act.activation(lg8, lg8, ACT.Exp).then_inc(S("lg_exp"), 1)
                    for u in range(4):
                        act.wait_ge(S("yw_full"), u + 1)
                        act.activation(YW[u], two(SM[u % 2]), ACT.Copy).then_inc(S("yw_copied"), 1)
            clear_block()


def kernel(**inputs):
    import numpy as np
    import concourse.bacc as bacc
    from concourse import mybir
    from concourse.bass_utils import run_bass_kernel_spmd as run

    a = {k: np.asarray(v) for k, v in inputs.items()}

    def chunks(w):
        k, n = w.shape
        return w.reshape(k // 128, 128, n).transpose(1, 0, 2).reshape(128, -1)

    def row(v, parts=128):
        return np.broadcast_to(np.reshape(v, (1, -1)), (128, v.size))

    def col(v):
        return v.reshape(-1, 128).T

    def first(w):
        z = np.zeros((128, w.shape[1]), w.dtype)
        z[:w.shape[0]] = w
        return z

    def tokens(v):
        return v.reshape(8, 2, 128, -1).transpose(0, 2, 1, 3)

    def feats(v):
        return v.transpose(0, 2, 1).reshape(8, 2, 128, 256).transpose(0, 2, 1, 3)

    f32 = np.float32
    p = "L0_xattn_"
    W = {"hist_W": chunks(a[p + "hist_W"]), "ctx_W1": chunks(a[p + "ctx_W1"]), "ctx_W2": a[p + "ctx_W2"],
         "ctx_b1": col(a[p + "ctx_b1"]), "kg_W1": chunks(a[p + "kg_W1"]), "kg_W2": chunks(a[p + "kg_W2"]),
         "hist_b": row(a[p + "hist_b"]), "hist_g": row(a[p + "hist_ln_g"]), "hist_lb": row(a[p + "hist_ln_b"]),
         "ctx_b2": row(a[p + "ctx_b2"]), "kg_b1": row(a[p + "kg_b1"]), "kg_g": row(a[p + "kg_ln_g"]),
         "kg_lb": row(a[p + "kg_ln_b"]), "kg_b2": row(a[p + "kg_b2"])}
    pos = np.arange(256, dtype=f32)[:, None]
    ang = pos * (1.0 / 10000.0 ** (np.arange(8, dtype=f32) / 8)).astype(f32)[None, :]
    ang = np.tile(ang.T, (16, 1))
    sign = np.tile(np.repeat(np.array([-1.0, 1.0], f32), 8), 8)[:, None]
    swap = np.arange(256) ^ 8
    q = "L0_ffn_"
    W.update({"wv": chunks(a["L0_attn_w_qkv"][512:].T), "wo": chunks(a["L0_attn_w_o"].T),
              "xqkv": chunks(np.concatenate([a[p + "Wq"], a[p + "Wk"], a[p + "Wv"]], axis=1)),
              "xproj": chunks(a[p + "proj_W"]), "proj_b": row(a[p + "proj_b"]),
              "mq": chunks(a[q + "Wq"].T), "mqs": chunks(a[q + "Wq"][swap].T), "muks": a[q + "Wuk"][swap].T,
              "mdkv": chunks(a[q + "Wdkv"].T),
              "mukv": np.concatenate([a[q + "Wuk"].T, a[q + "Wuv"].T], axis=1), "mo": chunks(a[q + "Wo"].T),
              "gate": chunks(a[q + "gate_w"].T), "W1": chunks(a[q + "W1"].reshape(4096, 256).T),
              "W2": chunks(a[q + "W2"].transpose(0, 2, 1).reshape(4096, 256)),
              "w1w": chunks(a["L1_attn_w1w"].T), "w2w": chunks(a["L1_attn_w2w"].T),
              "rw": chunks(np.concatenate([a["L1_attn_r1w"].T, a["L1_attn_r2w"].T], axis=1)),
              "memg": chunks(a["L1_attn_memg_w"].T), "norm1": row(a[q + "norm1_w"]), "norm2": row(a[q + "norm2_w"]),
              "ln_g": row(a[q + "ln_g"]), "ln_b": row(a[q + "ln_b"]), "gate_b": row(a[q + "gate_b"]),
              "b1": col(a[q + "b1"].reshape(-1)), "b2": row(a[q + "b2"]),
              "cos": np.cos(ang).astype(f32), "sin": (np.sin(ang) * sign).astype(f32)})
    r, s, t = "L1_attn_", "L1_xattn_", "L1_ffn_"

    def experts(w):
        return chunks(w.transpose(1, 0, 2).reshape(256, 512))

    def back(w):
        return chunks(w.transpose(0, 2, 1).reshape(512, 256))

    sel8 = np.zeros((128, 4, 128), f32)
    for m in range(4):
        for j in range(128):
            sel8[2 * m + j // 64, m, j] = 1.0
    W.update({"qkv": chunks(a[r + "qkv_w"].T), "memv": chunks(a[r + "memv_w"].T), "outw": chunks(a[r + "out_w"].T),
              "yq": chunks(a[s + "W_q"].T), "ydown": chunks(a[s + "W_kv_down"].T), "yup": a[s + "W_kv_up"].T,
              "yout": chunks(a[s + "W_out"].T), "fQ": chunks(a[t + "W_Q"].T), "fK": chunks(a[t + "W_K"].T),
              "fO": chunks(a[t + "W_O"].T), "finv": chunks(a[t + "W_inv"].T),
              "fV0": experts(a[t + "V_fwd"]), "fW0": experts(a[t + "W_fwd"]),
              "fV1": experts(a[t + "W_inv_exp"]), "fW1": experts(a[t + "V_inv"]),
              "fU0": back(a[t + "U_fwd"]), "fU1": back(a[t + "U_inv"]), "r1": chunks(a[t + "router_w1"].T),
              "r2": chunks(a[t + "router_w2"].T), "r1b": col(a[t + "router_b1"]), "r2b": row(a[t + "router_b2"]),
              "eb": row(a[t + "expert_bias"]), "alpha": row(a[t + "alpha_bi"]), "qkv_b": row(a[r + "qkv_b"]),
              "memv_b": row(a[r + "memv_b"]), "out_b": row(a[r + "out_b"]), "qkb": col(a[r + "qkv_b"][0:512]),
              "b8": first(np.concatenate([a[t + "b_fwd"], a[t + "b_inv"]], axis=1)), "sel8": sel8.reshape(128, 512),
              "rn": (1.0 / np.arange(1, 257, dtype=f32)).astype(f32).reshape(2, 128).T})
    shift = np.zeros((128, 3, 128), f32)
    for d in range(3):
        for i in range(128):
            if 0 <= i + d - 1 < 128:
                shift[i + d - 1, d, i] = 1.0
    up, dn = np.zeros((128, 32), f32), np.zeros((128, 32), f32)
    up[0, 31] = 1.0
    dn[127, 0] = 1.0
    bsel = np.zeros((128, 8), f32)
    for i in range(128):
        bsel[i, i // 16] = 1.0 / 16

    head1 = np.zeros((128, 8), f32)
    heads_on = np.zeros((128, 2, 128), f32)
    near0, near1 = np.zeros((128, 129), f32), np.zeros((128, 129), f32)
    for i in range(128):
        head1[i, i // 16] = 1.0
        near0[i, i] = near1[i, i + 1] = 1.0
        for k in range(2):
            heads_on[8 * k + i // 16, k, i] = 1.0

    def heads(v):
        return np.tile(v.reshape(16, 1), (8, 1))

    mask = a["mask_SxS_bc0"]
    W.update({"ident": np.eye(128, dtype=f32), "causal": np.triu(np.ones((256, 256), f32), 1).reshape(2, 128, 256).transpose(1, 0, 2), "shift": shift.reshape(128, 384), "halo_up": up,
              "halo_dn": dn, "iota": np.broadcast_to(np.arange(256, dtype=f32), (128, 256)),
              "half": np.full((128, 1), -0.5, f32), "decay": heads(a[r + "decay_logits"]), "mscale": heads(a[r + "mem_scale"]),
              "memg_b": heads(a[r + "memg_b"]), "mix": row(a[r + "iter_mix"]), "bsel": bsel, "headq": head1 * f32(SCALE),
              "head1": head1, "heads_on": heads_on.reshape(128, 256), "near0": near0, "near1": near1})

    def pack(table):
        return np.ascontiguousarray(np.concatenate([W[n].reshape(128, -1) for n, _ in table], axis=1))

    arrays = {"x": tokens(a["x"]), "xT": feats(a["x"]), "ctxT": feats(a["ctx_1024"]),
              "itok": tokens(a["itok_BxSx64_0_2047"]), "hist": pack(HIST), "lay0": pack(LAY0), "lay1": pack(LAY1),
              "const": pack(CONST), "mask": mask.reshape(2, 128, 256).transpose(1, 0, 2).astype(np.int32)}
    arrays = {k: np.ascontiguousarray(v) for k, v in arrays.items()}
    nc = bacc.Bacc("TRN2", target_bir_lowering=False, num_devices=1)
    ap = {k: nc.dram_tensor(k, v.shape, mybir.dt.from_np(v.dtype), kind="ExternalInput").ap() for k, v in arrays.items()}
    feat = nc.dram_tensor("feat", (B, 4, 64, T), F32, kind="Internal").ap()
    gate_d = nc.dram_tensor("gate_d", (B, H, T), F32, kind="Internal").ap()
    kern_d = nc.dram_tensor("kern_d", (B, 144), F32, kind="Internal").ap()
    flag_d = nc.dram_tensor("flag_d", (1, 1), I32, kind="Internal").ap()
    x4_d = nc.dram_tensor("x4_d", (B, P, TT, D), F32, kind="Internal").ap()
    out = nc.dram_tensor("out", (8, 128, 2, 256), F32, kind="ExternalOutput").ap()
    decoder(nc, ap["x"], ap["xT"], ap["ctxT"], ap["itok"], ap["hist"], ap["lay0"], ap["lay1"], ap["const"], ap["mask"],
            feat, gate_d, kern_d, flag_d, x4_d, out)
    got = run(nc, [arrays], core_ids=[0])
    return got.results[0]["out"].transpose(0, 2, 1, 3).reshape(8, 256, 256)
```

```python
from contextlib import ExitStack

import numpy as np

import concourse.bass as bass
from concourse import mybir

F32 = mybir.dt.float32
BF16 = mybir.dt.bfloat16
I32 = mybir.dt.int32
ALU = mybir.AluOpType
ACT = mybir.ActivationFunctionType
AX = mybir.AxisListType

P = 128
B, T, D = 8, 256, 256
TT = T // P
KT = D // P
H, HD = 16, 16
SCALE = 0.25
HC = 512
NE, HID = 4, 1024
MT = HID // P
LAT = 128
KE, R = 8, 64
NI = 64
NEG = -1.0e30
LN_EPS = 1e-5


HIST = [("hist_W", KT * HC), ("ctx_W1", 4 * P), ("ctx_W2", 1), ("ctx_b1", 1), ("kg_W1", 4 * D), ("kg_W2", KT * 144),
        ("hist_b", HC), ("hist_g", HC), ("hist_lb", HC), ("ctx_b2", 1),
        ("kg_b1", D), ("kg_g", D), ("kg_lb", D), ("kg_b2", 144)]
LAY0 = [("wv", 512), ("wo", 512), ("xqkv", KT * 768), ("xproj", 512), ("mq", 512), ("mqs", 512), ("muks", D), ("mdkv", KT * LAT), ("mukv", 512),
        ("mo", 512), ("gate", KT * NE), ("W1", KT * NE * HID), ("W2", NE * MT * D), ("w1w", KT * 64), ("w2w", KT * 64),
        ("rw", KT * P), ("memg", KT * H), ("proj_b", D), ("norm1", D), ("norm2", D), ("ln_g", LAT), ("ln_b", LAT),
        ("gate_b", NE), ("b1", NE * MT), ("b2", NE * D), ("cos", T), ("sin", T)]
LAY1 = [("qkv", KT * 768), ("memv", 512), ("outw", 512), ("yq", 512), ("ydown", KT * LAT), ("yup", 512), ("yout", 512),
        ("fQ", 512), ("fK", 512), ("fO", 512), ("finv", 512), ("fV0", 1024), ("fW0", 1024), ("fV1", 1024), ("fW1", 1024),
        ("fU0", 1024), ("fU1", 1024), ("r1", 512), ("r2", KT * KE), ("r1b", KT), ("r2b", KE), ("eb", KE), ("alpha", 1),
        ("qkv_b", 768), ("memv_b", D), ("out_b", D), ("qkb", 2 * KT), ("b8", 2 * D), ("sel8", 4 * P), ("rn", TT)]
CONST = [("ident", P), ("causal", TT * T), ("shift", 3 * P), ("halo_up", 32), ("halo_dn", 32), ("iota", T),
         ("half", 1), ("decay", 1), ("mscale", 1), ("memg_b", 1), ("mix", 1), ("bsel", B), ("headq", 8), ("head1", 8),
         ("heads_on", KT * P), ("near0", P + 1), ("near1", P + 1)]


def offsets(table):
    at, out = 0, {}
    for name, n in table:
        out[name] = (at, n)
        at += n
    return out, at


HIST_AT, HIST_N = offsets(HIST)
LAY0_AT, LAY0_N = offsets(LAY0)
LAY1_AT, LAY1_N = offsets(LAY1)
CONST_AT, CONST_N = offsets(CONST)


class Steps:

    def __init__(self, eng, own):
        self.eng, self.own, self.count, self.open = eng, own, {}, {}

    def post(self, ins, sem=None):
        sem = self.own if sem is None else sem
        n = self.count.get(sem.name, 0) + 1
        self.count[sem.name] = n
        ins.then_inc(sem, 1)
        self.open[sem.name] = (sem, n)
        return ins

    def settle(self):
        for sem, n in self.open.values():
            self.eng.wait_ge(sem, n)
        self.open = {}


class Ring:

    def __init__(self, banks, full, free):
        self.banks, self.full, self.free, self.filled, self.taken = banks, full, free, 0, 0

    def claim(self, pe):
        i, n = self.filled % len(self.banks), self.filled // len(self.banks)
        if n:
            pe.wait_ge(self.free[i], n)
        return self.banks[i]

    def fill(self, ins):
        ins.then_inc(self.full[self.filled % len(self.banks)], 1)
        self.filled += 1

    def moved(self, pe):
        for i in range(len(self.banks)):
            n = (self.filled - i + len(self.banks) - 1) // len(self.banks)
            if n:
                pe.wait_ge(self.free[i], n)

    def take(self, eng):
        i = self.taken % len(self.banks)
        eng.wait_ge(self.full[i], self.taken // len(self.banks) + 1)
        return self.banks[i]

    def release(self, steps, ins):
        steps.post(ins, self.free[self.taken % len(self.banks)])
        self.taken += 1


def decoder(nc, x, ctxT, itok, hist, lay0, lay1, const, negm, feat, gate_d, kern_d, x4_d, q_d, k_d, out):
    with ExitStack() as ctx:
        names = {}

        def sb(name, shape, dt=F32):
            return ctx.enter_context(nc.sbuf_tensor(name, shape, dt))

        def S(name):
            if name not in names:
                names[name] = ctx.enter_context(nc.semaphore(name))
            return names[name]

        SC = ctx.enter_context(nc.psum_tensor("SC", [P, 512], F32))
        SM = [ctx.enter_context(nc.psum_tensor(f"SM{i}", [P, 512], F32)) for i in range(2)]
        PT = [ctx.enter_context(nc.psum_tensor(f"PT{i}", [P, 512], F32)) for i in range(2)]
        OA = ctx.enter_context(nc.psum_tensor("OA", [P, 512], F32))
        PJ = [ctx.enter_context(nc.psum_tensor(f"PJ{i}", [P, 512], F32)) for i in range(2)]
        oa_free = S("oa_free")
        qkv_full, qkv_free = [S(f"qkv_full{i}") for i in range(2)], [S(f"qkv_free{i}") for i in range(2)]
        next_full, next_free = [S(f"next_full{i}") for i in range(2)], [S(f"next_free{i}") for i in range(2)]
        pj_full, pj_free = [S(f"pj_full{i}") for i in range(2)], [S(f"pj_free{i}") for i in range(2)]

        arena = sb("arena", [P, max(LAY0_N, LAY1_N + 7700, HIST_N)])
        const_sb = sb("const_sb", [P, CONST_N])
        KB = sb("KB", [P, B * 144])
        kcols = sb("kcols", [P, KT, B * 9])

        HIST0 = arena.shape[1] - HIST_N

        def hist_w(name):
            a, n = HIST_AT[name]
            return arena[:, HIST0 + a:HIST0 + a + n]

        def w0(name):
            a, n = LAY0_AT[name]
            return arena[:, a:a + n]

        def w1(name):
            a, n = LAY1_AT[name]
            return arena[:, a:a + n]

        def c(name):
            a, n = CONST_AT[name]
            return const_sb[:, a:a + n]

        def k3(ap, k):
            return ap.rearrange("p (k n) -> p k n", k=k)

        ident = c("ident")

        identb = sb("identb", [P, P], BF16)
        notmask = sb("notmask", [P, TT, T])
        masks = sb("masks", [P, 2, TT, T], BF16)
        ones = sb("ones", [P, T])
        OUT = sb("OUT", [P, TT, D])
        Xin = sb("Xin", [P, TT, D])
        X = sb("X", [P, TT, D])
        X2 = sb("X2", [P, TT, D])
        Y = sb("Y", [P, TT, D])
        Z = sb("Z", [P, TT, D])
        XT = sb("XT", [P, KT, T + 1])
        YT = sb("YT", [P, KT, T])
        CT = sb("CT", [P, KT, T])
        VM = sb("VM", [P, TT, KT, 9 * P])
        QF = sb("QF", [P, KT, T + 2])
        KF = sb("KF", [P, KT, T + 2])
        mask_in = OUT[:].bitcast(I32)
        PR = [sb(f"PR{i}", [P, TT, T]) for i in range(2)]
        PS = [sb(f"PS{i}", [P, 2, T]) for i in range(2)]
        AM = [sb(f"AM{i}", [P, TT, T + 2]) for i in range(2)]
        band = [sb(f"band{i}", [P, 3, P]) for i in range(2)]
        btmp = sb("btmp", [P, 3, P])
        haloU = sb("haloU", [P, H, 3, 32])
        KC = haloU[:].rearrange("p h s c -> p (h s c)").rearrange("p (k a t) -> p k a t", k=KT, a=3)
        haloD = sb("haloD", [P, H, 3, 32])
        kcur = sb("kcur", [P, H, 3, 3])
        negmax = sb("negmax", [P, H, TT])
        rsum = sb("rsum", [P, TT, H])
        rinv = sb("rinv", [P, TT, H])
        small = sb("small", [P, 128])
        stats = sb("stats", [P, TT, 6])
        mv = sb("mv", [P, TT, 2])
        var = sb("var", [P, TT])
        rstd = sb("rstd", [P, TT])
        square = sb("square", [P, TT])
        rrms = sb("rrms", [P, TT])
        CC = sb("CC", [P, B, 4])
        big = sb("big", [P, H * (T + 2)])
        Gt = sb("Gt", [P, TT, B])
        QM = big[:].rearrange("p (h t) -> p h t", h=H)
        QS = big[:, 8 * (T + 2):8 * (T + 2) + 8 * T].rearrange("p (h t) -> p h t", h=8)
        KS = haloD[:].rearrange("p h s c -> p (h s c)")[:, 0:4 * T].rearrange("p (r t) -> p r t", r=4)
        kcol = sb("kcol", [P, KT, 9])
        rT = sb("rT", [H, T])
        flag = sb("flag", [1, 1], I32)
        kfac = sb("kfac", [P, TT, 3, H])
        diag0 = sb("diag0", [P, TT, H])
        diag1 = sb("diag1", [P, TT, H])


        def flip(pe, ring, src, ready=None):
            bank = ring.claim(pe)
            for k in range(KT):
                for t in range(TT):
                    ins = pe.transpose(bank[:, k * T + t * P:k * T + (t + 1) * P], src[:, t, k * P:(k + 1) * P], ident)
            ring.fill(ins)

        def rows(pe, ring, actT, w, n0, n1):
            bank = ring.claim(pe)
            n = n1 - n0
            for t in range(TT):
                for k in range(KT):
                    ins = pe.matmul(bank[:, t * n:(t + 1) * n], actT[:, k, t * P:(t + 1) * P], w[:, k, n0:n1],
                                    start=k == 0, stop=k == KT - 1)
            ring.fill(ins)

        SUM = [SC[:, 0:D], SM[1][:, 0:D]]

        def tiles(src):
            return src if isinstance(src, list) else [src[:, t, :] for t in range(TT)]

        def residual(pe, src):
            for t in range(TT):
                ins = pe.matmul(SUM[t], ident, src[:, t, :], start=True, stop=False)
            ins.then_inc(S("residual_read"), 1)

        def keep_clock(pe, n):
            for _ in range(n):
                pe.matmul(SM[0][:], identb[:], masks[:, 1].rearrange("p t n -> p (t n)"), start=True, stop=True)

        def add_rows(pe, actT, w):
            for t in range(TT):
                for k in range(KT):
                    ins = pe.matmul(SUM[t], actT[:, k, t * P:(t + 1) * P], w[:, k, :],
                                    start=False, stop=k == KT - 1)
            ins.then_inc(S("sum_ready"), 1)

        def columns(pe, bank, w, actT, m0=0, stop=True):
            for m in range(2):
                for k in range(KT):
                    ins = pe.matmul(bank[:, m * T:(m + 1) * T], w[:, k, m0 + m * P:m0 + (m + 1) * P], actT[:, k, :],
                                    start=k == 0, stop=k == KT - 1)
            return ins

        def two(bank, n=256):
            return bank[:, 0:2 * n].rearrange("p (a b) -> p a b", a=2)

        def move(dve, st, ring, dst):
            bank = ring.take(dve)
            ring.release(st, dve.tensor_copy(dst, two(bank)))

        def root_dve(dve, st, src, scale, eps, n):
            st.post(dve.tensor_scalar(var[:], src, scale, eps, ALU.mult, ALU.add), S("var_ready"))
            dve.wait_ge(S("rstd_ready"), n)

        def root_pool(pool, n):
            pool.wait_ge(S("var_ready"), n)
            pool.tensor_tensor(rstd[:], var[:], c("half").broadcast_to([P, TT]), ALU.pow).then_inc(S("rstd_ready"), 1)

        def layernorm(dve, st, dst, src, n, flag):
            src = tiles(src)
            for t in range(TT):
                st.post(dve.bn_stats(stats[:, t, :], src[t]))
            st.settle()
            for t in range(TT):
                st.post(dve.bn_aggr(mv[:, t, :], stats[:, t, :]))
            st.settle()
            root_dve(dve, st, mv[:, :, 1], 1.0, LN_EPS, n)
            for t in range(TT):
                st.post(dve.tensor_scalar(dst[:, t, :], src[t], mv[:, t, 0:1], rstd[:, t:t + 1],
                                          ALU.subtract, ALU.mult), S(flag))

        def layernorm_rmsnorm(dve, st, dst, scaled, src, weight, n):
            src = tiles(src)
            for t in range(TT):
                st.post(dve.bn_stats(stats[:, t, :], src[t]))
            st.settle()
            for t in range(TT):
                st.post(dve.bn_aggr(mv[:, t, :], stats[:, t, :]))
            st.settle()
            st.post(dve.tensor_scalar(var[:], mv[:, :, 1], LN_EPS, None, ALU.add), S("var_ready"))
            st.settle()
            st.post(dve.reciprocal(square[:], var[:]))
            st.settle()
            st.post(dve.tensor_tensor(square[:], square[:], mv[:, :, 1], ALU.mult))
            st.settle()
            st.post(dve.tensor_scalar(square[:], square[:], 1e-6, None, ALU.add), S("square_ready"))
            dve.wait_ge(S("rstd_ready"), n)
            for t in range(TT):
                st.post(dve.tensor_scalar(dst[:, t, :], src[t], mv[:, t, 0:1], rstd[:, t:t + 1], ALU.subtract, ALU.mult),
                        S("x_ready"))
            dve.wait_ge(S("rrms_ready"), 1)
            st.settle()
            for t in range(TT):
                st.post(dve.scalar_tensor_tensor(scaled[:, t, :], dst[:, t, :], rrms[:, t:t + 1], weight, ALU.mult, ALU.mult),
                        S("xn_ready"))

        def rmsnorm(dve, st, dst, src, weight, n, flag):
            src = tiles(src)
            for t in range(TT):
                st.post(dve.bn_stats(stats[:, t, :], src[t]))
            st.settle()
            for t in range(TT):
                st.post(dve.bn_aggr(mv[:, t, :], stats[:, t, :]))
            st.settle()
            st.post(dve.tensor_tensor(small[:, 100:102], mv[:, :, 0], mv[:, :, 0], ALU.mult))
            st.settle()
            st.post(dve.tensor_tensor(small[:, 100:102], small[:, 100:102], mv[:, :, 1], ALU.add))
            st.settle()
            root_dve(dve, st, small[:, 100:102], 1.0, 1e-6, n)
            st.settle()
            for t in range(TT):
                st.post(dve.scalar_tensor_tensor(dst[:, t, :], src[t], rstd[:, t:t + 1], weight,
                                                 ALU.mult, ALU.mult), S(flag))

        def vm_diag(t):
            return VM[:, t].rearrange("p k (h n) -> p k h n", h=8)[:, :, :, 0:HD]

        def move_v(dve, st, ring, bias=None):
            bank = ring.take(dve)
            for t in range(TT):
                src = bank[:, t * D:(t + 1) * D].rearrange("p (k h d) -> p k h d", k=KT, h=8)
                if bias is None:
                    ins = dve.tensor_copy(vm_diag(t), src)
                else:
                    ins = dve.tensor_tensor(vm_diag(t), src, bias.rearrange("p (k h d) -> p k h d", k=KT, h=8), ALU.add)
                ring.release(st, ins) if t == TT - 1 else st.post(ins)

        def mask_q(act, h, factors="headq"):
            act.activation(QM[:, h, 1:T + 1], QF[:, h // 8, 1:T + 1], ACT.Copy,
                           scale=c(factors)[:, h % 8:h % 8 + 1]).then_inc(S("q_ready"), 1)

        SMs = [SM[0], SM[1], SC]

        def n_banks(mode):
            return 2 if mode == "conv" else 3

        def causal_like(mode):
            return mode in ("causal", "tally", "near")

        def attention_pe(pe, mode, inst, KFd, between=None, first=None):
            base = inst * H
            half = causal_like(mode)
            NB = n_banks(mode)
            stacks = 8 if first == "near" else 0

            def bank_free(n):
                done = max(n - NB + 1, base)
                if done > 0:
                    pe.wait_ge(S("exp_done"), 2 * done)

            def scores(h):
                n = base + h
                k = h // 8
                if mode == "conv":
                    if h:
                        pe.wait_ge(S("masked"), h)
                    bank = SC
                else:
                    bank = SMs[n % NB]
                    bank_free(n)
                if mode != "near" or h < 8:
                    pe.wait_ge(S("q_ready"), n + 1 - stacks)
                stacked = mode == "near" and h >= 8
                if mode == "near" and h == 0:
                    pe.wait_ge(S("q_edges"), 2)
                    pe.wait_ge(S("kc_ready0"), 6)
                if stacked and h == 8:
                    pe.wait_ge(S("q_stacked"), 16 * 6)
                    pe.wait_ge(S("k_stacked"), 16 * 3)
                for t in range(TT):
                    o = t * T
                    cols = P if half and t == 0 else T
                    if mode == "near" and not stacked:
                        for a in range(3):
                            ins = pe.matmul(bank[:, o:o + cols], QM[:, h, t * P + a:t * P + a + P], KC[:, k, a, 0:cols],
                                            start=a == 0, stop=t == 1 and a == 2)
                            if a == 0 and t == 1:
                                pe.matmul(bank[:, o + P:o + T], identb[:], masks[:, 1, 0, 0:P], start=False, stop=False,
                                          skip_group_check=True)
                    else:
                        if stacked:
                            q, keys = QS[:, h - 8, t * P:(t + 1) * P], KS[:, h // 2 - 4, 0:cols]
                        else:
                            q, keys = QM[:, h, t * P + 1:t * P + 1 + P], KFd[:, k, 0:cols]
                        ins = pe.matmul(bank[:, o:o + cols], q, keys, start=True, stop=mode == "conv")
                    if half and t == 0:
                        ins = pe.matmul(bank[:, 0:P], identb[:], masks[:, 1, 0, 0:P], start=False, stop=True)
                        if h < NB:
                            ins = pe.matmul(bank[:, P:T], identb[:], masks[:, 1, 0, P:T], start=True, stop=True)
                    elif half and (stacked or mode != "near"):
                        ins = pe.matmul(bank[:, o:o + T], identb[:], masks[:, 1, 1, :], start=False, stop=True)
                    elif mode == "count":
                        ins = pe.matmul(bank[:, o:o + T], identb[:], masks[:, 0, t, :], start=False, stop=True)
                ins.then_inc(S("raw_ready" if mode == "conv" else "scores_ready"), 1)

            def conv(h):
                n = base + h
                bank_free(n)
                pe.wait_ge(S("masked"), h + 1)
                pe.wait_ge(S("band_ready"), h + 1)
                a, bank, bd = AM[h % 2], SMs[n % NB], band[h % 2]
                for t in range(TT):
                    o = t * T
                    for s in range(3):
                        pe.matmul(bank[:, o:o + T], bd[:, s, :], a[:, t, s:s + T], start=s == 0, stop=False)
                    for s in range(3):
                        if t == 0:
                            pe.matmul(bank[96:128, o:o + T], haloU[0:1, h, s, :], a[0:1, 1, s:s + T],
                                      start=False, stop=False, skip_group_check=True)
                        else:
                            pe.matmul(bank[0:32, o:o + T], haloD[96:128, h, s, :], a[96:128, 0, s:s + T],
                                      start=False, stop=False, skip_group_check=True)
                    ins = pe.matmul(bank[:, o:o + T], identb[:], masks[:, 0, t, :], start=False, stop=True)
                ins.then_inc(S("scores_ready"), 1)

            def flip_probs(h):
                n = base + h
                if mode == "count":
                    pe.wait_ge(S("weighted"), 2 * (h + 1))
                else:
                    pe.wait_ge(S("exp_done"), 2 * (n + 1))
                if n >= 2:
                    pe.wait_ge(S("probs_moved"), n - 1)
                bank = PT[n % 2]
                for k in range(TT):
                    for t in range(k if half else 0, TT):
                        o = k * T + (0 if half and k else t) * P
                        ins = pe.transpose(bank[:, o:o + P], PR[n % 2][:, t, k * P:(k + 1) * P], ident)
                ins.then_inc(S("probs_flipped"), 1)

            def values(h):
                n = base + h
                g = h // 8
                pe.wait_ge(S("probs_moved"), n + 1)
                if h == 0 and inst:
                    pe.wait_ge(oa_free, inst)
                order = (1, 0) if half and h % 8 == 7 else (0, 1)
                for i, k in enumerate(order):
                    lo = P if half and k else 0
                    src = PS[n % 2][:, 1, 0:P] if lo else PS[n % 2][:, k, :]
                    ins = pe.matmul(OA[:, g * T + lo:(g + 1) * T], VM[:, k, g, (h % 8) * P:(h % 8 + 1) * P], src,
                                    start=h % 8 == 0 and i == 0, stop=h % 8 == 7 and i == 1, skip_group_check=lo > 0)
                ins.then_inc(S("values_done"), 1)

            for s in range(H + 3):
                if s < H:
                    scores(s)
                if mode == "conv" and 1 <= s <= H:
                    conv(s - 1)
                if 2 <= s < H + 2:
                    flip_probs(s - 2)
                if s >= 3:
                    values(s - 3)
                if between is not None:
                    between(s)

        def scale_pe(pe, ring, inst):
            pe.wait_ge(S("rinv_ready"), inst + 1)
            bank = ring.claim(pe)
            for t in range(TT):
                ins = pe.transpose(bank[0:H, t * P:(t + 1) * P], rinv[:, t, :], ident)
            ring.fill(ins)
            ring.moved(pe)
            bank = ring.claim(pe)
            for k in range(KT):
                ins = pe.matmul(bank[:, k * T:(k + 1) * T], k3(c("heads_on"), KT)[0:H, k, :], rT[:], start=True, stop=True)
            ring.fill(ins)

        def move_probs(eng, st, mode, n):
            eng.wait_ge(S("probs_flipped"), n + 1)
            if n >= 2:
                eng.wait_ge(S("values_done"), n - 1)
            if causal_like(mode):
                dst, src = PS[n % 2][:].rearrange("p k t -> p (k t)")[:, 0:3 * P], PT[n % 2][:, 0:3 * P]
            else:
                dst, src = PS[n % 2][:], two(PT[n % 2])
            ins = eng.tensor_copy(dst, src) if st is not None else eng.activation(dst, src, ACT.Copy)
            if st is not None:
                st.post(ins, S("probs_moved"))
            else:
                ins.then_inc(S("probs_moved"), 1)

        def attention_act(act, mode, inst, ready=None, aside=None):
            NB = n_banks(mode)
            half = causal_like(mode)
            ready = inst + 1 if ready is None else ready
            if ready:
                act.wait_ge(S("qk_ready"), ready)
            for h in range(8):
                mask_q(act, h)
                if aside is not None and h in (3, 5, 7):
                    next(aside)
                if mode == "near" and h == 1:
                    act.wait_ge(S("kcol_ready"), 2)
                    for a in range(3):
                        act.activation(KC[:, 0, a, :], KF[:, 0, 0:T], ACT.Copy,
                                       scale=kcol[:, 0, 3 * a:3 * a + 1]).then_inc(S("first_taps"), 1)
            for s in range(H + 2):
                if s >= 2 and act_moves(mode):
                    move_probs(act, None, mode, inst * H + s - 2)
                if s < H:
                    h = s
                    n = inst * H + h
                    act.wait_ge(S("max_ready"), n + 1)
                    if n >= 2:
                        act.wait_ge(S("probs_flipped"), n - 1)
                    for t in range(TT):
                        cols = P if half and t == 0 else T
                        dst, src = PR[n % 2][:, t, 0:cols], SMs[n % NB][:, t * T:t * T + cols]
                        if mode == "count":
                            ins = act.activation(dst, src, ACT.Exp, bias=negmax[:, h, t:t + 1])
                        else:
                            ins = act.activation(dst, src, ACT.Exp, bias=negmax[:, h, t:t + 1], accum_out=rsum[:, t, h:h + 1])
                        ins.then_inc(S("exp_done"), 1)
                if s < 8 and mode != "near":
                    mask_q(act, 8 + s, "head1" if mode == "conv" else "headq")
            act.wait_ge(S("values_done"), (inst + 1) * H)
            act.activation(YT[:], two(OA), ACT.Copy).then_inc(oa_free, 1)

        def act_moves(mode):
            return mode != "conv"

        def attention_dve(dve, st, mode, inst, counts=None, between=None):
            base = inst * H
            NB = n_banks(mode)

            def mask_scores(h):
                if h >= 2:
                    dve.wait_ge(S("scores_ready"), base + h - 1)
                dve.wait_ge(S("raw_ready"), h + 1)
                st.post(dve.tensor_tensor(AM[h % 2][:, :, 1:T + 1], two(SC), notmask[:], ALU.mult), S("masked"))

            def near_diagonals(h):
                n = base + h
                dve.wait_ge(S("scores_ready"), n + 1)
                for w, d in (("near0", diag1), ("near1", diag0)):
                    for t in range(TT):
                        lo = 1 - t
                        blk = SMs[n % NB][:, t * (T + P) - t:t * (T + P) + P]
                        st.post(dve.scalar_tensor_tensor(blk, c(w)[:, lo:P + 1], d[:, t, h:h + 1], blk, ALU.mult, ALU.add))
                    st.settle()

            def row_max(h):
                n = base + h
                dve.wait_ge(S("scores_ready"), n + 1)
                st.post(dve.tensor_reduce(negmax[:, h, :], two(SMs[n % NB]), AX.X, ALU.max, negate=True), S("max_ready"))

            def weight(h):
                n = base + h
                dve.wait_ge(S("exp_done"), 2 * (n + 1))
                for t in range(TT):
                    st.post(dve.scalar_tensor_tensor(PR[n % 2][:, t, :], PR[n % 2][:, t, :], 1.0, counts[:, t, :],
                                                     ALU.mult, ALU.mult, accum_out=rsum[:, t, h:h + 1]), S("weighted"))

            for s in range(H + 3):
                if mode == "conv" and s < H:
                    mask_scores(s)
                if mode == "near" and s < H:
                    near_diagonals(s)
                lag = 1 if mode == "conv" else 0
                if lag <= s < H + lag:
                    row_max(s - lag)
                if between is not None:
                    between(s)
                if mode == "count" and 1 <= s <= H:
                    weight(s - 1)
                if not act_moves(mode) and 2 <= s < H + 2:
                    move_probs(dve, st, mode, base + s - 2)
            dve.wait_ge(S("exp_done"), 2 * (base + H))
            st.settle()
            st.post(dve.reciprocal(rinv[:], rsum[:]), S("rinv_ready"))

        def scale_dve(dve, st, ring, inst):
            bank = ring.take(dve)
            ring.release(st, dve.tensor_copy(rT[:], bank[0:H, 0:T]))
            bank = ring.take(dve)
            dve.wait_ge(oa_free, inst + 1)
            ring.release(st, dve.tensor_tensor(YT[:], two(bank), YT[:], ALU.mult))

        def clear_block():
            sems = list(names.values())
            with nc.Block() as block:
                @block.sync
                def _(sp):
                    for s in sems[0::5]:
                        sp.sem_clear(s)

                @block.scalar
                def _(act):
                    for s in sems[1::5]:
                        act.sem_clear(s)

                @block.vector
                def _(dve):
                    for s in sems[2::5]:
                        dve.sem_clear(s)

                @block.gpsimd
                def _(pool):
                    for s in sems[3::5]:
                        pool.sem_clear(s)

                @block.tensor
                def _(pe):
                    for s in sems[4::5]:
                        pe.sem_clear(s)

        with nc.Block() as block:
            @block.sync
            def _(sp):
                sp.dma_start(const_sb[:], const).then_inc(S("const_in"), 16)
                sp.dma_start(mask_in, negm).then_inc(S("const_in"), 16)
                sp.dma_start(arena[:, HIST0:HIST0 + HIST_N], hist).then_inc(S("hist_in"), 16)
                sp.wait_ge(S("flag_ready"), 1)

            @block.vector
            def _(dve):
                st = Steps(dve, S("dve"))
                st.post(dve.memset(ones[:], 1.0))
                st.post(dve.memset(XT[:], 0.0))
                st.post(dve.memset(haloD[:], 0.0))
                st.post(dve.memset(QF[:], 0.0))
                st.post(dve.memset(KF[:], 0.0))
                for i in range(2):
                    st.post(dve.memset(AM[i][:], 0.0))
                dve.wait_ge(S("const_in"), 32)
                st.post(dve.tensor_copy(identb[:], ident))
                st.post(dve.tensor_scalar(masks[:, 0], mask_in, NEG, None, ALU.mult))
                st.post(dve.tensor_scalar(masks[:, 1], k3(c("causal"), TT), NEG, None, ALU.mult))
                st.post(dve.tensor_scalar(notmask[:], mask_in, -1.0, 1.0, ALU.mult, ALU.add))
                dve.wait_ge(S("hist_in"), 16)
                st.settle()
                st.post(dve.tensor_copy(X[:], mask_in))
                st.settle()
                st.post(dve.tensor_tensor(X[:], X[:], k3(c("causal"), TT), ALU.not_equal))
                st.settle()
                st.post(dve.tensor_reduce(small[:, 0:1], X[:], AX.XY, ALU.add), S("differ_rows"))
                dve.wait_ge(pj_full[0], 1)
                st.post(dve.tensor_copy(flag[:], PJ[0][0:1, 0:1]), S("flag_ready"))

            @block.tensor
            def _(pe):
                pe.wait_ge(S("differ_rows"), 1)
                pe.matmul(PJ[0][0:1, 0:1], small[:, 0:1], ones[:, 0:1], start=True, stop=True).then_inc(pj_full[0], 1)
        clear_block()

        scratch = (big, VM[:].rearrange("p t k n -> p (t k n)"))
        EH = [m[:, 0:1024].rearrange("p (t n) -> p t n", t=TT) for m in scratch]
        EG = [m[:, 1024:2048].rearrange("p (t n) -> p t n", t=TT) for m in scratch]
        EHT = [m[:, 2048:3072].rearrange("p (k t) -> p k t", k=4) for m in scratch]
        A1 = [m[:, 3072:3328] for m in scratch]
        awr = [m[0:1, 3328:3584] for m in scratch]
        awc = [small[:, 2 * i:2 * i + 2] for i in range(2)]
        awsum = [small[0:1, 8 + 4 * i:12 + 4 * i] for i in range(2)]
        hist_x = [CT[:], Z[:]]
        two_of = range(2)
        PARTS = B // 2
        PART = HIST0 // PARTS
        with nc.Fori(0, B // 2) as pair:
            with nc.Block() as block:
                ring = Ring(PJ, pj_full, pj_free)

                @block.sync
                def _(sp):
                    for i in two_of:
                        sp.dma_start(hist_x[i], ctxT[0:B].rearrange("(n i) p k t -> n i p k t", i=2)[bass.ds(pair, 1), i].rearrange("o p k t -> (o p) k t")).then_inc(S(f"ctx_in{i}"), 16)
                    sp.dma_start(arena[:, 0:PARTS * PART].rearrange("p (c n) -> p c n", c=PARTS)[:, bass.ds(pair, 1), :],
                                 lay0[:, 0:PARTS * PART].rearrange("p (c n) -> p c n", c=PARTS)[:, bass.ds(pair, 1), :]
                                 ).then_inc(S("lay0_in"), 16)
                    for i in two_of:
                        sp.wait_ge(S(f"ctx_in{i}"), 16)
                    sp.wait_ge(S("lay0_in"), 16)

                @block.tensor
                def _(pe):
                    W = k3(hist_w("hist_W"), KT)
                    for i in two_of:
                        pe.wait_ge(S(f"ctx_in{i}"), 16)
                        for t in range(TT):
                            bank = ring.claim(pe)
                            for k in range(KT):
                                ins = pe.matmul(bank[:], hist_x[i][:, k, t * P:(t + 1) * P], W[:, k, :], start=k == 0, stop=k == 1)
                            ring.fill(ins)
                    for i in two_of:
                        pe.wait_ge(S("gelu_done"), TT * (i + 1))
                        for c2 in range(2):
                            bank = ring.claim(pe)
                            for cc in range(2):
                                for t in range(TT):
                                    f = (2 * c2 + cc) * P
                                    ins = pe.transpose(bank[:, cc * T + t * P:cc * T + (t + 1) * P], EG[i][:, t, f:f + P], ident)
                            ring.fill(ins)
                        ring.moved(pe)
                        for k in range(4):
                            ins = pe.matmul(SM[i][:, 0:T], k3(hist_w("ctx_W1"), 4)[:, k, :], EHT[i][:, k, :],
                                            start=k == 0, stop=k == 3)
                        ins.then_inc(S("a1_full"), 1)
                    for i in two_of:
                        pe.wait_ge(S("gelu_done"), 2 * TT + 1 + i)
                        bank = ring.claim(pe)
                        ring.fill(pe.matmul(bank[0:1, 0:T], hist_w("ctx_W2"), A1[i], start=True, stop=True))
                    for i in two_of:
                        pe.wait_ge(S("aw_ready"), i + 1)
                        bank = ring.claim(pe)
                        for t in range(TT):
                            ins = pe.matmul(bank[:, t:t + 1], awr[i][:, t * P:(t + 1) * P], ones[0:1, 0:1], start=True, stop=True)
                        ring.fill(ins)
                    ring.moved(pe)
                    for i in two_of:
                        bank = ring.claim(pe)
                        for f in range(4):
                            for t in range(TT):
                                ins = pe.matmul(bank[:, f:f + 1], EG[i][:, t, f * P:(f + 1) * P], awc[i][:, t:t + 1],
                                                start=t == 0, stop=t == 1)
                        ring.fill(ins)

                @block.vector
                def _(dve):
                    st = Steps(dve, S("dve"))
                    for i in two_of:
                        for t in range(TT):
                            bank = ring.take(dve)
                            ring.release(st, dve.tensor_tensor(EH[i][:, t, :], bank[:], hist_w("hist_b"), ALU.add))
                    for i in two_of:
                        st.settle()
                        layernorm(dve, st, EH[i], EH[i], i + 1, "eh_norm")
                        st.settle()
                        for t in range(TT):
                            st.post(dve.tensor_tensor(EH[i][:, t, :], EH[i][:, t, :], hist_w("hist_g"), ALU.mult))
                        st.settle()
                        for t in range(TT):
                            st.post(dve.tensor_tensor(EH[i][:, t, :], EH[i][:, t, :], hist_w("hist_lb"), ALU.add), S("eh_ready"))
                    for i in two_of:
                        for c2 in range(2):
                            move(dve, st, ring, EHT[i][:, 2 * c2:2 * c2 + 2, :])
                    for i in two_of:
                        bank = ring.take(dve)
                        ring.release(st, dve.tensor_scalar(awr[i], bank[0:1, 0:T], hist_w("ctx_b2")[0:1, :], None, ALU.add))
                    st.settle()
                    for i in two_of:
                        st.post(dve.tensor_reduce(awsum[i][:, 0:1], awr[i], AX.X, ALU.max, negate=True), S("awmax"))
                    for i in two_of:
                        dve.wait_ge(S("awexp"), i + 1)
                        st.post(dve.reciprocal(awsum[i][:, 2:3], awsum[i][:, 1:2]))
                        st.settle()
                        st.post(dve.tensor_scalar(awr[i], awr[i], awsum[i][:, 2:3], None, ALU.mult), S("aw_ready"))
                    for i in two_of:
                        bank = ring.take(dve)
                        ring.release(st, dve.tensor_copy(awc[i], bank[:, 0:2]))
                    for i in two_of:
                        bank = ring.take(dve)
                        ring.release(st, dve.tensor_copy(CC[:].rearrange("p (n i) f -> p n i f", i=2)[:, bass.ds(pair, 1), i, :].rearrange("p o f -> p (o f)"), bank[:, 0:4]))
                    st.settle()

                @block.gpsimd
                def _(pool):
                    for n in range(1, 3):
                        root_pool(pool, n)

                @block.scalar
                def _(act):
                    for i in two_of:
                        for t in range(TT):
                            act.wait_ge(S("eh_ready"), TT * i + t + 1)
                            act.activation(EG[i][:, t, :], EH[i][:, t, :], ACT.Gelu).then_inc(S("gelu_done"), 1)
                    for i in two_of:
                        act.wait_ge(S("a1_full"), i + 1)
                        act.activation(A1[i], SM[i][:, 0:T], ACT.Gelu, bias=hist_w("ctx_b1")).then_inc(S("gelu_done"), 1)
                    for i in two_of:
                        act.wait_ge(S("awmax"), i + 1)
                        act.activation(awr[i], awr[i], ACT.Exp, bias=awsum[i][:, 0:1],
                                       accum_out=awsum[i][:, 1:2]).then_inc(S("awexp"), 1)
            clear_block()

        KP = big[0:B, 0:256]
        KG = big[0:B, 256:512]
        KPT = big[:, 512:528].rearrange("p (k b) -> p k b", k=2)
        K2 = big[0:B, 528:672]
        K2v = K2.rearrange("b (h n) -> b h n", n=9)
        KH = big[0:H, 700:772].rearrange("h (b n) -> h b n", b=B)
        with nc.Block() as block:
            ring = Ring(PJ, pj_full, pj_free)

            @block.tensor
            def _(pe):
                bank = ring.claim(pe)
                for f in range(4):
                    ins = pe.matmul(bank[0:B, 0:256], CC[:, :, f], k3(hist_w("kg_W1"), 4)[:, f, :], start=f == 0, stop=f == 3)
                ring.fill(ins)
                pe.wait_ge(S("gelu_done"), 1)
                bank = ring.claim(pe)
                for k in range(2):
                    ins = pe.transpose(bank[:, k * B:(k + 1) * B], KG[:, k * P:(k + 1) * P], ident[0:B, 0:B])
                ring.fill(ins)
                ring.moved(pe)
                bank = ring.claim(pe)
                for k in range(2):
                    ins = pe.matmul(bank[0:B, 0:144], KPT[:, k, :], k3(hist_w("kg_W2"), 2)[:, k, :], start=k == 0, stop=k == 1)
                ring.fill(ins)
                pe.wait_ge(S("k_in"), 32)
                bank = ring.claim(pe)
                for k in range(KT):
                    ins = pe.matmul(bank[:, k * 72:(k + 1) * 72], k3(c("heads_on"), KT)[0:H, k, :],
                                    KH.rearrange("h b n -> h (b n)"), start=True, stop=True)
                ring.fill(ins)

            @block.vector
            def _(dve):
                st = Steps(dve, S("dve"))
                bank = ring.take(dve)
                ring.release(st, dve.tensor_tensor(KP, bank[0:B, 0:256], hist_w("kg_b1")[0:B, :], ALU.add))
                st.post(dve.memset(var[:], 1.0))
                st.settle()
                st.post(dve.bn_stats(stats[0:B, 0, :], KP))
                st.settle()
                st.post(dve.bn_aggr(mv[0:B, 0, :], stats[0:B, 0, :]))
                st.settle()
                st.post(dve.tensor_scalar(var[0:B, 0:1], mv[0:B, 0, 1:2], LN_EPS, None, ALU.add), S("var_ready"))
                dve.wait_ge(S("rstd_ready"), 1)
                st.post(dve.tensor_scalar(KP, KP, mv[0:B, 0, 0:1], rstd[0:B, 0:1], ALU.subtract, ALU.mult))
                st.settle()
                st.post(dve.tensor_tensor(KP, KP, hist_w("kg_g")[0:B, :], ALU.mult))
                st.settle()
                st.post(dve.tensor_tensor(KP, KP, hist_w("kg_lb")[0:B, :], ALU.add), S("kp_ready"))
                bank = ring.take(dve)
                ring.release(st, dve.tensor_copy(KPT, bank[:, 0:2 * B].rearrange("p (k b) -> p k b", k=2)))
                bank = ring.take(dve)
                ring.release(st, dve.tensor_tensor(K2, bank[0:B, 0:144], hist_w("kg_b2")[0:B, :], ALU.add))
                st.settle()
                st.post(dve.tensor_reduce(small[0:B, 16:32], K2v, AX.X, ALU.max))
                st.settle()
                st.post(dve.tensor_tensor(K2v, K2v, small[0:B, 16:32].unsqueeze(2).broadcast_to([B, H, 9]), ALU.subtract),
                        S("k_shift"))
                dve.wait_ge(S("k_exp"), 1)
                st.post(dve.tensor_reduce(small[0:B, 32:48], K2v, AX.X, ALU.add))
                st.settle()
                st.post(dve.reciprocal(small[0:B, 48:64], small[0:B, 32:48]))
                st.settle()
                st.post(dve.tensor_tensor(K2v, K2v, small[0:B, 48:64].unsqueeze(2).broadcast_to([B, H, 9]), ALU.mult),
                        S("k_ready"))
                bank = ring.take(dve)
                ring.release(st, dve.tensor_copy(kcols[:], bank[:, 0:144].rearrange("p (k n) -> p k n", k=KT)))
                st.settle()

            @block.gpsimd
            def _(pool):
                root_pool(pool, 1)

            @block.scalar
            def _(act):
                act.wait_ge(S("kp_ready"), 1)
                act.activation(KG, KP, ACT.Gelu).then_inc(S("gelu_done"), 1)
                act.wait_ge(S("k_shift"), 1)
                act.activation(K2, K2, ACT.Exp).then_inc(S("k_exp"), 1)

            @block.sync
            def _(sp):
                sp.wait_ge(S("k_ready"), 1)
                sp.dma_start(kern_d, K2).then_inc(S("k_out"), 16)
                sp.wait_ge(S("k_out"), 16)
                sp.dma_start(KB[:], kern_d.rearrange("b n -> (b n)").unsqueeze(0).broadcast_to([P, B * 144])).then_inc(S("k_in"), 16)
                sp.dma_start(KH, kern_d.rearrange("b (h n) -> h b n", n=9)).then_inc(S("k_in"), 16)
                sp.wait_ge(S("k_in"), 32)
        clear_block()

        with nc.Block() as block:
            @block.sync
            def _(sp):
                sp.dma_start(arena[:, PARTS * PART:LAY0_N], lay0[:, PARTS * PART:LAY0_N]).then_inc(S("lay0_in"), 16)
                sp.dma_start(Xin[:], x[0]).then_inc(S("x_in"), 16)
                sp.wait_ge(S("x_in"), 16)
                sp.wait_ge(S("lay0_in"), 16)

            @block.vector
            def _(dve):
                dve.memset(OUT[:], 0.0)
                dve.memset(VM[:], 0.0)
        clear_block()

        HTv = [big[:, i * MT * T:(i + 1) * MT * T].rearrange("p (m t) -> p m t", m=MT) for i in range(2)]
        lat = Z[:, :, 0:LAT]
        FS = X2
        GS = btmp[:].rearrange("p a b -> p (a b)")[0:H, 0:T]
        onehot = small[:, 64:64 + 8].rearrange("p (t e) -> p t e", t=2)
        left = small[:, 72:80].rearrange("p (t e) -> p t e", t=2)
        NP = [AM[0][:, :, 0:T], AM[1][:, :, 0:T], PS[0][:]]

        def features_pe(pe, ring):
            flip(pe, ring, OUT)
            yield
            ring.moved(pe)
            bank = ring.claim(pe)
            for k in range(KT):
                pe.matmul(bank[0:64, 0:T], k3(w0("w1w"), 2)[:, k, :], XT[:, k, 0:T], start=k == 0, stop=k == 1)
            for k in range(KT):
                pe.matmul(bank[64:128, 0:T], k3(w0("w2w"), 2)[:, k, :], XT[:, k, 1:T + 1], start=k == 0, stop=k == 1)
            for k in range(KT):
                ins = pe.matmul(bank[:, T:2 * T], k3(w0("rw"), 2)[:, k, :], XT[:, k, 1:T + 1], start=k == 0, stop=k == 1)
            ring.fill(ins)
            yield
            bank = ring.claim(pe)
            for k in range(KT):
                ins = pe.matmul(bank[0:H, 0:T], k3(w0("memg"), 2)[:, k, :], XT[:, k, 1:T + 1], start=k == 0, stop=k == 1)
            ring.fill(ins)
            yield

        def features_act(act, ring):
            sa = Steps(act, S("act"))
            bank = ring.take(act)
            ring.release(sa, act.activation(XT[:, :, 1:T + 1], two(bank), ACT.Copy))
            yield
            bank = ring.take(act)
            ring.release(sa, act.activation(FS[:], two(bank), ACT.Copy))
            yield
            bank = ring.take(act)
            ring.release(sa, act.activation(GS, bank[0:H, 0:T], ACT.Copy))
            yield

        def store_features(sp, b):
            sp.wait_ge(next_free[1], 1)
            sp.wait_ge(next_free[0], 2)
            for m in range(4):
                sp.dma_start(feat[b, m].rearrange("o q t -> (o q) t"),
                             FS[64 * (m % 2):64 * (m % 2) + 64, m // 2, :]).then_inc(S("feat_out"), 16)
            sp.dma_start(gate_d[b].rearrange("o h t -> (o h) t"), GS).then_inc(S("feat_out"), 16)

        def first_sublayer_pe(pe, ring):
            bank = ring.claim(pe)
            for k in range(KT):
                for t in range(TT):
                    ins = pe.matmul(bank[:, k:k + 1], Xin[:, t, k * P:(k + 1) * P], ones[:, 0:1], start=t == 0,
                                    stop=t == TT - 1)
            ring.fill(ins)
            yield
            ring.moved(pe)
            bank = ring.claim(pe)
            for m in range(2):
                for k in range(KT):
                    ins = pe.matmul(bank[:, m:m + 1], k3(w0("wv"), 2)[:, k, m * P:(m + 1) * P], small[:, k:k + 1],
                                    start=k == 0, stop=k == 1)
            ring.fill(ins)
            yield
            ring.moved(pe)
            bank = ring.claim(pe)
            for k in range(KT):
                ins = pe.matmul(bank[:, 0:D], Z[:, k, 0:P], k3(w0("wo"), 2)[:, k, :], start=k == 0, stop=k == 1)
            ring.fill(ins)
            yield

        def first_sublayer_dve(dve, st, ring, n):
            bank = ring.take(dve)
            ring.release(st, dve.tensor_copy(small[:, 0:2], bank[:, 0:2]))
            yield
            bank = ring.take(dve)
            ring.release(st, dve.tensor_copy(Z[:, :, 0:P], bank[:, 0:2].unsqueeze(2).broadcast_to([P, 2, P])))
            yield
            bank = ring.take(dve)
            ring.release(st, dve.tensor_tensor(X[:], bank[:, 0:D].unsqueeze(1).broadcast_to([P, TT, D]), Xin[:], ALU.add))
            st.settle()
            st.post(dve.memset(small[:, 4:5], 0.0), S("x_used"))
            layernorm(dve, st, X, X, n, "x_ready")
            st.settle()
            yield

        with nc.Block() as block:
            ring = Ring(PJ, pj_full, pj_free)

            @block.sync
            def _(sp):
                sp.wait_ge(S("x_used"), 1)
                sp.dma_start(Xin[:], x[1]).then_inc(S("x_in"), 16)
                sp.wait_ge(S("x_in"), 16)

            @block.tensor
            def _(pe):
                for _ in first_sublayer_pe(pe, ring):
                    pass

            @block.vector
            def _(dve):
                for _ in first_sublayer_dve(dve, Steps(dve, S("dve")), ring, 1):
                    pass

            @block.gpsimd
            def _(pool):
                root_pool(pool, 1)
        clear_block()

        def qkv_pe(pe, ring):
            flip(pe, ring, X)
            ring.moved(pe)
            W = k3(w0("xqkv"), 2)
            for i in range(2):
                bank = ring.claim(pe)
                ring.fill(columns(pe, bank, W, XT[:, :, 1:T + 1], i * D))
            rows(pe, ring, XT[:, :, 1:T + 1], W, 2 * D, 3 * D)

        def qkv_act(act, ring):
            sa = Steps(act, S("act"))
            bank = ring.take(act)
            ring.release(sa, act.activation(XT[:, :, 1:T + 1], two(bank), ACT.Copy))
            for dst in (QF, KF):
                bank = ring.take(act)
                if dst is QF:
                    sa.post(act.activation(QF[:, 0, 1:T + 1], bank[:, 0:T], ACT.Copy))
                    ring.release(sa, act.activation(QF[:, 1, 1:T + 1], bank[:, T:2 * T], ACT.Copy, scale=SCALE))
                else:
                    ring.release(sa, act.activation(dst[:, :, 1:T + 1], two(bank), ACT.Copy))
            bank = ring.take(act)
            for t in range(TT):
                ins = act.activation(vm_diag(t), bank[:, t * D:(t + 1) * D].rearrange("p (k h d) -> p k h d", k=KT, h=8), ACT.Copy)
                ring.release(sa, ins) if t else sa.post(ins)

        with nc.Block() as block:
            qkv_ring = Ring(SM, qkv_full, qkv_free)

            @block.tensor
            def _(pe):
                qkv_pe(pe, qkv_ring)

            @block.scalar
            def _(act):
                qkv_act(act, qkv_ring)
        clear_block()

        def layer0(mode):
            with nc.Fori(0, B) as b:
                with nc.Block() as block:
                    ring = Ring(PJ, pj_full, pj_free)
                    ahead = Ring(PT, next_full, next_free)
                    qkv_ring = Ring(SM, qkv_full, qkv_free)

                    @block.sync
                    def _(sp):
                        sp.dma_start(x4_d[bass.ds(b, 1)].rearrange("o p t d -> (o p) t d"), OUT[:]).then_inc(S("feat_out"), 16)
                        store_features(sp, bass.ds(b, 1))
                        if mode == "near":
                            sp.dma_start(q_d, QF[:, 1, :]).then_inc(S("q_out"), 16)
                            sp.wait_ge(S("q_out"), 16)
                            sp.wait_ge(S("q_cleared"), 1)
                            for a in range(3):
                                src = q_d[:, a:a + T].rearrange("(r q d) c -> q d r c", r=4, q=2)
                                for q in range(2):
                                    sp.dma_start(QS[32 * a + HD * q:32 * a + HD * (q + 1), q:8:2, :],
                                                 src[q]).then_inc(S("q_stacked"), 16)
                            sp.wait_ge(S("kc_ready1"), 9)
                            sp.dma_start(k_d, KC[:, 1]).then_inc(S("k_out"), 16)
                            sp.wait_ge(S("k_out"), 16)
                            for a in range(3):
                                sp.dma_start(KS[32 * a:32 * (a + 1), :, :],
                                             k_d[:, a, :].rearrange("(r e) c -> e r c", r=4)).then_inc(S("k_stacked"), 16)
                            sp.wait_ge(S("q_stacked"), 16 * 6)
                            sp.wait_ge(S("k_stacked"), 16 * 3)
                        sp.wait_ge(S("x_used"), 1)
                        sp.dma_start(Xin[:], x[bass.ds(b + 2, 1)].rearrange("o p t d -> (o p) t d")).then_inc(S("x_in"), 16)
                        sp.wait_ge(S("feat_out"), 96)
                        sp.wait_ge(S("x_in"), 16)

                    @block.tensor
                    def _(pe):
                        steps = features_pe(pe, ahead)
                        next(steps)
                        if mode == "near":
                            pe.wait_ge(S("products"), 3)
                            bank = ring.claim(pe)
                            for t in range(TT):
                                for j in range(3):
                                    for k in range(KT):
                                        o = (t * 3 + j) * H + k * 8
                                        ins = pe.matmul(bank[:, o:o + 8], NP[j][:, k, t * P:(t + 1) * P], c("head1"),
                                                        start=True, stop=True)
                            ring.fill(ins)
                        next(steps)
                        next(steps)
                        ring.moved(pe)
                        ahead.moved(pe)
                        attention_pe(pe, mode, 0, KF[:, :, 1:T + 1])
                        scale_pe(pe, ring, 0)
                        pe.wait_ge(S("exp_done"), 2 * H)
                        pe.wait_ge(S("biased"), 1)
                        residual(pe, Y[:])
                        ring.moved(pe)
                        add_rows(pe, YT, k3(w0("xproj"), 2))
                        keep_clock(pe, 11)
                        pe.wait_ge(S("xn_ready"), 2)
                        flip(pe, ring, X)
                        ring.moved(pe)
                        rows(pe, ring, XT[:, :, 1:T + 1], k3(w0("mdkv"), 2), 0, LAT)
                        for w in ("mq", "mqs"):
                            bank = ring.claim(pe)
                            ring.fill(columns(pe, bank, k3(w0(w), 2), XT[:, :, 1:T + 1]))
                        pe.wait_ge(S("lat_ready"), 2)
                        bank = ring.claim(pe)
                        for t in range(TT):
                            ins = pe.transpose(bank[:, t * P:(t + 1) * P], lat[:, t, :], ident)
                        ring.fill(ins)
                        ring.moved(pe)
                        for w in (w0("mukv")[:, 0:D], w0("muks")):
                            bank = ring.claim(pe)
                            for m in range(2):
                                ins = pe.matmul(bank[:, m * T:(m + 1) * T], w[:, m * P:(m + 1) * P], YT[:, 0, :],
                                                start=True, stop=True)
                            ring.fill(ins)
                        bank = ring.claim(pe)
                        for t in range(TT):
                            ins = pe.matmul(bank[:, t * D:(t + 1) * D], YT[:, 0, t * P:(t + 1) * P],
                                            w0("mukv")[:, D:2 * D], start=True, stop=True)
                        ring.fill(ins)
                        pe.wait_ge(S("k_rotated"), 1)
                        ring.moved(pe)
                        attention_pe(pe, "causal", 1, KF[:, :, 1:T + 1], first=mode)
                        scale_pe(pe, ring, 1)
                        pe.wait_ge(S("exp_done"), 4 * H)
                        pe.wait_ge(S("x_ready"), 2)
                        residual(pe, X2[:])
                        ring.moved(pe)
                        add_rows(pe, YT, k3(w0("mo"), 2))
                        pe.wait_ge(S("exp_done"), 4 * H)
                        keep_clock(pe, 8)
                        pe.wait_ge(S("xn_ready"), 4)
                        flip(pe, ring, Z)
                        ring.moved(pe)
                        bank = ring.claim(pe)
                        for t in range(TT):
                            for k in range(KT):
                                ins = pe.matmul(bank[:, t * NE:(t + 1) * NE], YT[:, k, t * P:(t + 1) * P],
                                                k3(w0("gate"), 2)[:, k, :], start=k == 0, stop=k == 1)
                        ring.fill(ins)
                        W = k3(w0("W1"), 2)
                        W2 = k3(w0("W2"), NE * MT)

                        def up(e):
                            for j in range(MT // 2):
                                u = e * (MT // 2) + j
                                if u < 3:
                                    pe.wait_ge(S("exp_done"), 4 * H)
                                    if u:
                                        pe.wait_ge(S("sum_used"), TT)
                                else:
                                    pe.wait_ge(S("relu_done"), 2 * (u - 2))
                                columns(pe, SMs[u % 3], W, YT, e * HID + 2 * j * P).then_inc(S("up_done"), 1)

                        def down(e):
                            pe.wait_ge(S("relu_done"), MT * (e + 1))
                            if e < 2:
                                pe.wait_ge(S("probs_moved"), 2 * H)
                            else:
                                pe.wait_ge(S("y_used"), e - 1)
                            for t in range(TT):
                                for m in range(MT):
                                    ins = pe.matmul(PT[e % 2][:, t * D:(t + 1) * D], HTv[e % 2][:, m, t * P:(t + 1) * P],
                                                    W2[:, e * MT + m, :], start=m == 0, stop=m == MT - 1)
                            ins.then_inc(S("down_done"), 1)

                        steps = first_sublayer_pe(pe, ring)
                        for e in range(NE + 1):
                            if e < NE:
                                up(e)
                            if e:
                                down(e - 1)
                            if e < 3:
                                next(steps)
                        pe.wait_ge(S("relu_done"), NE * MT)
                        pe.wait_ge(S("x_ready"), 4)
                        qkv_pe(pe, qkv_ring)

                    @block.vector
                    def _(dve):
                        st = Steps(dve, S("dve"))
                        def tap(k, a, j):
                            return dve.scalar_tensor_tensor(KC[:, k, a, :], KF[:, k, j:j + T],
                                                            kcol[:, k, 3 * a + j:3 * a + j + 1], KC[:, k, a, :],
                                                            ALU.mult, ALU.add)

                        def combine_high(a):
                            st.post(dve.tensor_scalar(KC[:, 1, a, :], KF[:, 1, 0:T], kcol[:, 1, 3 * a:3 * a + 1], None,
                                                      ALU.mult), S("kc_ready1"))
                            st.settle()
                            for j in range(1, 3):
                                st.post(tap(1, a, j), S("kc_ready1"))
                                st.settle()

                        if mode == "near":
                            for j, (i0, i1) in enumerate(((0, 1), (0, 2), (1, 2))):
                                st.post(dve.tensor_tensor(NP[j], QF[:, :, i0:i0 + T], KF[:, :, i1:i1 + T], ALU.mult), S("products"))
                            dve.wait_ge(S("kcol_ready"), 2)
                            dve.wait_ge(S("first_taps"), 3)
                            for j in range(1, 3):
                                for a in range(3):
                                    st.post(tap(0, a, j), S("kc_ready0"))
                                st.settle()
                        if mode == "near":
                            bank = ring.take(dve)
                            ring.release(st, dve.tensor_copy(kfac[:], bank[:, 0:TT * 3 * H].rearrange("p (t j h) -> p t j h", t=TT, j=3)))
                            st.settle()

                            def kf(a, j):
                                return kcur[:, :, a, j].unsqueeze(1).broadcast_to([P, TT, H])

                            st.post(dve.tensor_tensor(diag1[:], kfac[:, :, 0, :], kf(0, 2), ALU.mult))
                            st.post(dve.tensor_tensor(diag0[:], kfac[:, :, 0, :], kf(0, 1), ALU.mult))
                            st.post(dve.tensor_tensor(kfac[:, :, 1, :], kfac[:, :, 1, :], kf(0, 2), ALU.mult))
                            st.post(dve.tensor_tensor(kfac[:, :, 2, :], kfac[:, :, 2, :], kf(1, 2), ALU.mult))
                            st.settle()
                            st.post(dve.tensor_tensor(diag0[:], diag0[:], kfac[:, :, 1, :], ALU.add))
                            for k, f in ((0, -SCALE), (1, -1.0)):
                                st.post(dve.tensor_scalar(diag1[:, :, 8 * k:8 * k + 8], diag1[:, :, 8 * k:8 * k + 8], f, None,
                                                          ALU.mult))
                            st.settle()
                            st.post(dve.tensor_tensor(diag0[:], diag0[:], kfac[:, :, 2, :], ALU.add))
                            st.settle()
                            for k, f in ((0, -SCALE), (1, -1.0)):
                                st.post(dve.tensor_scalar(diag0[:, :, 8 * k:8 * k + 8], diag0[:, :, 8 * k:8 * k + 8], f, None,
                                                          ALU.mult))
                            st.settle()

                        def prepare(s):
                            if mode == "near" and s < 3:
                                combine_high(s)
                            if s == 4:
                                st.post(dve.tensor_tensor(Y[:], X[:], w0("proj_b").unsqueeze(1).broadcast_to([P, TT, D]), ALU.add),
                                        S("biased"))

                        attention_dve(dve, st, mode, 0, between=prepare)
                        scale_dve(dve, st, ring, 0)
                        dve.wait_ge(S("feat_out"), 96)
                        dve.wait_ge(S("sum_ready"), 1)
                        layernorm_rmsnorm(dve, st, X2, X, SUM, w0("norm1"), 1)
                        move(dve, st, ring, XT[:, :, 1:T + 1])

                        def rotate(dst):
                            for w, to in ((w0("cos"), dst[:, :, 1:T + 1]), (w0("sin"), Y[:])):
                                bank = ring.take(dve)
                                ring.release(st, dve.tensor_tensor(to, two(bank), w.unsqueeze(1).broadcast_to([P, KT, T]),
                                                                   ALU.mult))
                            st.settle()
                            return dve.tensor_tensor(dst[:, :, 1:T + 1], dst[:, :, 1:T + 1], Y[:], ALU.add)

                        bank = ring.take(dve)
                        ring.release(st, dve.tensor_copy(lat, two(bank, LAT)))
                        st.settle()
                        layernorm(dve, st, lat, lat, 2, "lat_norm")
                        st.settle()
                        for t in range(TT):
                            st.post(dve.tensor_tensor(lat[:, t, :], lat[:, t, :], w0("ln_g"), ALU.mult))
                        st.settle()
                        for t in range(TT):
                            st.post(dve.tensor_tensor(lat[:, t, :], lat[:, t, :], w0("ln_b"), ALU.add), S("lat_ready"))
                        st.settle()
                        st.post(rotate(QF), S("qk_ready"))
                        bank = ring.take(dve)
                        ring.release(st, dve.tensor_copy(YT[:, 0, :], bank[:, 0:T]))
                        st.settle()
                        st.post(rotate(KF), S("k_rotated"))
                        move_v(dve, st, ring)
                        attention_dve(dve, st, "causal", 1)
                        scale_dve(dve, st, ring, 1)
                        dve.wait_ge(S("sum_ready"), 2)
                        rmsnorm(dve, st, Z, SUM, w0("norm2"), 3, "xn_ready")
                        for t in range(TT):
                            st.post(dve.tensor_tensor(Y[:, t, :], SUM[t], X2[:, t, :], ALU.add), S("sum_used"))
                        move(dve, st, ring, YT[:])
                        lg = small[:, 80:88].rearrange("p (t e) -> p t e", t=2)
                        bank = ring.take(dve)
                        ring.release(st, dve.tensor_tensor(lg, two(bank, NE), w0("gate_b").unsqueeze(1).broadcast_to([P, TT, NE]),
                                                           ALU.add))
                        st.settle()
                        st.post(dve.tensor_reduce(small[:, 88:90], lg, AX.X, ALU.max))
                        st.settle()
                        st.post(dve.tensor_tensor(onehot, lg, small[:, 88:90].unsqueeze(2).broadcast_to([P, TT, NE]),
                                                  ALU.is_equal))
                        st.settle()
                        st.post(dve.tensor_scalar(left[:, :, 1], onehot[:, :, 0], -1.0, 1.0, ALU.mult, ALU.add))
                        st.settle()
                        for e in range(1, NE):
                            st.post(dve.tensor_tensor(onehot[:, :, e], onehot[:, :, e], left[:, :, e], ALU.mult))
                            st.settle()
                            if e < NE - 1:
                                st.post(dve.tensor_tensor(left[:, :, e + 1], left[:, :, e], onehot[:, :, e], ALU.subtract))
                                st.settle()
                        for e in range(NE):
                            for t in range(TT):
                                st.post(dve.scalar_tensor_tensor(Y[:, t, :], w0("b2")[:, e * D:(e + 1) * D], onehot[:, t, e:e + 1],
                                                                 Y[:, t, :], ALU.mult, ALU.add))
                            st.settle()
                        steps = first_sublayer_dve(dve, st, ring, 4)
                        for e in range(NE):
                            if e < 3:
                                next(steps)
                            dve.wait_ge(S("down_done"), e + 1)
                            for t in range(TT):
                                ins = dve.scalar_tensor_tensor(Y[:, t, :], PT[e % 2][:, t * D:(t + 1) * D], onehot[:, t, e:e + 1],
                                                               Y[:, t, :], ALU.mult, ALU.add)
                                st.post(ins, S("y_used") if t else None)
                            st.settle()
                        layernorm(dve, st, OUT, Y, 5, "x_ready")
                        st.settle()

                    @block.gpsimd
                    def _(pool):
                        ps = Steps(pool, S("pool"))
                        kb4 = KB[:].rearrange("p (b n) -> p b n", b=B)
                        ps.post(pool.tensor_copy(kcur[:].rearrange("p h a s -> p (h a s)"),
                                                 kb4[:, bass.ds(b, 1), :].rearrange("p o n -> p (o n)")), S("kcol_ready"))
                        kc4 = kcols[:].rearrange("p k (b n) -> p k b n", b=B)
                        ps.post(pool.tensor_copy(kcol[:], kc4[:, :, bass.ds(b, 1), :].rearrange("p k o n -> p k (o n)")),
                                S("kcol_ready"))
                        if mode == "near":
                            ps.post(pool.memset(QM[:, 0:8, 0:1], 0.0), S("q_edges"))
                            ps.post(pool.memset(QM[:, 0:8, T + 1:T + 2], 0.0), S("q_edges"))
                            ps.post(pool.memset(QS, 0.0), S("q_cleared"))
                        ps.settle()
                        if mode == "conv":
                            for src, dst, a in ((c("halo_up"), haloU, 2), (c("halo_dn"), haloD, 0)):
                                for h in range(H):
                                    ps.post(pool.tensor_tensor(dst[:, h], src.unsqueeze(1).broadcast_to([P, 3, 32]),
                                                               kcur[:, h, a, :].unsqueeze(2).broadcast_to([P, 3, 32]), ALU.mult))
                            ps.settle()
                        if mode == "conv":
                            pool.wait_ge(S("feat_out"), 96)
                            sh = k3(c("shift"), 3)
                            for h in range(H):
                                if h >= 2:
                                    pool.wait_ge(S("scores_ready"), h - 1)
                                for a in range(3):
                                    dst = band[h % 2] if a == 0 else btmp
                                    ps.post(pool.tensor_tensor(dst[:], sh[:, a, :].unsqueeze(1).broadcast_to([P, 3, P]),
                                                               kcur[:, h, a, :].unsqueeze(2).broadcast_to([P, 3, P]), ALU.mult))
                                    ps.settle()
                                    if a:
                                        ps.post(pool.tensor_tensor(band[h % 2][:], band[h % 2][:], btmp[:], ALU.add),
                                                S("band_ready") if a == 2 else None)
                                        ps.settle()
                        root_pool(pool, 1)
                        pool.wait_ge(S("square_ready"), 1)
                        pool.tensor_tensor(rrms[:], square[:], c("half").broadcast_to([P, TT]), ALU.pow).then_inc(S("rrms_ready"), 1)
                        for n in range(2, 6):
                            root_pool(pool, n)

                    @block.scalar
                    def _(act):
                        attention_act(act, mode, 0, ready=0, aside=features_act(act, ahead))
                        attention_act(act, "causal", 1, ready=1)
                        for e in range(NE):
                            if e >= 2:
                                act.wait_ge(S("down_done"), e - 1)
                            for j in range(MT // 2):
                                u = e * (MT // 2) + j
                                act.wait_ge(S("up_done"), u + 1)
                                for m in range(2):
                                    col = e * MT + 2 * j + m
                                    ins = act.activation(HTv[e % 2][:, 2 * j + m, :], SMs[u % 3][:, m * T:(m + 1) * T], ACT.Relu,
                                                         bias=w0("b1")[:, col:col + 1])
                                    ins.then_inc(S("relu_done"), 1)
                        qkv_act(act, qkv_ring)
                clear_block()

        differs = nc.values_load(flag[:])
        with nc.If(differs == 0):
            layer0("near")
        with nc.Else():
            layer0("conv")

        with nc.Block() as block:
            ahead = Ring(PT, next_full, next_free)

            @block.sync
            def _(sp):
                for i in range(2):
                    sp.dma_start(x4_d[B + i], OUT[:]).then_inc(S("feat_out"), 16)
                store_features(sp, slice(B, B + 1))
                sp.wait_ge(S("feat_out"), 112)

            @block.tensor
            def _(pe):
                for _ in features_pe(pe, ahead):
                    pass

            @block.scalar
            def _(act):
                for _ in features_act(act, ahead):
                    pass
        clear_block()

        spare = arena[:, LAY1_N + 3584:LAY1_N + 7700]
        idx_i = haloD[:, 0:2].rearrange("p h s c -> p (h s c)")[:, 0:TT * NI].bitcast(I32).rearrange("p (t n) -> p t n", t=TT)
        idx = small[:].rearrange("p (t n) -> p t n", t=TT)
        idxn = spare[:, 128:256].rearrange("p (t n) -> p t n", t=TT)
        iotab = spare[:, 256:384].bitcast(BF16)
        oneh = [spare[:, a:a + 1024].bitcast(BF16).rearrange("p (j n) -> p j n", j=8) for a in (384, 1966)]
        zerob = spare[:, 2990:2991].bitcast(BF16)[:, 0:1]
        Cn = arena[:, LAY1_N:LAY1_N + 512].rearrange("p (t n) -> p t n", t=2)
        gcur = spare[:, 1408:1410]
        lg8 = spare[:, 1410:1442].rearrange("p (i e) -> p i e", i=4)
        mx4 = spare[:, 1442:1454].rearrange("p (i e) -> p i e", i=3)
        WT8 = spare[0:KE, 1454:1966].rearrange("p (a t) -> p a t", a=2)
        big2 = arena[:, LAY1_N:LAY1_N + 3584]
        XC = big[:, 0:512].rearrange("p (k t) -> p k t", k=2)
        FQ = [big[:, 512 + i * 512:1024 + i * 512].rearrange("p (k t) -> p k t", k=2) for i in range(4)]
        HR = [big[:, 2560 + i * 512:3072 + i * 512].rearrange("p (k t) -> p k t", k=2) for i in range(2)]
        YW = [big2[:, 512 + i * 512:1024 + i * 512].rearrange("p (k t) -> p k t", k=2) for i in range(4)]
        PD = [m.rearrange("p (k t) -> p k t", k=4) for m in (big2[:, 2560:3584], spare[:, 384:1408])]
        with nc.Block() as block:
            @block.sync
            def _(sp):
                for i in range(B):
                    sp.dma_start(big[i * H:(i + 1) * H, 0:4096].rearrange("h (m n) -> h m n", m=4),
                                 feat[i + 1].rearrange("m (h c) t -> h m (c t)", h=H)).then_inc(S("feat_in"), 16)
                sp.dma_start(Z[:, 0, :], gate_d[1:B + 1].rearrange("b h t -> (b h) t")).then_inc(S("feat_in"), 16)
                sp.dma_start(arena[:, 0:LAY1_N], lay1).then_inc(S("lay1_in"), 16)
                sp.dma_start(Xin[:], x4_d[1]).then_inc(S("x_in"), 16)
                sp.dma_start(CT[:], ctxT[0]).then_inc(S("x_in"), 16)
                sp.dma_start(idx_i, itok[0]).then_inc(S("x_in"), 16)
                sp.wait_ge(S("lay1_in"), 16)
                sp.wait_ge(S("x_in"), 48)

            pl = big[:, 0:4096].rearrange("p (m c t) -> p m c t", m=4, c=4)
            free = arena[:, LAY1_N:LAY1_N + 7700]
            sq = free[:, 0:1536].rearrange("p (c t) -> p c t", c=6)
            sqs = [sq, free[:, 1536:3072].rearrange("p (c t) -> p c t", c=6)]
            outer = free[:, 1536:3072].rearrange("p (c t) -> p c t", c=6)
            rows_ = [sq, free[:, 3072:4608].rearrange("p (c t) -> p c t", c=6)]
            MM = free[:, 4608:4608 + 6 * 257].rearrange("p (c t) -> p c t", c=6)
            L = [free[:, a:a + 1536].rearrange("p (c t) -> p c t", c=6) for a in (6150, 4608)]
            n2 = PR[0][:, 0, :]
            nr = PR[0][:, 1, :]
            dt_ = PR[1][:, 0, :]
            wt = PR[1][:, 1, :]
            rdp = big[:, 0:1536].rearrange("p (c t) -> p c t", c=6)
            tmpb = outer[:, 0:3, :]

            def bc(ap, n):
                return ap.unsqueeze(1).broadcast_to([P, n, T])

            @block.vector
            def _(dve):
                st = Steps(dve, S("dve"))
                dve.wait_ge(S("feat_in"), 16 * (B + 1))
                for s in range(2):
                    p1, p2 = pl[:, 2 * s], pl[:, 2 * s + 1]
                    for lo, n, at in ((0, 3, 0), (1, 2, 3), (2, 1, 5)):
                        st.post(dve.tensor_tensor(L[s][:, at:at + n, :], bc(p1[:, lo, :], n), p2[:, lo + 1:lo + 1 + n, :], ALU.mult))
                        st.post(dve.tensor_tensor(tmpb[:, 0:n, :], p1[:, lo + 1:lo + 1 + n, :], bc(p2[:, lo, :], n), ALU.mult))
                        st.settle()
                        st.post(dve.tensor_tensor(L[s][:, at:at + n, :], L[s][:, at:at + n, :], tmpb[:, 0:n, :], ALU.subtract))
                        st.settle()
                for s in range(2):
                    st.post(dve.tensor_tensor(sqs[s], L[s], L[s], ALU.mult))
                st.settle()
                for s in range(2):
                    st.post(dve.tensor_reduce(PR[0][:, s, :], sqs[s].rearrange("p c t -> p t c"), AX.X, ALU.add), S("n2_ready"))
                dve.wait_ge(S("root_ready"), 1)
                st.post(dve.tensor_scalar(PR[1][:], PR[1][:], 1e-12, None, ALU.max))
                st.settle()
                st.post(dve.reciprocal(PR[1][:], PR[1][:]))
                st.settle()
                st.post(dve.tensor_tensor(L[0], L[0], bc(PR[1][:, 0, :], 6), ALU.mult))
                for i in range(6):
                    st.post(dve.scalar_tensor_tensor(rdp[:, 5 - i, :], L[1][:, i, :], -1.0 if i in (1, 4) else 1.0, PR[1][:, 1, :],
                                                     ALU.mult, ALU.mult))
                st.settle()
                dve.wait_ge(S("sig_exp"), 3)
                sg = small[:, 0:8]
                st.post(dve.tensor_scalar(sg[:, 0:2], small[:, 8:10], 1.0, None, ALU.add))
                st.post(dve.tensor_scalar(Z[:, 0, :], Z[:, 0, :], 1.0, None, ALU.add))
                st.settle()
                st.post(dve.reciprocal(sg[:, 2:4], sg[:, 0:2]))
                st.post(dve.reciprocal(Z[:, 0, :], Z[:, 0, :]))
                st.settle()
                dec, mix = sg[:, 2:3], sg[:, 3:4]
                st.post(dve.tensor_scalar(sg[:, 4:5], dec, 1e-6, None, ALU.max))
                st.settle()
                st.post(dve.reciprocal(sg[:, 5:6], sg[:, 4:5]))
                st.post(dve.tensor_scalar(sg[:, 0:1], dec, 1e-6, None, ALU.is_ge))
                st.settle()
                st.post(dve.tensor_tensor(sg[:, 6:7], dec, sg[:, 5:6], ALU.mult))
                st.settle()
                st.post(dve.tensor_scalar(sg[:, 6:7], sg[:, 6:7], sg[:, 0:1], 1.0, ALU.max, ALU.min))
                st.post(dve.tensor_scalar(dt_, ones[:], dec, None, ALU.mult))
                st.post(dve.memset(MM[:, :, 0:1], 0.0))
                st.settle()
                st.post(dve.tensor_scalar(n2, ones[:], sg[:, 6:7], None, ALU.mult))
                st.post(dve.memset(nr, 0.0))
                st.settle()
                st.post(dve.tensor_tensor_scan(wt[:, 1:T], n2[:, 1:T], nr[:, 1:T], 1.0, ALU.mult, ALU.add))
                st.post(dve.memset(wt[:, 0:1], 1.0))
                st.settle()
                for i in range(6):
                    st.post(dve.tensor_tensor(n2, L[0][:, i, :], wt, ALU.mult))
                    st.settle()
                    st.post(dve.tensor_tensor(outer, L[0], bc(n2, 6), ALU.mult))
                    st.settle()
                    for j in range(6):
                        st.post(dve.tensor_tensor_scan(MM[:, j, 1:T + 1], dt_, outer[:, j, :], 0.0, ALU.mult, ALU.add))
                    st.settle()
                    if i >= 2:
                        dve.wait_ge(S("row_summed"), i - 1)
                    st.post(dve.tensor_tensor(rows_[i % 2], MM[:, :, 0:T], bc(rdp[:, i, :], 6), ALU.mult), S("row_ready"))
                dve.wait_ge(S("row_summed"), 6)
                for g in range(3):
                    st.post(dve.tensor_scalar(outer[:, 2 * g:2 * g + 2, :], two(SMs[g]), dec, None, ALU.mult))
                st.settle()
                st.post(dve.tensor_tensor(rows_[0], outer, rdp, ALU.mult))
                st.post(dve.tensor_tensor(rows_[1], outer, outer, ALU.mult))
                st.settle()
                st.post(dve.tensor_reduce(n2, rows_[0].rearrange("p c t -> p t c"), AX.X, ALU.add))
                st.post(dve.tensor_reduce(nr, rows_[1].rearrange("p c t -> p t c"), AX.X, ALU.add))
                st.post(dve.tensor_scalar(sg[:, 7:8], mix, -1.0, 1.0, ALU.mult, ALU.add))
                st.settle()
                st.post(dve.tensor_scalar(n2, n2, sg[:, 7:8], None, ALU.mult))
                st.settle()
                st.post(dve.scalar_tensor_tensor(n2, nr, mix, n2, ALU.mult, ALU.add))
                st.settle()
                st.post(dve.tensor_scalar(n2, n2, c("mscale"), None, ALU.mult), S("score_ready"))
                dve.wait_ge(S("score_exp"), 1)
                st.post(dve.tensor_scalar(n2, n2, 1.0, None, ALU.add))
                st.settle()
                st.post(dve.reciprocal(n2, n2))
                st.settle()
                st.post(dve.tensor_tensor(n2, n2, Z[:, 0, :], ALU.mult), S("gated_ready"))
                dve.wait_ge(pj_full[0], 1)
                st.post(dve.tensor_copy(Gt[:], PJ[0][:, 0:TT * B].rearrange("p (t b) -> p t b", t=TT)))
                dve.wait_ge(S("lay1_in"), 16)
                st.post(dve.tensor_tensor(w1("r2b"), w1("r2b"), w1("eb"), ALU.add))
                st.settle()

            @block.scalar
            def _(act):
                act.wait_ge(S("feat_in"), 16 * (B + 1))
                act.activation(small[:, 8:9], c("decay"), ACT.Exp, scale=-1.0).then_inc(S("sig_exp"), 1)
                act.activation(small[:, 9:10], c("mix"), ACT.Exp, scale=-1.0).then_inc(S("sig_exp"), 1)
                act.activation(Z[:, 1, :], Z[:, 0, :], ACT.Identity, bias=c("memg_b")).then_inc(S("gate_biased"), 1)
                act.wait_ge(S("gate_biased"), 1)
                act.activation(Z[:, 0, :], Z[:, 1, :], ACT.Exp, scale=-1.0).then_inc(S("sig_exp"), 1)
                act.wait_ge(S("n2_ready"), 2)
                act.activation(PR[1][:], PR[0][:], ACT.Sqrt).then_inc(S("root_ready"), 1)
                act.wait_ge(S("score_ready"), 1)
                act.activation(n2, n2, ACT.Exp, scale=-1.0).then_inc(S("score_exp"), 1)

            @block.tensor
            def _(pe):
                for i in range(6):
                    pe.wait_ge(S("row_ready"), i + 1)
                    for g in range(3):
                        ins = pe.matmul(SMs[g][:], ident, rows_[i % 2][:, 2 * g:2 * g + 2, :].rearrange("p c t -> p (c t)"),
                                        start=i == 0, stop=i == 5)
                    ins.then_inc(S("row_summed"), 1)
                pe.wait_ge(S("gated_ready"), 1)
                for t in range(TT):
                    ins = pe.matmul(PJ[0][:, t * B:(t + 1) * B], n2[:, t * P:(t + 1) * P], c("bsel"), start=True, stop=True)
                ins.then_inc(pj_full[0], 1)
        clear_block()

        XN = big[:, 3584:4096].rearrange("p (k t) -> p k t", k=KT)

        def project_pe(pe, ring):
            flip(pe, ring, Xin)
            ring.moved(pe)
            W = k3(w1("qkv"), 2)
            for i in range(2):
                bank = ring.claim(pe)
                ring.fill(columns(pe, bank, W, XN, i * D))
            yield
            for w, n0, bias in ((W, 2 * D, w1("qkv_b")[0:1, 2 * D:3 * D]), (k3(w1("memv"), 2), 0, w1("memv_b")[0:1, :])):
                bank = ring.claim(pe)
                for t in range(TT):
                    pe.matmul(bank[:, t * D:(t + 1) * D], ones[0:1, 0:P], bias, start=True, stop=False)
                    for k in range(KT):
                        ins = pe.matmul(bank[:, t * D:(t + 1) * D], XN[:, k, t * P:(t + 1) * P], w[:, k, n0:n0 + D],
                                        start=False, stop=k == KT - 1)
                ring.fill(ins)
            yield

        def project_act(act, ring):
            sa = Steps(act, S("act"))
            bank = ring.take(act)
            ring.release(sa, act.activation(XN, two(bank), ACT.Copy))
            for i, dst in enumerate((QF, KF)):
                bank = ring.take(act)
                for k in range(KT):
                    ins = act.activation(dst[:, k, 1:T + 1], bank[:, k * T:(k + 1) * T], ACT.Identity,
                                         bias=w1("qkb")[:, 2 * i + k:2 * i + k + 1])
                    ring.release(sa, ins) if k else sa.post(ins)
            yield
            bank = ring.take(act)
            for t in range(TT):
                ins = act.activation(vm_diag(t), bank[:, t * D:(t + 1) * D].rearrange("p (k h d) -> p k h d", k=KT, h=8), ACT.Copy)
                ring.release(sa, ins) if t else sa.post(ins)
            bank = ring.take(act)
            ring.release(sa, act.activation(Z[:], two(bank), ACT.Copy))
            yield

        with nc.Block() as block:
            ahead = Ring(PT, next_full, next_free)

            @block.tensor
            def _(pe):
                for _ in project_pe(pe, ahead):
                    pass

            @block.scalar
            def _(act):
                for _ in project_act(act, ahead):
                    pass
        clear_block()

        with nc.Fori(0, B) as b:
            with nc.Block() as block:
                ring = Ring(PJ, pj_full, pj_free)
                ahead = Ring(PT, next_full, next_free)

                @block.sync
                def _(sp):
                    sp.dma_start(out[bass.ds(b, 1)].rearrange("o p t d -> (o p) t d"), OUT[:]).then_inc(S("out_done"), 16)
                    sp.wait_ge(S("idx_used"), 1)
                    sp.dma_start(idx_i, itok[bass.ds(b + 1, 1)].rearrange("o p t n -> (o p) t n")).then_inc(S("next_in"), 16)
                    sp.wait_ge(S("residual_read"), 1)
                    sp.dma_start(Xin[:], x4_d[bass.ds(b + 2, 1)].rearrange("o p t d -> (o p) t d")).then_inc(S("x_next"), 16)
                    sp.wait_ge(S("ctx_used"), 1)
                    sp.dma_start(CT[:], ctxT[bass.ds(b + 1, 1)].rearrange("o p k t -> (o p) k t")).then_inc(S("next_in"), 16)
                    sp.wait_ge(S("out_done"), 16)
                    sp.wait_ge(S("x_next"), 16)
                    sp.wait_ge(S("next_in"), 32)

                @block.tensor
                def _(pe):
                    XTc = XT[:, :, 1:T + 1]
                    tally = ring.claim(pe)

                    def sum_hot(s):
                        g = s - 1
                        if not 0 <= g < TT * NI // 8:
                            return
                        t, j0 = g // 8, g % 8 * 8
                        pe.wait_ge(S("hot_ready"), g + 1)
                        for j in range(8):
                            ins = pe.matmul(tally[:, t * T:(t + 1) * T], identb[:], oneh[g % 2][:, j, :],
                                            start=j0 + j == 0, stop=j0 + j == NI - 1)
                        ins.then_inc(S("hot_used"), 1)

                    attention_pe(pe, "tally", 0, KF[:, :, 1:T + 1], sum_hot)
                    pe.wait_ge(S("hot_used"), TT * NI // 8)
                    ring.fill(pe.matmul(tally[0:1, 0:1], identb[:, 0:1], zerob, start=False, stop=True, skip_group_check=True))
                    pe.wait_ge(S("y_ready"), 2)
                    flip(pe, ring, Z)
                    scale_pe(pe, ring, 0)
                    pe.wait_ge(S("exp_done"), 2 * H)
                    pe.wait_ge(S("biased"), 1)
                    residual(pe, Xin[:])
                    pe.wait_ge(S("mixed_in"), 1)
                    ring.moved(pe)
                    add_rows(pe, YT, k3(w1("outw"), 2))
                    keep_clock(pe, 14)
                    pe.wait_ge(S("x_ready"), 2)
                    flip(pe, ring, X2)
                    bank = ring.claim(pe)
                    for k in range(KT):
                        ins = pe.matmul(bank[:, 0:T], k3(w1("ydown"), 2)[:, k, :], CT[:, k, :], start=k == 0, stop=k == 1)
                    ring.fill(ins)
                    ring.moved(pe)
                    bank = ring.claim(pe)
                    ring.fill(columns(pe, bank, k3(w1("yq"), 2), XTc))
                    bank = ring.claim(pe)
                    for m in range(2):
                        ins = pe.matmul(bank[:, m * T:(m + 1) * T], w1("yup")[:, m * P:(m + 1) * P], YT[:, 0, :],
                                        start=True, stop=True)
                    ring.fill(ins)
                    bank = ring.claim(pe)
                    for t in range(TT):
                        ins = pe.matmul(bank[:, t * D:(t + 1) * D], YT[:, 0, t * P:(t + 1) * P],
                                        w1("yup")[:, D:2 * D], start=True, stop=True)
                    ring.fill(ins)
                    ring.moved(pe)
                    pe.wait_ge(S("count_ready"), 1)
                    attention_pe(pe, "count", 1, KF[:, :, 1:T + 1])
                    scale_pe(pe, ring, 1)
                    pe.wait_ge(S("exp_done"), 4 * H)
                    residual(pe, X2[:])
                    ring.moved(pe)
                    add_rows(pe, YT, k3(w1("yout"), 2))
                    pe.wait_ge(S("x_next"), 16)
                    pe.wait_ge(S("probs_moved"), 2 * H)
                    steps = project_pe(pe, ahead)
                    next(steps)
                    pe.wait_ge(S("x_ready"), 4)
                    flip(pe, ring, X)
                    ring.moved(pe)
                    pe.wait_ge(S("cum_ready"), 2)

                    def cols(w, act_):
                        bank = ring.claim(pe)
                        ring.fill(columns(pe, bank, k3(w, 2), act_))

                    cols(w1("fQ"), XTc)
                    cols(w1("fK"), XC)
                    ring.moved(pe)
                    YB = [SC, OA]

                    def router(br):
                        columns(pe, SM[br], k3(w1("r1"), 2), FQ[2 * br]).then_inc(S("router_full"), 1)

                    def factors(br):
                        for j in range(2):
                            u = br * 2 + j
                            if u >= 2:
                                pe.wait_ge(S("yw_copied"), u - 1)
                            columns(pe, YB[j], k3(w1(f"fW{br}"), 2), FQ[2 * br + 1], 2 * j * P).then_inc(S("yw_full"), 1)
                            bank = ring.claim(pe)
                            ring.fill(columns(pe, bank, k3(w1(f"fV{br}"), 2), FQ[2 * br], 2 * j * P))

                    pe.wait_ge(S("exp_done"), 4 * H)
                    pe.wait_ge(oa_free, 2)
                    router(0)
                    cols(w1("finv"), FQ[0])
                    cols(w1("finv"), FQ[1])
                    factors(0)
                    router(1)
                    next(steps)
                    pe.wait_ge(S("router_act"), 4)
                    bank = ring.claim(pe)
                    for br in range(2):
                        for t in range(TT):
                            i = br * 2 + t
                            for k in range(KT):
                                ins = pe.matmul(bank[:, i * KE:(i + 1) * KE], HR[br][:, k, t * P:(t + 1) * P],
                                                k3(w1("r2"), 2)[:, k, :], start=k == 0, stop=k == 1)
                    ring.fill(ins)
                    factors(1)
                    pe.wait_ge(S("wts_ready"), 1)
                    bank = ring.claim(pe)
                    for i in range(4):
                        ins = pe.transpose(bank[0:KE, i * P:(i + 1) * P], lg8[:, i, :], ident)
                    ring.fill(ins)
                    ring.moved(pe)

                    def spread(br):
                        for j in range(2):
                            bank = ring.claim(pe)
                            for m in range(2):
                                ins = pe.matmul(bank[:, m * T:(m + 1) * T], k3(w1("sel8"), 4)[0:KE, 2 * j + m, :], WT8[:, br, :],
                                                start=True, stop=True)
                            ring.fill(ins)

                    def back(br):
                        bank = ring.claim(pe)
                        for t in range(TT):
                            for m in range(4):
                                pe.matmul(bank[:, t * D:(t + 1) * D], PD[br][:, m, t * P:(t + 1) * P],
                                          k3(w1(f"fU{br}"), 4)[:, m, :], start=m == 0, stop=False)
                            ins = pe.matmul(bank[:, t * D:(t + 1) * D], WT8[:, br, t * P:(t + 1) * P],
                                            k3(w1("b8"), 2)[0:KE, br, :], start=False, stop=True)
                        ring.fill(ins)

                    spread(0)
                    spread(1)
                    back(0)
                    ring.moved(pe)
                    back(1)
                    pe.wait_ge(S("mixed"), 2)
                    flip(pe, ring, Y)
                    pe.wait_ge(S("yw_copied"), 4)
                    residual(pe, X[:])
                    ring.moved(pe)
                    add_rows(pe, YT, k3(w1("fO"), 2))

                @block.vector
                def _(dve):
                    st = Steps(dve, S("dve"))
                    st.post(dve.tensor_copy(gcur, Gt[:, :, bass.ds(b, 1)].rearrange("p t o -> p (t o)")))
                    st.post(dve.tensor_copy(iotab, c("iota")))
                    st.post(dve.memset(zerob, 0.0))
                    st.post(dve.tensor_copy(idx, idx_i), S("idx_used"))
                    st.settle()
                    st.post(dve.tensor_scalar(idxn, idx, 0.0, float(T), ALU.is_lt, ALU.mult))
                    st.settle()
                    st.post(dve.tensor_tensor(idx, idx, idxn, ALU.add))
                    st.settle()
                    st.post(dve.tensor_scalar(idx, idx, 0.0, float(T - 1), ALU.max, ALU.min))
                    for t in range(TT):
                        st.post(dve.tensor_scalar(Z[:, t, :], Z[:, t, :], gcur[:, t:t + 1], None, ALU.mult), S("y_ready"))
                    st.settle()

                    def make_hot(g):
                        if g >= TT * NI // 8:
                            return
                        if g >= 2:
                            dve.wait_ge(S("hot_used"), g - 1)
                        t, j0 = g // 8, g % 8 * 8
                        for j in range(8):
                            ins = dve.tensor_scalar(oneh[g % 2][:, j, :], iotab, idx[:, t, j0 + j:j0 + j + 1], None, ALU.is_equal)
                            st.post(ins, S("hot_ready") if j == 7 else None)

                    def prepare(s):
                        make_hot(s)
                        if s == 14:
                            st.post(dve.tensor_tensor(Xin[:], Xin[:], w1("out_b").unsqueeze(1).broadcast_to([P, TT, D]), ALU.add),
                                    S("biased"))

                    attention_dve(dve, st, "tally", 0, between=prepare)
                    bank = ring.take(dve)
                    st.post(dve.tensor_copy(Cn, two(bank)), S("count_ready"))
                    ring.release(st, dve.tensor_scalar(masks[:, 0], two(bank), 0.0, NEG, ALU.is_equal, ALU.mult))
                    move(dve, st, ring, Y[:])
                    scale_dve(dve, st, ring, 0)
                    st.settle()
                    st.post(dve.tensor_tensor(YT[:], YT[:], Y[:], ALU.add), S("mixed_in"))
                    dve.wait_ge(S("sum_ready"), 1)
                    layernorm(dve, st, X2, SUM, 1, "x_ready")
                    move(dve, st, ring, XT[:, :, 1:T + 1])
                    bank = ring.take(dve)
                    ring.release(st, dve.tensor_copy(YT[:, 0, :], bank[:, 0:T]))
                    st.post(dve.memset(zerob, 0.0), S("ctx_used"))
                    for dst in (QF, KF):
                        bank = ring.take(dve)
                        ring.release(st, dve.tensor_copy(dst[:, :, 1:T + 1], two(bank)))
                    st.settle()
                    st.post(dve.memset(mx4[:, 0, 0:1], 0.0), S("qk_ready"))
                    move_v(dve, st, ring)
                    attention_dve(dve, st, "count", 1, Cn)
                    scale_dve(dve, st, ring, 1)
                    dve.wait_ge(S("sum_ready"), 2)
                    layernorm(dve, st, X, SUM, 2, "x_ready")
                    move(dve, st, ring, XT[:, :, 1:T + 1])
                    st.settle()
                    for k in range(KT):
                        st.post(dve.tensor_tensor_scan(XC[:, k, :], ones[:], XT[:, k, 1:T + 1], 0.0, ALU.mult, ALU.add),
                                S("cum_ready"))
                    move(dve, st, ring, FQ[0])
                    move(dve, st, ring, FQ[1])
                    move(dve, st, ring, FQ[2])
                    move(dve, st, ring, FQ[3])

                    def product(br):
                        for j in range(2):
                            dve.wait_ge(S("yw_copied"), br * 2 + j + 1)
                            bank = ring.take(dve)
                            ring.release(st, dve.tensor_tensor(PD[br][:, 2 * j:2 * j + 2, :], two(bank), YW[br * 2 + j], ALU.mult))

                    def weigh(br):
                        for j in range(2):
                            bank = ring.take(dve)
                            ring.release(st, dve.tensor_tensor(PD[br][:, 2 * j:2 * j + 2, :], two(bank), PD[br][:, 2 * j:2 * j + 2, :],
                                                               ALU.mult))

                    product(0)
                    bank = ring.take(dve)
                    ring.release(st, dve.tensor_tensor(lg8, bank[:, 0:4 * KE].rearrange("p (i e) -> p i e", i=4),
                                                       w1("r2b").unsqueeze(1).broadcast_to([P, 4, KE]), ALU.add))
                    st.settle()
                    st.post(dve.tensor_reduce(mx4[:, 0, :], lg8, AX.X, ALU.max))
                    st.settle()
                    st.post(dve.tensor_tensor(lg8, lg8, mx4[:, 0, :].unsqueeze(2).broadcast_to([P, 4, KE]), ALU.subtract),
                            S("lg_shift"))
                    dve.wait_ge(S("lg_exp"), 1)
                    st.post(dve.tensor_reduce(mx4[:, 1, :], lg8, AX.X, ALU.add))
                    st.settle()
                    st.post(dve.reciprocal(mx4[:, 2, :], mx4[:, 1, :]))
                    st.settle()
                    st.post(dve.tensor_tensor(lg8, lg8, mx4[:, 2, :].unsqueeze(2).broadcast_to([P, 4, KE]), ALU.mult),
                            S("wts_ready"))
                    product(1)
                    bank = ring.take(dve)
                    ring.release(st, dve.tensor_copy(WT8.rearrange("e a t -> e (a t)"), bank[0:KE, :]))
                    st.settle()
                    weigh(0)
                    weigh(1)
                    bank = ring.take(dve)
                    ring.release(st, dve.tensor_copy(Y[:], two(bank)))
                    st.settle()
                    bank = ring.take(dve)
                    for t in range(TT):
                        ins = dve.scalar_tensor_tensor(Y[:, t, :], bank[:, t * D:(t + 1) * D], w1("alpha"), Y[:, t, :],
                                                       ALU.mult, ALU.add)
                        ring.release(st, ins) if t else st.post(ins)
                    st.settle()
                    for t in range(TT):
                        st.post(dve.tensor_scalar(Y[:, t, :], Y[:, t, :], w1("rn")[:, t:t + 1], None, ALU.mult), S("mixed"))
                    move(dve, st, ring, YT[:])
                    dve.wait_ge(S("out_done"), 16)
                    dve.wait_ge(S("sum_ready"), 3)
                    layernorm(dve, st, OUT, SUM, 3, "out_ready")
                    st.settle()

                @block.gpsimd
                def _(pool):
                    for n in range(1, 4):
                        root_pool(pool, n)

                @block.scalar
                def _(act):
                    attention_act(act, "tally", 0, ready=0)
                    attention_act(act, "count", 1, ready=1)
                    steps = project_act(act, ahead)
                    next(steps)

                    def router(br):
                        act.wait_ge(S("router_full"), br + 1)
                        for m in range(2):
                            act.activation(HR[br][:, m, :], SM[br][:, m * T:(m + 1) * T], ACT.Gelu,
                                           bias=w1("r1b")[:, m:m + 1]).then_inc(S("router_act"), 1)

                    def copy_factor(u):
                        act.wait_ge(S("yw_full"), u + 1)
                        act.activation(YW[u], two([SC, OA][u % 2]), ACT.Copy).then_inc(S("yw_copied"), 1)

                    router(0)
                    copy_factor(0)
                    copy_factor(1)
                    router(1)
                    next(steps)
                    act.wait_ge(S("lg_shift"), 1)
                    act.activation(lg8, lg8, ACT.Exp).then_inc(S("lg_exp"), 1)
                    copy_factor(2)
                    copy_factor(3)
            clear_block()

        with nc.Block() as block:
            @block.sync
            def _(sp):
                sp.dma_start(out[B], OUT[:]).then_inc(S("out_done"), 16)
                sp.wait_ge(S("out_done"), 16)


def kernel(**inputs):
    import numpy as np
    import concourse.bacc as bacc
    from concourse import mybir
    from concourse.bass_utils import run_bass_kernel_spmd as run

    a = {k: np.asarray(v) for k, v in inputs.items()}

    def chunks(w):
        k, n = w.shape
        return w.reshape(k // 128, 128, n).transpose(1, 0, 2).reshape(128, -1)

    def row(v, parts=128):
        return np.broadcast_to(np.reshape(v, (1, -1)), (128, v.size))

    def col(v):
        return v.reshape(-1, 128).T

    def first(w):
        z = np.zeros((128, w.shape[1]), w.dtype)
        z[:w.shape[0]] = w
        return z

    def tokens(v):
        return v.reshape(8, 2, 128, -1).transpose(0, 2, 1, 3)

    def feats(v):
        return v.transpose(0, 2, 1).reshape(8, 2, 128, 256).transpose(0, 2, 1, 3)

    f32 = np.float32
    p = "L0_xattn_"
    W = {"hist_W": chunks(a[p + "hist_W"]), "ctx_W1": chunks(a[p + "ctx_W1"]), "ctx_W2": a[p + "ctx_W2"],
         "ctx_b1": col(a[p + "ctx_b1"]), "kg_W1": chunks(a[p + "kg_W1"]), "kg_W2": chunks(a[p + "kg_W2"]),
         "hist_b": row(a[p + "hist_b"]), "hist_g": row(a[p + "hist_ln_g"]), "hist_lb": row(a[p + "hist_ln_b"]),
         "ctx_b2": row(a[p + "ctx_b2"]), "kg_b1": row(a[p + "kg_b1"]), "kg_g": row(a[p + "kg_ln_g"]),
         "kg_lb": row(a[p + "kg_ln_b"]), "kg_b2": row(a[p + "kg_b2"])}
    pos = np.arange(256, dtype=f32)[:, None]
    ang = pos * (1.0 / 10000.0 ** (np.arange(8, dtype=f32) / 8)).astype(f32)[None, :]
    ang = np.tile(ang.T, (16, 1))
    sign = np.tile(np.repeat(np.array([-1.0, 1.0], f32), 8), 8)[:, None]
    swap = np.arange(256) ^ 8
    q = "L0_ffn_"
    W.update({"wv": chunks(a["L0_attn_w_qkv"][512:].T), "wo": chunks(a["L0_attn_w_o"].T),
              "xqkv": chunks(np.concatenate([a[p + "Wq"], a[p + "Wk"], a[p + "Wv"]], axis=1)),
              "xproj": chunks(a[p + "proj_W"]), "proj_b": row(a[p + "proj_b"]),
              "mq": chunks(a[q + "Wq"].T), "mqs": chunks(a[q + "Wq"][swap].T), "muks": a[q + "Wuk"][swap].T,
              "mdkv": chunks(a[q + "Wdkv"].T),
              "mukv": np.concatenate([a[q + "Wuk"].T, a[q + "Wuv"].T], axis=1), "mo": chunks(a[q + "Wo"].T),
              "gate": chunks(a[q + "gate_w"].T), "W1": chunks(a[q + "W1"].reshape(4096, 256).T),
              "W2": chunks(a[q + "W2"].transpose(0, 2, 1).reshape(4096, 256)),
              "w1w": chunks(a["L1_attn_w1w"].T), "w2w": chunks(a["L1_attn_w2w"].T),
              "rw": chunks(np.concatenate([a["L1_attn_r1w"].T, a["L1_attn_r2w"].T], axis=1)),
              "memg": chunks(a["L1_attn_memg_w"].T), "norm1": row(a[q + "norm1_w"]), "norm2": row(a[q + "norm2_w"]),
              "ln_g": row(a[q + "ln_g"]), "ln_b": row(a[q + "ln_b"]), "gate_b": row(a[q + "gate_b"]),
              "b1": col(a[q + "b1"].reshape(-1)), "b2": row(a[q + "b2"]),
              "cos": np.cos(ang).astype(f32), "sin": (np.sin(ang) * sign).astype(f32)})
    r, s, t = "L1_attn_", "L1_xattn_", "L1_ffn_"

    def experts(w):
        return chunks(w.transpose(1, 0, 2).reshape(256, 512))

    def back(w):
        return chunks(w.transpose(0, 2, 1).reshape(512, 256))

    sel8 = np.zeros((128, 4, 128), f32)
    for m in range(4):
        for j in range(128):
            sel8[2 * m + j // 64, m, j] = 1.0
    W.update({"qkv": chunks(a[r + "qkv_w"].T), "memv": chunks(a[r + "memv_w"].T), "outw": chunks(a[r + "out_w"].T),
              "yq": chunks(a[s + "W_q"].T), "ydown": chunks(a[s + "W_kv_down"].T), "yup": a[s + "W_kv_up"].T,
              "yout": chunks(a[s + "W_out"].T), "fQ": chunks(a[t + "W_Q"].T), "fK": chunks(a[t + "W_K"].T),
              "fO": chunks(a[t + "W_O"].T), "finv": chunks(a[t + "W_inv"].T),
              "fV0": experts(a[t + "V_fwd"]), "fW0": experts(a[t + "W_fwd"]),
              "fV1": experts(a[t + "W_inv_exp"]), "fW1": experts(a[t + "V_inv"]),
              "fU0": back(a[t + "U_fwd"]), "fU1": back(a[t + "U_inv"]), "r1": chunks(a[t + "router_w1"].T),
              "r2": chunks(a[t + "router_w2"].T), "r1b": col(a[t + "router_b1"]), "r2b": row(a[t + "router_b2"]),
              "eb": row(a[t + "expert_bias"]), "alpha": row(a[t + "alpha_bi"]), "qkv_b": row(a[r + "qkv_b"]),
              "memv_b": row(a[r + "memv_b"]), "out_b": row(a[r + "out_b"]), "qkb": col(a[r + "qkv_b"][0:512]),
              "b8": first(np.concatenate([a[t + "b_fwd"], a[t + "b_inv"]], axis=1)), "sel8": sel8.reshape(128, 512),
              "rn": (1.0 / np.arange(1, 257, dtype=f32)).astype(f32).reshape(2, 128).T})
    shift = np.zeros((128, 3, 128), f32)
    for d in range(3):
        for i in range(128):
            if 0 <= i + d - 1 < 128:
                shift[i + d - 1, d, i] = 1.0
    up, dn = np.zeros((128, 32), f32), np.zeros((128, 32), f32)
    up[0, 31] = 1.0
    dn[127, 0] = 1.0
    bsel = np.zeros((128, 8), f32)
    for i in range(128):
        bsel[i, i // 16] = 1.0 / 16

    head1 = np.zeros((128, 8), f32)
    heads_on = np.zeros((128, 2, 128), f32)
    near0, near1 = np.zeros((128, 129), f32), np.zeros((128, 129), f32)
    for i in range(128):
        head1[i, i // 16] = 1.0
        near0[i, i] = near1[i, i + 1] = 1.0
        for k in range(2):
            heads_on[8 * k + i // 16, k, i] = 1.0

    def heads(v):
        return np.tile(v.reshape(16, 1), (8, 1))

    mask = a["mask_SxS_bc0"]
    W.update({"ident": np.eye(128, dtype=f32), "causal": np.triu(np.ones((256, 256), f32), 1).reshape(2, 128, 256).transpose(1, 0, 2), "shift": shift.reshape(128, 384), "halo_up": up,
              "halo_dn": dn, "iota": np.broadcast_to(np.arange(256, dtype=f32), (128, 256)),
              "half": np.full((128, 1), -0.5, f32), "decay": heads(a[r + "decay_logits"]), "mscale": heads(a[r + "mem_scale"]),
              "memg_b": heads(a[r + "memg_b"]), "mix": row(a[r + "iter_mix"]), "bsel": bsel, "headq": head1 * f32(SCALE),
              "head1": head1, "heads_on": heads_on.reshape(128, 256), "near0": near0, "near1": near1})

    def pack(table):
        return np.ascontiguousarray(np.concatenate([W[n].reshape(128, -1) for n, _ in table], axis=1))

    arrays = {"x": tokens(a["x"]), "ctxT": feats(a["ctx_1024"]),
              "itok": tokens(a["itok_BxSx64_0_2047"]), "hist": pack(HIST), "lay0": pack(LAY0), "lay1": pack(LAY1),
              "const": pack(CONST), "mask": mask.reshape(2, 128, 256).transpose(1, 0, 2).astype(np.int32)}
    for k in ("x", "ctxT", "itok"):
        arrays[k] = np.concatenate([arrays[k]] + [arrays[k][-1:]] * (2 if k == "x" else 1))
    arrays = {k: np.ascontiguousarray(v) for k, v in arrays.items()}
    nc = bacc.Bacc("TRN2", target_bir_lowering=False, num_devices=1)
    ap = {k: nc.dram_tensor(k, v.shape, mybir.dt.from_np(v.dtype), kind="ExternalInput").ap() for k, v in arrays.items()}
    feat = nc.dram_tensor("feat", (B + 1, 4, 64, T), F32, kind="Internal").ap()
    gate_d = nc.dram_tensor("gate_d", (B + 1, H, T), F32, kind="Internal").ap()
    kern_d = nc.dram_tensor("kern_d", (B, 144), F32, kind="Internal").ap()
    x4_d = nc.dram_tensor("x4_d", (B + 2, P, TT, D), F32, kind="Internal").ap()
    q_d = nc.dram_tensor("q_d", (P, T + 2), F32, kind="Internal").ap()
    k_d = nc.dram_tensor("k_d", (P, 3, T), F32, kind="Internal").ap()
    out = nc.dram_tensor("out", (9, 128, 2, 256), F32, kind="ExternalOutput").ap()
    decoder(nc, ap["x"], ap["ctxT"], ap["itok"], ap["hist"], ap["lay0"], ap["lay1"], ap["const"], ap["mask"],
            feat, gate_d, kern_d, x4_d, q_d, k_d, out)
    got = run(nc, [arrays], core_ids=[0])
    return got.results[0]["out"][1:].transpose(0, 2, 1, 3).reshape(8, 256, 256)
```
